# Optimizing a Trainium2 kernel written in Bass

```python
import numpy as np
import jax
import jax.numpy as jnp

def _softmax(x, axis=-1):
    return jax.nn.softmax(x, axis=axis)

def _gelu(x):
    return jax.nn.gelu(x, approximate=True)

def _silu(x):
    return jax.nn.silu(x)

def _sigmoid(x):
    return jax.nn.sigmoid(x)

def _layernorm(x, axis=-1, eps=1e-05):
    m = jnp.mean(x, axis=axis, keepdims=True)
    v = jnp.var(x, axis=axis, keepdims=True)
    return (x - m) / jnp.sqrt(v + eps)

def _scatter_add(tgt, idx, src, axis=0):
    return tgt.at[idx].add(src)

def _segment_sum(src, seg, n):
    return jax.ops.segment_sum(src, seg, n)
kernel_name = 'mk_gnn_ffn_d2_gnn_r8_70038a'

def setup_inputs(seed: int=0):
    np.random.seed(seed)
    _w = jnp.asarray

    def _rec_inputs():
        import jax
        import jax.numpy as jnp
        _gk = jax.random.key(seed)
        x = -8.776e-05 + 1 * jax.random.normal(jax.random.fold_in(_gk, 1), (1250, 512), jnp.float32)
        src = jax.random.randint(jax.random.fold_in(_gk, 2), (20000,), 0, 1250, jnp.int32)
        dst = jax.random.randint(jax.random.fold_in(_gk, 3), (20000,), 0, 1250, jnp.int32)
        _o = jnp.argsort(dst, stable=True)
        src = src[_o]
        dst = dst[_o]
        return (x, src, dst)
    x, src, dst = _rec_inputs()

    def _L0_gnn_setup():
        import jax, jax.numpy as jnp
        import numpy as np
        N_NODES = 1250
        N_EDGES = 20000
        IN_DIM = 512
        OUT_DIM = 512
        LN_EPS = 1e-05
        key = jax.random.key(seed)
        k_x, k_src, k_ws, k_wn = jax.random.split(key, 4)
        x = jax.random.normal(k_x, (N_NODES, IN_DIM), dtype=jnp.float32)
        edge_src = jax.random.randint(k_src, (N_EDGES,), 0, N_NODES, dtype=jnp.int32)
        edge_dst = jnp.repeat(jnp.arange(N_NODES, dtype=jnp.int32), N_EDGES // N_NODES)
        deg = jnp.full((N_NODES,), float(N_EDGES // N_NODES), dtype=jnp.float32)
        scale = 1.0 / np.sqrt(IN_DIM)
        W_self = jax.random.normal(k_ws, (OUT_DIM, IN_DIM), dtype=jnp.float32) * scale
        W_neigh = jax.random.normal(k_wn, (OUT_DIM, IN_DIM), dtype=jnp.float32) * scale
        bias = jnp.zeros((OUT_DIM,), dtype=jnp.float32)
        gamma = jnp.ones((OUT_DIM,), dtype=jnp.float32)
        beta = jnp.zeros((OUT_DIM,), dtype=jnp.float32)
        return {'x': x, 'edge_src': edge_src, 'edge_dst': edge_dst, 'deg': deg, 'W_self': W_self, 'W_neigh': W_neigh, 'bias': bias, 'gamma': gamma, 'beta': beta}
    _L0_gnn_all = _L0_gnn_setup()
    _L0_gnn_in = {k: v for k, v in _L0_gnn_all.items() if k in ('W_self', 'W_neigh', 'bias', 'gamma', 'beta')}
    del _L0_gnn_all

    def _L0_ffn_setup():
        import jax, jax.numpy as jnp
        import numpy as np
        B, S, D, H, E = (4, 256, 512, 8, 8)
        FF = 4 * D
        HD = D // H
        EPS = 1e-05

        def _layernorm(x, g, b):
            mu = jnp.mean(x, axis=-1, keepdims=True)
            var = jnp.mean((x - mu) ** 2, axis=-1, keepdims=True)
            return (x - mu) * jax.lax.rsqrt(var + EPS) * g + b
        key = jax.random.key(seed)
        ks = jax.random.split(key, 16)
        s = 0.02
        return {'x': jax.random.normal(ks[0], (B, S, D), dtype=jnp.float32), 'ln1_g': jnp.ones((D,), jnp.float32), 'ln1_b': jnp.zeros((D,), jnp.float32), 'Wq': jax.random.normal(ks[1], (D, D), jnp.float32) * s, 'bq': jnp.zeros((D,), jnp.float32), 'Wk': jax.random.normal(ks[2], (D, D), jnp.float32) * s, 'bk': jnp.zeros((D,), jnp.float32), 'Wv': jax.random.normal(ks[3], (D, D), jnp.float32) * s, 'bv': jnp.zeros((D,), jnp.float32), 'Wo': jax.random.normal(ks[4], (D, D), jnp.float32) * s, 'bo': jnp.zeros((D,), jnp.float32), 'gate_W': jax.random.normal(ks[5], (D, E), jnp.float32) * s, 'gate_b': jnp.zeros((E,), jnp.float32), 'W1': jax.random.normal(ks[6], (E, D, FF), jnp.float32) * s, 'b1': jnp.zeros((E, FF), jnp.float32), 'W2': jax.random.normal(ks[7], (E, FF, D), jnp.float32) * s, 'b2': jnp.zeros((E, D), jnp.float32)}
    _L0_ffn_all = _L0_ffn_setup()
    _L0_ffn_in = {k: v for k, v in _L0_ffn_all.items() if k in ('ln1_g', 'ln1_b', 'Wq', 'bq', 'Wk', 'bk', 'Wv', 'bv', 'Wo', 'bo', 'gate_W', 'gate_b', 'W1', 'b1', 'W2', 'b2')}
    del _L0_ffn_all

    def _L1_gnn_setup():
        import jax, jax.numpy as jnp
        import numpy as np
        N, E, H, D_IN, D_PRIME = (6250, 100000, 8, 512, 64)

        def _segment_softmax(scores, seg, num_segments):
            smax = jax.ops.segment_max(scores, seg, num_segments=num_segments)
            ex = jnp.exp(scores - smax[seg])
            denom = jax.ops.segment_sum(ex, seg, num_segments=num_segments)
            return ex / denom[seg]
        key = jax.random.key(seed)
        ks = jax.random.split(key, 6)
        x = jax.random.normal(ks[0], (N, D_IN), dtype=jnp.float32)
        edge_index = jax.random.randint(ks[1], (2, E), 0, N)
        Ws = jax.random.normal(ks[2], (H, D_IN, D_PRIME), dtype=jnp.float32) * 0.05
        Wb = jax.random.normal(ks[3], (H, D_PRIME), dtype=jnp.float32) * 0.05
        a_w = jax.random.normal(ks[4], (H, 2 * D_PRIME), dtype=jnp.float32) * 0.05
        a_b = jax.random.normal(ks[5], (H,), dtype=jnp.float32) * 0.05
        return dict(x=x, edge_index=edge_index, Ws=Ws, Wb=Wb, a_w=a_w, a_b=a_b)
    _L1_gnn_all = _L1_gnn_setup()
    _L1_gnn_in = {k: v for k, v in _L1_gnn_all.items() if k in ('Ws', 'Wb', 'a_w', 'a_b')}
    del _L1_gnn_all

    def _L1_ffn_setup():
        import jax, jax.numpy as jnp
        import numpy as np
        MARK_AX = 0
        OP_MUL = 1
        OPCODE_BASE = 2
        ALU_LO, ALU_HI = (64, 80)
        AX_CARRY_LO, AX_CARRY_HI = (96, 112)
        OUTPUT_LO, OUTPUT_HI = (128, 144)
        NIB_A, NIB_B, RESULT, OP_START = (0, 1, 2, 3)
        GE_DIM = 160
        N_POS = 8
        N_LAYERS = 7
        OPCODE = 27

        def _decode_nibble(x16):
            return jnp.argmax(x16 > 0.5, axis=-1).astype(x16.dtype)
        key = jax.random.key(seed)
        k1, k2, k3 = jax.random.split(key, 3)
        x_bd = jax.random.uniform(k1, (4, 1024, 512), dtype=jnp.float32)
        W = jax.random.normal(k2, (N_LAYERS, GE_DIM, GE_DIM), dtype=jnp.float32) * 0.05
        b = jax.random.normal(k3, (N_LAYERS, GE_DIM), dtype=jnp.float32) * 0.01
        return {'x_bd': x_bd, 'W': W, 'b': b}
    _L1_ffn_all = _L1_ffn_setup()
    _L1_ffn_in = {k: v for k, v in _L1_ffn_all.items() if k in ('W', 'b')}
    del _L1_ffn_all
    return {'x': x, 'src': src, 'dst': dst, 'L0_gnn_W_self': _L0_gnn_in['W_self'], 'L0_gnn_W_neigh': _L0_gnn_in['W_neigh'], 'L0_gnn_bias': _L0_gnn_in['bias'], 'L0_gnn_gamma': _L0_gnn_in['gamma'], 'L0_gnn_beta': _L0_gnn_in['beta'], 'L0_ffn_ln1_g': _L0_ffn_in['ln1_g'], 'L0_ffn_ln1_b': _L0_ffn_in['ln1_b'], 'L0_ffn_Wq': _L0_ffn_in['Wq'], 'L0_ffn_bq': _L0_ffn_in['bq'], 'L0_ffn_Wk': _L0_ffn_in['Wk'], 'L0_ffn_bk': _L0_ffn_in['bk'], 'L0_ffn_Wv': _L0_ffn_in['Wv'], 'L0_ffn_bv': _L0_ffn_in['bv'], 'L0_ffn_Wo': _L0_ffn_in['Wo'], 'L0_ffn_bo': _L0_ffn_in['bo'], 'L0_ffn_gate_W': _L0_ffn_in['gate_W'], 'L0_ffn_gate_b': _L0_ffn_in['gate_b'], 'L0_ffn_W1': _L0_ffn_in['W1'], 'L0_ffn_b1': _L0_ffn_in['b1'], 'L0_ffn_W2': _L0_ffn_in['W2'], 'L0_ffn_b2': _L0_ffn_in['b2'], 'L1_gnn_Ws': _L1_gnn_in['Ws'], 'L1_gnn_Wb': _L1_gnn_in['Wb'], 'L1_gnn_a_w': _L1_gnn_in['a_w'], 'L1_gnn_a_b': _L1_gnn_in['a_b'], 'L1_ffn_W': _L1_ffn_in['W'], 'L1_ffn_b': _L1_ffn_in['b']}

def reference(x, src, dst, L0_gnn_W_self, L0_gnn_W_neigh, L0_gnn_bias, L0_gnn_gamma, L0_gnn_beta, L0_ffn_ln1_g, L0_ffn_ln1_b, L0_ffn_Wq, L0_ffn_bq, L0_ffn_Wk, L0_ffn_bk, L0_ffn_Wv, L0_ffn_bv, L0_ffn_Wo, L0_ffn_bo, L0_ffn_gate_W, L0_ffn_gate_b, L0_ffn_W1, L0_ffn_b1, L0_ffn_W2, L0_ffn_b2, L1_gnn_Ws, L1_gnn_Wb, L1_gnn_a_w, L1_gnn_a_b, L1_ffn_W, L1_ffn_b):
    import jax
    import jax.numpy as jnp

    def _L0_gnn_ref(x, edge_src, edge_dst, deg, W_self, W_neigh, bias, gamma, beta):
        import jax, jax.numpy as jnp
        import numpy as np
        N_NODES = 1250
        N_EDGES = 20000
        IN_DIM = 512
        OUT_DIM = 512
        LN_EPS = 1e-05
        n = x.shape[0]
        h_self = jnp.einsum('nd,od->no', x, W_self)
        neigh_sum = jax.ops.segment_sum(x[edge_src], edge_dst, num_segments=n)
        neigh_mean = neigh_sum / jnp.maximum(deg, 1.0)[:, None]
        h_neigh = jnp.einsum('nd,od->no', neigh_mean, W_neigh)
        h = h_self + h_neigh + bias
        mu = jnp.mean(h, axis=-1, keepdims=True)
        var = jnp.mean(jnp.square(h - mu), axis=-1, keepdims=True)
        h = (h - mu) * jax.lax.rsqrt(var + LN_EPS)
        return h * gamma + beta

    def _L0_ffn_ref(x, ln1_g, ln1_b, Wq, bq, Wk, bk, Wv, bv, Wo, bo, gate_W, gate_b, W1, b1, W2, b2):
        import jax, jax.numpy as jnp
        import numpy as np
        B, S, D, H, E = (4, 256, 512, 8, 8)
        FF = 4 * D
        HD = D // H
        EPS = 1e-05

        def _layernorm(x, g, b):
            mu = jnp.mean(x, axis=-1, keepdims=True)
            var = jnp.mean((x - mu) ** 2, axis=-1, keepdims=True)
            return (x - mu) * jax.lax.rsqrt(var + EPS) * g + b
        b, s, d = x.shape
        q = (x @ Wq + bq).reshape(b, s, H, HD)
        k = (x @ Wk + bk).reshape(b, s, H, HD)
        v = (x @ Wv + bv).reshape(b, s, H, HD)
        scores = jnp.einsum('bqhd,bkhd->bhqk', q, k) / jnp.sqrt(jnp.float32(HD))
        attn = jax.nn.softmax(scores, axis=-1)
        o = jnp.einsum('bhqk,bkhd->bqhd', attn, v).reshape(b, s, d) @ Wo + bo
        h = _layernorm(x + o, ln1_g, ln1_b)
        t = h.reshape(b * s, d)
        probs = jax.nn.softmax(t @ gate_W + gate_b, axis=-1)
        idx = jnp.argmax(probs, axis=-1)
        gw = jnp.max(probs, axis=-1)
        hid = jax.nn.gelu(jnp.einsum('nd,edf->enf', t, W1) + b1[:, None, :])
        out_all = jnp.einsum('enf,efd->end', hid, W2) + b2[:, None, :]
        onehot = jax.nn.one_hot(idx, E, dtype=t.dtype)
        out = jnp.einsum('ne,end->nd', onehot, out_all)
        out = out * gw[:, None]
        return out.reshape(b, s, d)

    def _L1_gnn_ref(x, edge_index, Ws, Wb, a_w, a_b):
        import jax, jax.numpy as jnp
        import numpy as np
        N, E, H, D_IN, D_PRIME = (6250, 100000, 8, 512, 64)

        def _segment_softmax(scores, seg, num_segments):
            smax = jax.ops.segment_max(scores, seg, num_segments=num_segments)
            ex = jnp.exp(scores - smax[seg])
            denom = jax.ops.segment_sum(ex, seg, num_segments=num_segments)
            return ex / denom[seg]
        v_src, v_tgt = (edge_index[0], edge_index[1])
        n = x.shape[0]
        outs = []
        for h in range(Ws.shape[0]):
            Wx = x @ Ws[h] + Wb[h]
            d = Wx.shape[-1]
            s = Wx[v_tgt] @ a_w[h, :d] + Wx[v_src] @ a_w[h, d:] + a_b[h]
            s = jax.nn.leaky_relu(s, negative_slope=0.2)
            alpha = _segment_softmax(s, v_tgt, n)
            outs.append(jax.ops.segment_sum(alpha[:, None] * Wx[v_src], v_tgt, num_segments=n))
        return jnp.stack(outs, axis=1).reshape(n, -1)

    def _L1_ffn_ref(x_bd, W, b):
        import jax, jax.numpy as jnp
        import numpy as np
        MARK_AX = 0
        OP_MUL = 1
        OPCODE_BASE = 2
        ALU_LO, ALU_HI = (64, 80)
        AX_CARRY_LO, AX_CARRY_HI = (96, 112)
        OUTPUT_LO, OUTPUT_HI = (128, 144)
        NIB_A, NIB_B, RESULT, OP_START = (0, 1, 2, 3)
        GE_DIM = 160
        N_POS = 8
        N_LAYERS = 7
        OPCODE = 27

        def _decode_nibble(x16):
            return jnp.argmax(x16 > 0.5, axis=-1).astype(x16.dtype)
        B, S, D = x_bd.shape
        mask = (x_bd[..., MARK_AX] >= 0.5) & (x_bd[..., OP_MUL] >= 0.5)
        a_lo = _decode_nibble(x_bd[..., ALU_LO:ALU_LO + 16])
        a_hi = _decode_nibble(x_bd[..., ALU_HI:ALU_HI + 16])
        b_lo = _decode_nibble(x_bd[..., AX_CARRY_LO:AX_CARRY_LO + 16])
        b_hi = _decode_nibble(x_bd[..., AX_CARRY_HI:AX_CARRY_HI + 16])
        op_val = x_bd[..., OPCODE_BASE + OPCODE]
        x_ge = jnp.zeros((B, S, N_POS, GE_DIM), dtype=x_bd.dtype)
        x_ge = x_ge.at[..., 0, NIB_A].set(a_lo)
        x_ge = x_ge.at[..., 1, NIB_A].set(a_hi)
        x_ge = x_ge.at[..., 0, NIB_B].set(b_lo)
        x_ge = x_ge.at[..., 1, NIB_B].set(b_hi)
        x_ge = x_ge.at[..., :, OP_START + OPCODE].set(op_val[..., None])
        h = x_ge
        for i in range(N_LAYERS):
            h = jnp.einsum('bspd,ed->bspe', h, W[i]) + b[i]
            if i < N_LAYERS - 1:
                h = jax.nn.relu(h)
        res_lo = jnp.clip(jnp.round(h[..., 0, RESULT]), 0, 15).astype(jnp.int32)
        res_hi = jnp.clip(jnp.round(h[..., 1, RESULT]), 0, 15).astype(jnp.int32)
        m = mask[..., None].astype(x_bd.dtype)
        add_lo = 2.0 * jax.nn.one_hot(res_lo, 16, dtype=x_bd.dtype) * m
        add_hi = 2.0 * jax.nn.one_hot(res_hi, 16, dtype=x_bd.dtype) * m
        out = x_bd.at[..., OUTPUT_LO:OUTPUT_LO + 16].add(add_lo)
        out = out.at[..., OUTPUT_HI:OUTPUT_HI + 16].add(add_hi)
        return out
    edge_index = jnp.stack([src, dst])
    deg = jnp.maximum(jax.ops.segment_sum(jnp.ones(dst.shape, jnp.float32), dst, num_segments=1250), 1.0)
    x = x + _L0_gnn_ref(_layernorm(x, axis=-1), src, dst, deg, L0_gnn_W_self, L0_gnn_W_neigh, L0_gnn_bias, L0_gnn_gamma, L0_gnn_beta)
    x = x + _L0_ffn_ref(_layernorm(x, axis=-1)[None], L0_ffn_ln1_g, L0_ffn_ln1_b, L0_ffn_Wq, L0_ffn_bq, L0_ffn_Wk, L0_ffn_bk, L0_ffn_Wv, L0_ffn_bv, L0_ffn_Wo, L0_ffn_bo, L0_ffn_gate_W, L0_ffn_gate_b, L0_ffn_W1, L0_ffn_b1, L0_ffn_W2, L0_ffn_b2)[0]
    x = x + _L1_gnn_ref(_layernorm(x, axis=-1), edge_index, L1_gnn_Ws, L1_gnn_Wb, L1_gnn_a_w, L1_gnn_a_b)
    x = x + _L1_ffn_ref(_layernorm(x, axis=-1)[None], L1_ffn_W, L1_ffn_b)[0]
    return x

_drawn_inputs = setup_inputs


def setup_inputs(seed=0):
    import zlib

    import numpy as np

    out = dict(_drawn_inputs(seed))
    spreads = {'L0_gnn_bias': (0.0, 0.1),
     'L0_gnn_gamma': (1.0, 0.2),
     'L0_gnn_beta': (0.0, 0.1),
     'L0_ffn_ln1_g': (1.0, 0.6),
     'L0_ffn_ln1_b': (0.0, 0.678),
     'L0_ffn_bq': (0.0, 0.8),
     'L0_ffn_bk': (0.0, 2.0),
     'L0_ffn_bv': (0.0, 0.8),
     'L0_ffn_bo': (0.0, 0.683),
     'L0_ffn_gate_b': (0.0, 0.332),
     'L0_ffn_b1': (0.0, 0.8),
     'L0_ffn_b2': (0.0, 0.451)}
    factors = {'L0_ffn_Wq': 8.0,
     'L0_ffn_Wk': 8.0,
     'L0_ffn_Wv': 8.0,
     'L0_ffn_Wo': 8.0,
     'L1_gnn_a_b': 23.88}
    for name, (base, spread) in spreads.items():
        noise = np.random.default_rng([zlib.crc32(name.encode()), seed]).standard_normal(out[name].shape)
        drawn = base * np.exp(spread * noise) if base else spread * noise
        out[name] = jnp.asarray(drawn.astype(out[name].dtype))
    for name, factor in factors.items():
        out[name] = (out[name] * factor).astype(out[name].dtype)
    return out
```

```python
from contextlib import ExitStack

import concourse.bass as bass
from concourse import mybir

ALU = mybir.AluOpType
ACT = mybir.ActivationFunctionType
AX = mybir.AxisListType
F32 = mybir.dt.float32
BF16 = mybir.dt.bfloat16
I32 = mybir.dt.int32
I16 = mybir.dt.int16

NODES = 1250
EDGES = 20000
D = 512
P = 125
T = NODES // P
C = D // 128
EPS = 1e-5

RING = 3
CHUNKS = 6
GROUP = 128 * CHUNKS
GROUPS = -(-((EDGES + T * (GROUP - 1)) // GROUP) // 2) * 2
NOWHERE = 5000.0
EXPERTS = 8
FF = 4 * D
HEADS = 8
HD = D // HEADS
SLOPE = 0.2
LOWEST = -1e20
NEVER = 1e30
SLOT = 128
SLOTS = (NODES + EXPERTS * (SLOT - 1)) // SLOT
BANKS = 8
QUADS = [(0, 4), (4, 4), (8, 2)]
COLS = [(0, 512), (512, 512), (1024, 226)]


class Steps:

    def __init__(self, eng, sem, base=0):
        self.eng, self.sem, self.base, self.n = eng, sem, base, 0

    def __call__(self, ins):
        self.n += 1
        ins.then_inc(self.sem, 1)
        self.eng.wait_ge(self.sem, self.base + self.n)


class Build:
    def __init__(self, nc, a, out, ctx):
        self.nc, self.a, self.out, self.ctx = nc, a, out, ctx
        self.full = [self.sem(ctx, f"bank_full{i}") for i in range(BANKS)]
        self.free = [self.sem(ctx, f"bank_free{i}") for i in range(BANKS)]
        self.filled, self.emptied = [0] * BANKS, [0] * BANKS

    def scope(self):
        return ExitStack()

    def sb(self, ctx, name, shape, dt=F32):
        return ctx.enter_context(self.nc.sbuf_tensor(name, shape, dt))

    def ps(self, ctx, name, shape, dt=F32):
        return ctx.enter_context(self.nc.psum_tensor(name, shape, dt))

    def sem(self, ctx, name):
        return self.ctx.enter_context(self.nc.semaphore(name))


def index_edges(b, keep):
    nc, a = b.nc, b.a
    with ExitStack() as ctx:
        src_i = b.sb(ctx, "src_i", [P, EDGES // P], I32)
        dst_i = b.sb(ctx, "dst_i", [P, EDGES // P], I32)
        src_f = b.sb(ctx, "src_f", [P, EDGES // P])
        dst_f = b.sb(ctx, "dst_f", [P, EDGES // P])
        pad = b.sb(ctx, "pad", [2, GROUP])
        bounds = b.sb(ctx, "bounds", [P, T])
        below = b.sb(ctx, "below", [P, T, EDGES // P])
        part = b.sb(ctx, "part", [P, T])
        J = -(-EDGES // GROUP)
        steps_j = b.sb(ctx, "steps_j", [128, J])
        group_no = b.sb(ctx, "group_no", [128, GROUPS])
        more = b.sb(ctx, "more", [128, T, J])
        lo = b.sb(ctx, "lo", [128, T + 1])
        length = b.sb(ctx, "length", [128, T])
        n_groups = b.sb(ctx, "n_groups", [128, T])
        ends = b.sb(ctx, "ends", [128, T + 1])
        first = b.sb(ctx, "first", [128, T])
        past = b.sb(ctx, "past", [128, GROUPS, T])
        tile_of = b.sb(ctx, "tile_of", [128, GROUPS])
        shift = b.sb(ctx, "shift", [128, GROUPS])
        offset = b.sb(ctx, "offset", [128, GROUPS])
        counts = b.ps(ctx, "counts", [128, T])
        edges_in = b.sem(ctx, "edges_in")
        const_ok = b.sem(ctx, "const_ok")
        ident_ok = b.sem(ctx, "ident_ok")
        lists_ok = b.sem(ctx, "lists_ok")
        zeros = b.sb(ctx, "zeros", [128, D])
        zeros_ok = b.sem(ctx, "zeros_ok")
        zeros_out = b.sem(ctx, "zeros_out")
        lists_out = b.sem(ctx, "lists_out")
        parts_ok = b.sem(ctx, "parts_ok")
        counts_ok = b.sem(ctx, "counts_ok")
        step = b.sem(ctx, "index_step")
        with nc.Block() as block:

            @block.sync
            def _(sp):
                sp.dma_start(dst_i[:], a["dst"].rearrange("(p e) -> p e", p=P)).then_inc(edges_in, 16)
                sp.dma_start(src_i[:], a["src"].rearrange("(p e) -> p e", p=P)).then_inc(edges_in, 16)
                sp.dma_start(keep.x, a["x"].rearrange("(t p) d -> p t d", p=P)).then_inc(keep.x_in, 16)
                for w, name in enumerate(("L0_gnn_W_self", "L0_gnn_W_neigh")):
                    sp.dma_start(keep.w_rows[:, w], a[name].rearrange("(k p) d -> p k d", p=128)).then_inc(keep.w_in, 16)
                sp.wait_ge(zeros_ok, 1)
                sp.dma_start(keep.slots_in.rearrange("(s p) d -> p s d", p=SLOT),
                             zeros[:].unsqueeze(1).to_broadcast([128, SLOTS + 1, D])).then_inc(zeros_out, 16)
                sp.wait_ge(lists_ok, 2)
                sp.wait_ge(const_ok, 1)
                sp.dma_start(keep.edges[0, 0:EDGES].rearrange("(p e) -> p e", p=P), src_f[:]).then_inc(lists_out, 16)
                sp.dma_start(keep.edges[1, 0:EDGES].rearrange("(p e) -> p e", p=P), dst_f[:]).then_inc(lists_out, 16)
                sp.dma_start(keep.edges[:, EDGES:EDGES + GROUP], pad[:]).then_inc(lists_out, 16)
                sp.wait_ge(lists_out, 48)
                sp.wait_ge(zeros_out, 16)

            @block.gpsimd
            def _(pool):
                pool.memset(zeros[:], 0.0).then_inc(zeros_ok, 1)
                pool.memset(pad[:], NOWHERE).then_inc(const_ok, 1)
                pool.iota(bounds[:], [[P, T]], base=P, channel_multiplier=0,
                          allow_small_or_imprecise_dtypes=True).then_inc(const_ok, 1)
                pool.memset(keep.ones[:], 1.0).then_inc(const_ok, 1)
                pool.memset(keep.minus_half[:], -0.5)
                pool.iota(steps_j[:], [[GROUP, J]], base=0, channel_multiplier=0,
                          allow_small_or_imprecise_dtypes=True).then_inc(const_ok, 1)
                pool.iota(group_no[:], [[1, GROUPS]], base=0, channel_multiplier=0,
                          allow_small_or_imprecise_dtypes=True).then_inc(const_ok, 1)
                pool.iota(keep.node_no[:], [[1, NODES]], base=0, channel_multiplier=0).then_inc(const_ok, 1)
                pool.memset(keep.ident[:], 0.0).then_inc(ident_ok, 1)
                pool.wait_ge(ident_ok, 1)
                pool.affine_select(out=keep.ident[:], in_=keep.ident[:], compare_op=ALU.not_equal, fill=1.0,
                                   base=0, pattern=[[-1, 128]], channel_multiplier=1).then_inc(ident_ok, 1)
                pool.memset(keep.count[:], 0.0).then_inc(ident_ok, 1)

            @block.tensor
            def _(pe):
                pe.wait_ge(parts_ok, 1)
                pe.wait_ge(const_ok, 6)
                pe.matmul(counts[:], keep.ones[0:P, :], part[:], start=True, stop=True).then_inc(counts_ok, 1)

            @block.vector
            def _(v):
                v.wait_ge(edges_in, 32)
                v.tensor_copy(dst_f[:], dst_i[:]).then_inc(lists_ok, 1)
                v.tensor_copy(src_f[:], src_i[:]).then_inc(lists_ok, 1)
                v.wait_ge(lists_ok, 2)
                v.wait_ge(const_ok, 6)
                link = Steps(v, step)
                link(v.tensor_tensor(below[:], dst_f[:].unsqueeze(1).to_broadcast([P, T, EDGES // P]),
                                     bounds[:].unsqueeze(2).to_broadcast([P, T, EDGES // P]), ALU.is_lt))
                v.tensor_reduce(part[:], below[:], AX.X, ALU.add).then_inc(parts_ok, 1)
                link(v.memset(lo[:, 0:1], 0.0))
                link(v.memset(ends[:, 0:1], 0.0))
                v.wait_ge(counts_ok, 1)
                link(v.tensor_copy(lo[:, 1:T + 1], counts[:]))
                link(v.tensor_tensor(length[:], lo[:, 1:T + 1], lo[:, 0:T], ALU.subtract))
                link(v.tensor_tensor(more[:], length[:].unsqueeze(2).to_broadcast([128, T, J]),
                                     steps_j[:].unsqueeze(1).to_broadcast([128, T, J]), ALU.is_gt))
                link(v.tensor_reduce(n_groups[:], more[:], AX.X, ALU.add))
                link(v.tensor_tensor_scan(ends[:, 1:T + 1], keep.ones[:, 0:T], n_groups[:], 0.0, ALU.mult, ALU.add))
                link(v.scalar_tensor_tensor(first[:], ends[:, 0:T], -float(GROUP), lo[:, 0:T], ALU.mult, ALU.add))
                link(v.tensor_tensor(past[:], group_no[:].unsqueeze(2).to_broadcast([128, GROUPS, T]),
                                     ends[:, 1:T + 1].unsqueeze(1).to_broadcast([128, GROUPS, T]), ALU.is_ge))
                link(v.tensor_reduce(tile_of[:], past[:], AX.X, ALU.add))
                link(v.tensor_scalar(keep.tile_base[:], tile_of[:], float(P), None, ALU.mult))
                link(v.tensor_scalar(shift[:], past[:, :, 0], -1.0, 1.0, ALU.mult, ALU.add))
                link(v.tensor_scalar(offset[:], shift[:], first[:, 0:1], None, ALU.mult))
                for t in range(1, T):
                    link(v.tensor_tensor(shift[:], past[:, :, t - 1], past[:, :, t], ALU.subtract))
                    link(v.scalar_tensor_tensor(offset[:], shift[:], first[:, t:t + 1], offset[:], ALU.mult, ALU.add))
                link(v.scalar_tensor_tensor(offset[:], group_no[:], float(GROUP), offset[:], ALU.mult, ALU.add))
                link(v.tensor_scalar(offset[:], offset[:], float(EDGES), 0.0, ALU.min, ALU.max))
                link(v.tensor_copy(keep.group_offset[:], offset[0:1, :]))
                link(v.tensor_copy(keep.group_tile[:], tile_of[0:1, :]))


def count_edges(b, keep):
    nc = b.nc
    with ExitStack() as ctx:
        ends = b.sb(ctx, "edge_ends", [128, 2, 2, CHUNKS])
        near = b.sb(ctx, "near", [128, 2, CHUNKS])
        hot_src = b.sb(ctx, "hot_src", [128, RING, NODES], BF16)
        hot_dst = b.sb(ctx, "hot_dst", [128, RING, P], BF16)
        sums = b.ps(ctx, "sums", [128, 2, 2048])
        ends_in = [b.sem(ctx, f"ends_in{u}") for u in range(2)]
        near_ok = b.sem(ctx, "near_ok")
        hot_ok = b.sem(ctx, "hot_ok")
        hot_free = b.sem(ctx, "hot_free")
        sums_added = b.sem(ctx, "sums_added")
        with nc.Block() as block:

            @block.sync
            def _(sp):
                def load(m, u):
                    at = sp.value_load(keep.group_offset[0:1, bass.ds(m, 1)], min_val=0, max_val=EDGES)
                    sp.dma_start(ends[:, u], keep.edges[:, bass.ds(at, GROUP)].rearrange("e (p c) -> p e c", p=128)
                                 ).then_inc(ends_in[u], 16)

                load(0, 0)
                load(1, 1)
                with sp.Fori(1, GROUPS // 2) as i:
                    for u in range(2):
                        sp.wait_ge(hot_ok, CHUNKS * (2 * i + u - 1))
                        load(2 * i + u, u)

            @block.vector
            def _(v):
                v.sem_inc(hot_free, RING)

                def hots(m, u, k):
                    v.wait_ge(ends_in[u], 16 * k + 16)
                    v.tensor_scalar(near[:, u], ends[:, u, 1], keep.tile_base[:, bass.ds(m, 1)], None,
                                    ALU.subtract).then_inc(near_ok, 1)
                    v.wait_ge(near_ok, m + 1)
                    for c in range(CHUNKS):
                        v.wait_ge(hot_free, CHUNKS * m + c + 1)
                        n = c % RING
                        v.tensor_scalar(hot_dst[:, n], keep.node_no[:, 0:P], near[:, u, c:c + 1], None, ALU.is_equal)
                        v.tensor_scalar(hot_src[:, n], keep.node_no[:], ends[:, u, 0, c:c + 1], None,
                                        ALU.is_equal).then_inc(hot_ok, 1)

                def add(m, u):
                    v.wait_ge(hot_free, RING + CHUNKS * (m + 1))
                    row = v.value_load(keep.group_tile[0:1, bass.ds(m, 1)], min_val=0, max_val=T)
                    v.wait_ge(sums_added, m)
                    to = keep.count[:, bass.ds(row, 1), :].rearrange("p a n -> p (a n)")
                    v.tensor_tensor(to, sums[0:P, u, 0:NODES], to, ALU.add).then_inc(sums_added, 1)

                hots(0, 0, 0)
                with v.Fori(0, GROUPS // 2 - 1) as i:
                    hots(2 * i + 1, 1, i)
                    add(2 * i, 0)
                    hots(2 * i + 2, 0, i + 1)
                    add(2 * i + 1, 1)
                hots(GROUPS - 1, 1, GROUPS // 2 - 1)
                add(GROUPS - 2, 0)
                add(GROUPS - 1, 1)

            @block.tensor
            def _(pe):
                def group(m, u):
                    for c in range(CHUNKS):
                        pe.wait_ge(hot_ok, CHUNKS * m + c + 1)
                        n = c % RING
                        for c0, w in COLS:
                            ins = pe.matmul(sums[0:P, u, c0:c0 + w], hot_dst[:, n], hot_src[:, n, c0:c0 + w],
                                            start=(c == 0), stop=(c == CHUNKS - 1))
                        ins.then_inc(hot_free, 1)

                group(0, 0)
                group(1, 1)
                with pe.Fori(1, GROUPS // 2) as i:
                    for u in range(2):
                        pe.wait_ge(sums_added, 2 * i + u - 1)
                        group(2 * i + u, u)


class Banks:

    def __init__(self, b, ctx, name, ring=BANKS):
        self.b, self.ring = b, ring
        self.at = b.ps(ctx, name, [128, ring, 512])
        self.full0, self.free0 = list(b.filled), list(b.emptied)

    def __getitem__(self, j):
        return self.at[:, j % self.ring]

    def wait_emptied(self, eng, j):
        i = j % self.ring
        eng.wait_ge(self.b.free[i], self.free0[i] + j // self.ring + 1)

    def wait_free(self, pe, j):
        if j >= self.ring:
            self.wait_emptied(pe, j - self.ring)

    def wait_full(self, eng, j):
        i = j % self.ring
        eng.wait_ge(self.b.full[i], self.full0[i] + j // self.ring + 1)

    def filled(self, ins, j):
        self.b.filled[j % self.ring] += 1
        ins.then_inc(self.b.full[j % self.ring], 1)

    def emptied(self, ins, j):
        self.b.emptied[j % self.ring] += 1
        ins.then_inc(self.b.free[j % self.ring], 1)

    def release(self, eng, j):
        self.b.emptied[j % self.ring] += 1
        eng.sem_inc(self.b.free[j % self.ring], 1)


def variance_root(pool, rstd, var, minus_half):
    return pool.tensor_tensor(rstd, var, minus_half, ALU.pow)


def sage(b, keep):
    nc, a = b.nc, b.a
    with ExitStack() as ctx:
        w_t = b.sb(ctx, "w_t", [128, 2, C, D])
        xt = b.sb(ctx, "xt", [128, T * D])
        xn_t = xt[:, 0:C * NODES].rearrange("p (c n) -> p c n", c=C)
        x_again = xt[0:P, :].rearrange("p (t d) -> p t d", t=T)
        from_src = b.sb(ctx, "from_src", [P, 2, T, P])
        absent = b.sb(ctx, "absent", [P, 2, NODES], BF16)
        tiny = b.sb(ctx, "tiny", [P, 1])
        logs = b.sb(ctx, "logs", [P, 2, T, P])
        worth = b.sb(ctx, "worth_part", [P, 2, T, P])
        tiny_ok = b.sem(ctx, "tiny_ok")
        logs_ok = b.sem(ctx, "logs_ok")
        worth_ok = b.sem(ctx, "worth_ok")
        worth_out = [b.sem(ctx, f"worth_out{u}") for u in range(2)]
        row3 = b.sb(ctx, "sage_rows", [P, 3, D])
        stats = b.sb(ctx, "stats", [P, T, 3, 6])
        mv = b.sb(ctx, "mv", [P, T, 3, 2])
        var = b.sb(ctx, "var", [P, T, 3])
        rstd = b.sb(ctx, "rstd", [P, T, 3])
        degree = b.sb(ctx, "degree", [P, T])
        rdeg = b.sb(ctx, "rdeg", [P, T])
        banks = Banks(b, ctx, "sage_banks")
        rows_in = b.sem(ctx, "sage_rows_in")
        x_again_in = b.sem(ctx, "x_again_in")
        var_ok = b.sem(ctx, "var_ok")
        rstd_ok = b.sem(ctx, "rstd_ok")
        xn_ok = b.sem(ctx, "xn_ok")
        wt_ok = b.sem(ctx, "wt_ok")
        xnt_ok = b.sem(ctx, "xnt_ok")
        z_ok = b.sem(ctx, "z_ok")
        from_ok = b.sem(ctx, "from_ok")
        agg_ok = b.sem(ctx, "agg_ok")
        absent_ok = b.sem(ctx, "absent_ok")
        absent_out = [b.sem(ctx, f"absent_out{u}") for u in range(2)]
        step = b.sem(ctx, "sage_step")
        vstep = b.sem(ctx, "sage_v_step")

        W0 = 0
        X0 = W0 + 2 * C
        Z0 = X0 + C * len(QUADS)
        S0 = Z0 + T
        E0 = S0 + T
        def turn_job(t, q):
            return E0 + (q if t == 0 else 3 + 4 * (t - 1) + q)
        def sum_job(t):
            return E0 + (3 + 4 * t + 3 if t < T - 1 else 3 + 4 * (T - 1))

        with nc.Block() as block:

            @block.sync
            def _(sp):
                for k, name in enumerate(("L0_gnn_bias", "L0_gnn_gamma", "L0_gnn_beta")):
                    sp.dma_start(row3[:, k], a[name].unsqueeze(0).to_broadcast([P, D])).then_inc(rows_in, 16)
                for t in range(T):
                    sp.wait_ge(absent_ok, t + 1)
                    sp.dma_start(keep.absent[t * P:(t + 1) * P, :], absent[:, t % 2]).then_inc(absent_out[t % 2], 16)
                banks.wait_full(sp, S0 + T - 1)
                sp.dma_start(x_again, a["x"].rearrange("(t p) d -> p t d", p=P)).then_inc(x_again_in, 16)
                for t in range(T):
                    sp.wait_ge(worth_ok, 2 * t + 2)
                    sp.dma_start(keep.worth_rows.rearrange("(s p) n -> p s n", p=P)[:, :, P * t:P * t + P], worth[:, t % 2]
                                 ).then_inc(worth_out[t % 2], 16)
                for u in range(2):
                    sp.wait_ge(absent_out[u], 16 * T // 2)
                    sp.wait_ge(worth_out[u], 16 * T // 2)

            @block.tensor
            def _(pe):
                pe.wait_ge(keep.w_in, 32)
                for w in range(2):
                    for c in range(C):
                        j = W0 + w * C + c
                        banks.wait_free(pe, j)
                        for k in range(C):
                            ins = pe.transpose(banks[j][:, 128 * k:128 * k + 128],
                                               keep.w_rows[:, w, k, 128 * c:128 * c + 128], keep.ident[:])
                        banks.filled(ins, j)
                for q, (t0, n) in enumerate(QUADS):
                    pe.wait_ge(xn_ok, t0 + n)
                    for c in range(C):
                        j = X0 + C * q + c
                        banks.wait_free(pe, j)
                        for t in range(n):
                            ins = pe.transpose(banks[j][:, P * t:P * t + P],
                                               keep.y[:, t0 + t, 128 * c:128 * c + 128], keep.ident[0:P, 0:P])
                        banks.filled(ins, j)
                pe.wait_ge(wt_ok, 2 * C)
                pe.wait_ge(xnt_ok, C * len(QUADS))
                for w, first in ((1, Z0), (0, S0)):
                    for t in range(T):
                        banks.wait_free(pe, first + t)
                        for c in range(C):
                            ins = pe.matmul(banks[first + t][0:P, :], xn_t[:, c, P * t:P * t + P], w_t[:, w, c],
                                            start=(c == 0), stop=(c == C - 1))
                        banks.filled(ins, first + t)

                def turn(t):
                    for q, (s0, n) in enumerate(QUADS):
                        j = turn_job(t, q)
                        banks.wait_free(pe, j)
                        for s in range(n):
                            ins = pe.transpose(banks[j][0:P, P * s:P * s + P],
                                               keep.count[:, t, P * (s0 + s):P * (s0 + s) + P], keep.ident[0:P, 0:P])
                        banks.filled(ins, j)

                turn(0)
                pe.wait_ge(z_ok, T)
                for t in range(T):
                    if t + 1 < T:
                        turn(t + 1)
                    pe.wait_ge(from_ok, 3 * t + 3)
                    j = sum_job(t)
                    banks.wait_free(pe, j)
                    for s in range(T):
                        ins = pe.matmul(banks[j][0:P, :], from_src[:, t % 2, s], keep.y[:, s],
                                        start=(s == 0), stop=(s == T - 1))
                    banks.filled(ins, j)

            @block.scalar
            def _(act):
                def evacuate(j, to, of, done):
                    banks.wait_full(act, j)
                    banks.emptied(act.activation(to, of, ACT.Copy), j)

                for j in range(2 * C):
                    banks.wait_full(act, W0 + j)
                    act.activation(w_t[:, j // C, j % C], banks[W0 + j][:, :], ACT.Copy).then_inc(wt_ok, 1)
                    act.wait_ge(wt_ok, j + 1)
                    banks.release(act, W0 + j)
                for q, (t0, n) in enumerate(QUADS):
                    for c in range(C):
                        j = X0 + C * q + c
                        banks.wait_full(act, j)
                        act.activation(xn_t[:, c, P * t0:P * (t0 + n)], banks[j][:, 0:P * n], ACT.Copy).then_inc(xnt_ok, 1)
                        act.wait_ge(xnt_ok, C * q + c + 1)
                        banks.release(act, j)
                for t in range(T):
                    banks.wait_full(act, Z0 + t)
                    act.activation(keep.y[:, t], banks[Z0 + t][0:P, :], ACT.Copy).then_inc(z_ok, 1)
                    act.wait_ge(z_ok, t + 1)
                    banks.release(act, Z0 + t)

                act.wait_ge(tiny_ok, 1)
                for t in range(T):
                    for q, (s0, n) in enumerate(QUADS):
                        j = turn_job(t, q)
                        banks.wait_full(act, j)
                        if t >= 2:
                            banks.wait_full(act, sum_job(t - 2))
                            act.wait_ge(worth_ok, 2 * t - 2)
                        act.activation(from_src[:, t % 2, s0:s0 + n],
                                       banks[j][0:P, 0:P * n].rearrange("p (s d) -> p s d", s=n), ACT.Copy).then_inc(from_ok, 1)
                        act.wait_ge(from_ok, 3 * t + q + 1)
                        banks.release(act, j)
                    act.activation(logs[:, t % 2], from_src[:, t % 2], ACT.Ln, bias=tiny[:]).then_inc(logs_ok, 1)

            @block.gpsimd
            def _(pool):
                pool.memset(tiny[:], 1e-19).then_inc(tiny_ok, 1)
                pool.wait_ge(var_ok, 1)
                variance_root(pool, rstd[:, :, 0], var[:, :, 0], keep.minus_half[0:P, 0:T]).then_inc(rstd_ok, 1)
                for t in range(T + 1):
                    if t < T:
                        pool.wait_ge(from_ok, 3 * t + 3)
                        if t >= 2:
                            pool.wait_ge(worth_out[t % 2], 16 * (t // 2))
                        pool.tensor_scalar(worth[:, t % 2], from_src[:, t % 2], 0.0, NEVER, ALU.is_equal, ALU.mult).then_inc(worth_ok, 1)
                        pool.wait_ge(worth_ok, 2 * t + 1)
                        pool.wait_ge(logs_ok, t + 1)
                        pool.tensor_tensor(worth[:, t % 2], worth[:, t % 2], logs[:, t % 2], ALU.subtract).then_inc(worth_ok, 1)
                    if t >= 1:
                        for k in (1, 2):
                            pool.wait_ge(var_ok, 2 * (t - 1) + k + 1)
                            variance_root(pool, rstd[:, t - 1, k:k + 1], var[:, t - 1, k:k + 1],
                                          keep.minus_half[0:P, 0:1]).then_inc(rstd_ok, 1)

            @block.vector
            def _(v):
                link = Steps(v, vstep)
                v.wait_ge(keep.x_in, 16)
                for t in range(T):
                    ins = v.bn_stats(stats[:, t, 0], keep.y[:, t])
                link(ins)
                for t in range(T):
                    ins = v.bn_aggr(mv[:, t, 0], stats[:, t, 0])
                link(ins)
                v.tensor_scalar(var[:, :, 0], mv[:, :, 0, 1], EPS, None, ALU.add).then_inc(var_ok, 1)
                v.wait_ge(rstd_ok, 1)
                for t in range(T):
                    v.tensor_scalar(keep.y[:, t], keep.y[:, t], mv[:, t, 0, 0:1], rstd[:, t, 0:1],
                                    ALU.subtract, ALU.mult).then_inc(xn_ok, 1)
                for t in range(T):
                    if t >= 2:
                        v.wait_ge(absent_out[t % 2], 16 * (t // 2))
                    v.tensor_scalar(absent[:, t % 2], keep.count[:, t], 0.0, -3e38, ALU.is_equal, ALU.mult).then_inc(absent_ok, 1)
                    link(v.tensor_reduce(degree[:, t:t + 1], keep.count[:, t], AX.X, ALU.add))
                link(v.tensor_scalar(degree[:], degree[:], 1.0, None, ALU.max))
                link(v.reciprocal(rdeg[:], degree[:]))
                v.wait_ge(rows_in, 48)
                for t in range(T):
                    banks.wait_full(v, S0 + t)
                    link(v.tensor_tensor(keep.res[:, t], banks[S0 + t][0:P, :], row3[:, 0], ALU.add))
                    banks.release(v, S0 + t)
                for t in range(T):
                    r = keep.res[:, t]
                    j = sum_job(t)
                    banks.wait_full(v, j)
                    link(v.scalar_tensor_tensor(r, banks[j][0:P, :], rdeg[:, t:t + 1], r, ALU.mult, ALU.add))
                    banks.release(v, j)

                    def normed(k, to):
                        link(v.bn_stats(stats[:, t, k], r))
                        link(v.bn_aggr(mv[:, t, k], stats[:, t, k]))
                        v.tensor_scalar(var[:, t, k:k + 1], mv[:, t, k, 1:2], EPS, None, ALU.add).then_inc(var_ok, 1)
                        v.wait_ge(rstd_ok, 2 * t + k + 1)
                        link(v.tensor_scalar(to, r, mv[:, t, k, 0:1], rstd[:, t, k:k + 1], ALU.subtract, ALU.mult))

                    normed(1, r)
                    link(v.tensor_tensor(r, r, row3[:, 1], ALU.mult))
                    link(v.tensor_tensor(r, r, row3[:, 2], ALU.add))
                    if t == 0:
                        v.wait_ge(x_again_in, 16)
                    link(v.tensor_tensor(r, r, x_again[:, t], ALU.add))
                    normed(2, x_again[:, t])
                banks.wait_full(v, sum_job(T - 1))
                v.tensor_copy(keep.y, x_again)


def turn_rows(pe, banks, first, rows, ident):
    for q, (t0, n) in enumerate(QUADS):
        for c in range(C):
            j = first + C * q + c
            banks.wait_free(pe, j)
            for t in range(n):
                ins = pe.transpose(banks[j][:, P * t:P * t + P], rows[:, t0 + t, 128 * c:128 * c + 128], ident[0:P, 0:P])
            banks.filled(ins, j)


def turned_out(act, banks, first, cols):
    for q, (t0, n) in enumerate(QUADS):
        for c in range(C):
            j = first + C * q + c
            banks.wait_full(act, j)
            banks.emptied(act.activation(cols[:, c, P * t0:P * (t0 + n)], banks[j][:, 0:P * n], ACT.Copy), j)


def attention(b, keep):
    nc, a = b.nc, b.a
    H, HD = 8, 64
    PAIRS = H // 2
    U = 2 * T
    with ExitStack() as ctx:
        y_t = b.sb(ctx, "y_t", [128, C, NODES])
        vals = b.sb(ctx, "vals", [P, T, H, HD])
        w_v = b.sb(ctx, "w_v", [128, C, D])
        bv = b.sb(ctx, "bv", [P, D])
        bq = b.sb(ctx, "bq", [128, 2, PAIRS])
        w_qk = b.sb(ctx, "w_qk", [128, 2, C, 128])
        v_in = b.sem(ctx, "v_in")
        bqk_in = b.sem(ctx, "bqk_in")
        w_qk_in = b.sem(ctx, "w_qk_in")
        sources = [a["L0_ffn_" + n].rearrange("(c p) n -> p c n", p=128) for n in ("Wq", "Wk")]
        with ExitStack() as stage:
            banks = Banks(b, stage, "value_banks")
            with nc.Block() as block:

                @block.sync
                def _(sp):
                    sp.dma_start(w_v[:], a["L0_ffn_Wv"].rearrange("(c p) n -> p c n", p=128)).then_inc(v_in, 16)
                    sp.dma_start(bv[:], a["L0_ffn_bv"].unsqueeze(0).to_broadcast([P, D])).then_inc(v_in, 16)
                    for k, n in enumerate(("bq", "bk")):
                        sp.dma_start(bq[:, k], a["L0_ffn_" + n].rearrange("(i p) -> p i", p=128),
                                     allow_slow_non_contiguous=True).then_inc(bqk_in, 16)
                    for k in range(2):
                        sp.dma_start(w_qk[:, k], sources[k][:, :, 0:128]).then_inc(w_qk_in, 16)

                @block.tensor
                def _(pe):
                    turn_rows(pe, banks, 0, keep.y, keep.ident)
                    first = C * len(QUADS)
                    pe.wait_ge(v_in, 32)
                    for j in range(first - BANKS, first):
                        banks.wait_emptied(pe, j)
                    for t in range(T):
                        j = first + t
                        banks.wait_free(pe, j)
                        for c in range(C):
                            ins = pe.matmul(banks[j][0:P, :], y_t[:, c, P * t:P * t + P], w_v[:, c],
                                            start=(c == 0), stop=(c == C - 1))
                        banks.filled(ins, j)

                @block.scalar
                def _(act):
                    turned_out(act, banks, 0, y_t)

                @block.vector
                def _(v):
                    v.wait_ge(v_in, 32)
                    for t in range(T):
                        j = C * len(QUADS) + t
                        banks.wait_full(v, j)
                        banks.emptied(v.tensor_tensor(vals[:, t].rearrange("p h d -> p (h d)"), banks[j][0:P, :], bv[:], ALU.add), j)

        with ExitStack() as stage:
            q_t = b.sb(stage, "q_t", [HD, 2, NODES])
            k_t = b.sb(stage, "k_t", [HD, 2, NODES])
            probs = b.sb(stage, "probs", [P, 2, NODES])
            probs_t = b.sb(stage, "probs_t", [P, 2, T, P])
            top = b.sb(stage, "top", [P, 2])
            shift = b.sb(stage, "neg_max", [P, 2])
            bq_now = b.sb(stage, "bq_now", [128, 1])
            bq_ok = b.sem(stage, "bq_ok")
            total = b.sb(stage, "total", [P, 4])
            share = b.sb(stage, "share", [P, 4])
            scores = b.ps(stage, "scores", [128, 3 * 512])
            turned = b.ps(stage, "turned", [128, 3, 512])
            mixed = b.ps(stage, "mixed", [128, 2, 512])
            proj_ok = b.sem(stage, "proj_ok")
            q_ok = b.sem(stage, "q_ok")
            k_ok = b.sem(stage, "k_ok")
            scores_ok = b.sem(stage, "scores_ok")
            max_ok = b.sem(stage, "max_ok")
            shift_ok = b.sem(stage, "shift_ok")
            probs_ok = b.sem(stage, "probs_ok")
            turned_ok = b.sem(stage, "turned_ok")
            turned_v = b.sem(stage, "turned_v")
            turned_a = b.sem(stage, "turned_a")
            mixed_ok = b.sem(stage, "mixed_ok")
            share_ok = b.sem(stage, "share_ok")
            out_ok = b.sem(stage, "out_ok")
            with nc.Block() as block:

                @block.sync
                def _(sp):
                    with sp.Fori(1, PAIRS) as i:
                        sp.wait_ge(proj_ok, 6 * i)
                        for k in range(2):
                            sp.dma_start(w_qk[:, k], sources[k][:, :, bass.ds(128 * i, 128)]).then_inc(w_qk_in, 16)

                @block.tensor
                def _(pe):
                    pe.sem_inc(turned_ok, 3)
                    pe.sem_inc(mixed_ok, 1)
                    with pe.Fori(0, PAIRS) as i:
                        pe.wait_ge(w_qk_in, 32 * i + 32)
                        pe.wait_ge(probs_ok, U * i)
                        pe.wait_ge(turned_v, U * i)
                        pe.wait_ge(turned_a, 2 * U * i)
                        for k, to in enumerate((scores, turned[:].rearrange("p a n -> p (a n)"))):
                            for c0, w in COLS:
                                for c in range(C):
                                    ins = pe.matmul(to[:, c0:c0 + w], w_qk[:, k, c], y_t[:, c, c0:c0 + w],
                                                    start=(c == 0), stop=(c == C - 1))
                                ins.then_inc(proj_ok, 1)
                        pe.wait_ge(q_ok, 6 * i + 6)
                        pe.wait_ge(k_ok, 6 * i + 6)
                        for j in range(U + 2):
                            n = U * i + j
                            if j < U:
                                pe.wait_ge(probs_ok, n)
                                h, t = divmod(j, T)
                                for c0, w in COLS:
                                    ins = pe.matmul(scores[0:P, c0:c0 + w], q_t[:, h, P * t:P * t + P], k_t[:, h, c0:c0 + w],
                                                    start=True, stop=True)
                                ins.then_inc(scores_ok, 1)
                            if 1 <= j <= U:
                                pe.wait_ge(probs_ok, n)
                                pe.wait_ge(turned_v, n - 1)
                                pe.wait_ge(turned_a, 2 * n - 2)
                                for q, (s0, m) in enumerate(QUADS):
                                    for s in range(m):
                                        ins = pe.transpose(turned[0:P, q, P * s:P * s + P],
                                                           probs[:, (j - 1) % 2, P * (s0 + s):P * (s0 + s) + P],
                                                           keep.ident[0:P, 0:P])
                                    ins.then_inc(turned_ok, 1)
                            if j >= 2:
                                pe.wait_ge(turned_v, n - 1)
                                pe.wait_ge(turned_a, 2 * n - 2)
                                pe.wait_ge(out_ok, n - 2)
                                h = (j - 2) // T
                                for s in range(T):
                                    ins = pe.matmul(mixed[0:P, j % 2, 0:HD], probs_t[:, j % 2, s],
                                                    vals[:, s, bass.ds(2 * i + h, 1), :].rearrange("p a d -> p (a d)"),
                                                    start=(s == 0), stop=(s == T - 1))
                                ins.then_inc(mixed_ok, 1)

                @block.scalar
                def _(act):
                    with act.Fori(0, PAIRS) as i:
                        act.wait_ge(bq_ok, i + 1)
                        for x, (c0, w) in enumerate(COLS):
                            act.wait_ge(proj_ok, 6 * i + x + 1)
                            for h in range(2):
                                rows = slice(HD * h, HD * h + HD)
                                act.activation(q_t[:, h, c0:c0 + w], scores[rows, c0:c0 + w], ACT.Identity,
                                               bias=bq_now[rows, :]).then_inc(q_ok, 1)
                        for j in range(U + 1):
                            n = U * i + j
                            if j < U:
                                act.wait_ge(shift_ok, n + 1)
                                act.wait_ge(turned_ok, 3 * n)
                                act.activation(probs[:, j % 2], scores[0:P, 0:NODES], ACT.Exp, bias=shift[:, j % 2:j % 2 + 1],
                                               scale=HD ** -0.5, accum_out=total[:, j % 4:j % 4 + 1]).then_inc(probs_ok, 1)
                            if j >= 1:
                                act.wait_ge(mixed_ok, n - 1)
                                for q in (1, 2):
                                    s0, m = QUADS[q]
                                    act.wait_ge(turned_ok, 3 * n + q + 1)
                                    act.activation(probs_t[:, (j - 1) % 2, s0:s0 + m],
                                                   turned[0:P, q, 0:P * m].rearrange("p (s d) -> p s d", s=m),
                                                   ACT.Copy).then_inc(turned_a, 1)

                @block.vector
                def _(v):
                    v.sem_inc(out_ok, 1)
                    v.wait_ge(bqk_in, 32)
                    with v.Fori(0, PAIRS) as i:
                        v.wait_ge(q_ok, 6 * i)
                        v.tensor_scalar(bq_now[:], bq[:, 0, bass.ds(i, 1)], 1.0, None, ALU.mult).then_inc(bq_ok, 1)
                        for x, (c0, w) in enumerate(COLS):
                            v.wait_ge(proj_ok, 6 * i + 3 + x + 1)
                            for h in range(2):
                                rows = slice(HD * h, HD * h + HD)
                                v.tensor_scalar(k_t[:, h, c0:c0 + w], turned[:].rearrange("p a n -> p (a n)")[rows, c0:c0 + w],
                                                bq[rows, 1, bass.ds(i, 1)], None, ALU.add).then_inc(k_ok, 1)
                        for j in range(U + 2):
                            n = U * i + j
                            if j < U:
                                v.wait_ge(scores_ok, n + 1)
                                v.tensor_reduce(top[:, j % 2:j % 2 + 1], scores[0:P, 0:NODES], AX.X, ALU.max).then_inc(max_ok, 1)
                                v.wait_ge(max_ok, n + 1)
                                v.wait_ge(probs_ok, n)
                                v.tensor_scalar(shift[:, j % 2:j % 2 + 1], top[:, j % 2:j % 2 + 1], -HD ** -0.5, None,
                                                ALU.mult).then_inc(shift_ok, 1)
                            if 1 <= j <= U:
                                v.wait_ge(mixed_ok, n - 1)
                                s0, m = QUADS[0]
                                v.wait_ge(turned_ok, 3 * n + 1)
                                v.tensor_copy(probs_t[:, (j - 1) % 2, s0:s0 + m],
                                              turned[0:P, 0, 0:P * m].rearrange("p (s d) -> p s d", s=m)).then_inc(turned_v, 1)
                            if j >= 2:
                                h, t = divmod(j - 2, T)
                                k = (j - 2) % 4
                                v.reciprocal(share[:, k:k + 1], total[:, k:k + 1]).then_inc(share_ok, 1)
                                v.wait_ge(share_ok, n - 1)
                                v.wait_ge(mixed_ok, n)
                                v.tensor_scalar(keep.o[:, t, bass.ds(HD * (2 * i + h), HD)], mixed[0:P, j % 2, 0:HD],
                                                share[:, k:k + 1], None, ALU.mult).then_inc(out_ok, 1)


def routing(b, keep):
    nc, a = b.nc, b.a
    with ExitStack() as ctx:
        o_t = b.sb(ctx, "o_t", [128, C, NODES])
        t_t = b.sb(ctx, "t_t", [128, C, NODES])
        w_o = b.sb(ctx, "w_o", [128, C, D])
        rows = b.sb(ctx, "route_rows", [P, 3, D])
        gate_w = b.sb(ctx, "gate_w", [128, C, EXPERTS])
        gate_b = b.sb(ctx, "gate_b", [P, EXPERTS])
        earlier = b.sb(ctx, "earlier", [P, P])
        expert_no = b.sb(ctx, "expert_no", [P, EXPERTS])
        slot_no = b.sb(ctx, "slot_no", [1, SLOTS + 1])
        J = -(-NODES // SLOT)
        slot_steps = b.sb(ctx, "slot_steps", [128, J])
        stats = b.sb(ctx, "route_stats", [P, T, 6])
        mv = b.sb(ctx, "route_mv", [P, T, 2])
        var = b.sb(ctx, "route_var", [P, T])
        rstd = b.sb(ctx, "route_rstd", [P, T])
        logits = b.sb(ctx, "logits", [P, T, EXPERTS])
        best = b.sb(ctx, "best", [P, T])
        exps = b.sb(ctx, "exps", [P, T, EXPERTS])
        chosen = b.sb(ctx, "chosen", [P, T, EXPERTS])
        before = b.sb(ctx, "before", [P, T + 1, EXPERTS])
        place = b.sb(ctx, "place_f", [P, T])
        placed = b.sb(ctx, "placed", [P, T, EXPERTS])
        counts = b.sb(ctx, "expert_counts", [128, EXPERTS])
        over = b.sb(ctx, "over", [128, EXPERTS, J])
        n_slots = b.sb(ctx, "n_slots", [128, EXPERTS])
        ends = b.sb(ctx, "slot_ends", [128, EXPERTS])
        base = b.sb(ctx, "slot_base", [128, EXPERTS])
        passed = b.sb(ctx, "passed", [1, SLOTS + 1, EXPERTS])
        tables = b.sb(ctx, "slot_tables", [1, 4, SLOTS + 1])
        banks = Banks(b, ctx, "route_banks")
        w_in = b.sem(ctx, "route_w_in")
        const_ok = b.sem(ctx, "route_const_ok")
        o_t_ok = b.sem(ctx, "o_t_ok")
        var_ok = b.sem(ctx, "route_var_ok")
        rstd_ok = b.sem(ctx, "route_rstd_ok")
        t_ok = b.sem(ctx, "t_ok")
        shifted_ok = b.sem(ctx, "shifted_ok")
        exps_ok = b.sem(ctx, "exps_ok")
        chosen_ok = b.sem(ctx, "chosen_ok")
        place_ok = b.sem(ctx, "place_ok")
        sent = b.sem(ctx, "tokens_sent")
        step = b.sem(ctx, "route_step")
        N = C * len(QUADS)
        PROJ, TURN, GATE, RANK = N, N + T, 2 * N + T, 2 * N + T + 1
        with nc.Block() as block:

            @block.sync
            def _(sp):
                sp.dma_start(w_o[:], a["L0_ffn_Wo"].rearrange("(c p) n -> p c n", p=128)).then_inc(w_in, 16)
                for k, n in enumerate(("bo", "ln1_g", "ln1_b")):
                    sp.dma_start(rows[:, k], a["L0_ffn_" + n].unsqueeze(0).to_broadcast([P, D])).then_inc(w_in, 16)
                sp.dma_start(gate_w[:], a["L0_ffn_gate_W"].rearrange("(c p) n -> p c n", p=128)).then_inc(w_in, 16)
                sp.dma_start(gate_b[:], a["L0_ffn_gate_b"].unsqueeze(0).to_broadcast([P, EXPERTS])).then_inc(w_in, 16)

            @block.gpsimd
            def _(pool):
                iota = dict(base=0, channel_multiplier=0, allow_small_or_imprecise_dtypes=True)
                pool.iota(expert_no[:], [[1, EXPERTS]], **iota).then_inc(const_ok, 1)
                pool.iota(slot_no[:], [[1, SLOTS + 1]], **iota).then_inc(const_ok, 1)
                pool.iota(slot_steps[:], [[SLOT, J]], **iota).then_inc(const_ok, 1)
                pool.memset(earlier[:], 1.0).then_inc(const_ok, 1)
                pool.wait_ge(const_ok, 4)
                pool.affine_select(out=earlier[:], in_=earlier[:], compare_op=ALU.is_gt, fill=0.0, base=0,
                                   pattern=[[1, P]], channel_multiplier=-1).then_inc(const_ok, 1)
                for t in range(T):
                    pool.wait_ge(var_ok, t + 1)
                    variance_root(pool, rstd[:, t:t + 1], var[:, t:t + 1], keep.minus_half[0:P, 0:1]).then_inc(rstd_ok, 1)
                pool.wait_ge(place_ok, 1)
                for t in range(T):
                    pool.indirect_dma_start(out=keep.slots_in, out_offset=bass.IndirectOffsetOnAxis(ap=keep.place[:, t:t + 1], axis=0),
                                            in_=keep.y[:, t], in_offset=None).then_inc(sent, 16)
                pool.wait_ge(sent, 16 * T)

            @block.tensor
            def _(pe):
                turn_rows(pe, banks, 0, keep.o, keep.ident)
                pe.wait_ge(w_in, 96)
                pe.wait_ge(o_t_ok, 1)
                for t in range(T):
                    j = PROJ + t
                    banks.wait_free(pe, j)
                    for c in range(C):
                        ins = pe.matmul(banks[j][0:P, :], o_t[:, c, P * t:P * t + P], w_o[:, c], start=(c == 0), stop=(c == C - 1))
                    banks.filled(ins, j)
                pe.wait_ge(t_ok, T)
                turn_rows(pe, banks, TURN, keep.y, keep.ident)
                pe.wait_ge(o_t_ok, 2)
                banks.wait_free(pe, GATE)
                for t in range(T):
                    for c in range(C):
                        ins = pe.matmul(banks[GATE][0:P, EXPERTS * t:EXPERTS * t + EXPERTS], t_t[:, c, P * t:P * t + P],
                                        gate_w[:, c], start=(c == 0), stop=(c == C - 1))
                banks.filled(ins, GATE)
                pe.wait_ge(chosen_ok, 1)
                pe.wait_ge(const_ok, 5)
                banks.wait_free(pe, RANK)
                flat = "p t e -> p (t e)"
                pe.matmul(banks[RANK][0:P, 0:T * EXPERTS], earlier[:], chosen[:].rearrange(flat), start=True, stop=False)
                ins = pe.matmul(banks[RANK][0:P, 0:T * EXPERTS], keep.ones[0:P, 0:P], before[:, 0:T].rearrange(flat),
                                start=False, stop=True)
                banks.filled(ins, RANK)
                banks.wait_free(pe, RANK + 1)
                ins = pe.matmul(banks[RANK + 1][:, 0:EXPERTS], keep.ones[0:P, :], before[:, T], start=True, stop=True)
                banks.filled(ins, RANK + 1)

            @block.scalar
            def _(act):
                turned_out(act, banks, 0, o_t)
                for j in range(N - BANKS, N):
                    banks.wait_emptied(act, j)
                act.sem_inc(o_t_ok, 1)
                turned_out(act, banks, TURN, t_t)
                for j in range(TURN + N - BANKS, TURN + N):
                    banks.wait_emptied(act, j)
                act.sem_inc(o_t_ok, 1)
                act.wait_ge(shifted_ok, 1)
                act.activation(exps[:], exps[:], ACT.Exp).then_inc(exps_ok, 1)

            @block.vector
            def _(v):
                link = Steps(v, step)
                v.wait_ge(w_in, 96)
                for t in range(T):
                    y = keep.y[:, t]
                    j = PROJ + t
                    banks.wait_full(v, j)
                    link(v.tensor_tensor(y, banks[j][0:P, :], y, ALU.add))
                    banks.release(v, j)
                    link(v.tensor_tensor(y, y, rows[:, 0], ALU.add))
                    link(v.bn_stats(stats[:, t], y))
                    link(v.bn_aggr(mv[:, t], stats[:, t]))
                    v.tensor_scalar(var[:, t:t + 1], mv[:, t, 1:2], EPS, None, ALU.add).then_inc(var_ok, 1)
                    v.wait_ge(rstd_ok, t + 1)
                    link(v.tensor_scalar(y, y, mv[:, t, 0:1], rstd[:, t:t + 1], ALU.subtract, ALU.mult))
                    link(v.tensor_tensor(y, y, rows[:, 1], ALU.mult))
                    v.tensor_tensor(y, y, rows[:, 2], ALU.add).then_inc(t_ok, 1)
                wide = [P, T, EXPERTS]
                banks.wait_full(v, GATE)
                link(v.tensor_tensor(logits[:], banks[GATE][0:P, 0:T * EXPERTS].rearrange("p (t e) -> p t e", t=T),
                                     gate_b[:].unsqueeze(1).to_broadcast(wide), ALU.add))
                banks.release(v, GATE)
                link(v.tensor_reduce(best[:], logits[:], AX.X, ALU.max))
                v.tensor_tensor(exps[:], logits[:], best[:].unsqueeze(2).to_broadcast(wide), ALU.subtract).then_inc(shifted_ok, 1)
                link(v.tensor_tensor(chosen[:], logits[:], best[:].unsqueeze(2).to_broadcast(wide), ALU.is_equal))
                v.wait_ge(const_ok, 5)
                link(v.scalar_tensor_tensor(chosen[:], chosen[:], -float(EXPERTS), expert_no[:].unsqueeze(1).to_broadcast(wide),
                                            ALU.mult, ALU.add))
                link(v.tensor_reduce(best[:], chosen[:], AX.X, ALU.min))
                link(v.tensor_scalar(best[:], best[:], float(EXPERTS), None, ALU.add))
                link(v.tensor_tensor(chosen[:], expert_no[:].unsqueeze(1).to_broadcast(wide),
                                     best[:].unsqueeze(2).to_broadcast(wide), ALU.is_equal))
                link(v.memset(before[:, 0], 0.0))
                for t in range(T - 1):
                    link(v.tensor_tensor(before[:, t + 1], before[:, t], chosen[:, t], ALU.add))
                v.tensor_tensor(before[:, T], before[:, T - 1], chosen[:, T - 1], ALU.add).then_inc(chosen_ok, 1)
                v.wait_ge(exps_ok, 1)
                link(v.tensor_reduce(keep.gate[:], exps[:], AX.X, ALU.add))
                link(v.reciprocal(keep.gate[:], keep.gate[:]))
                banks.wait_full(v, RANK + 1)
                link(v.tensor_copy(counts[:], banks[RANK + 1][:, 0:EXPERTS]))
                link(v.tensor_tensor(over[:], counts[:].unsqueeze(2).to_broadcast([128, EXPERTS, J]),
                                     slot_steps[:].unsqueeze(1).to_broadcast([128, EXPERTS, J]), ALU.is_gt))
                link(v.tensor_reduce(n_slots[:], over[:], AX.X, ALU.add))
                link(v.tensor_tensor_scan(ends[:], keep.ones[:, 0:EXPERTS], n_slots[:], 0.0, ALU.mult, ALU.add))
                link(v.tensor_tensor(base[:], ends[:], n_slots[:], ALU.subtract))
                link(v.tensor_scalar(base[:], base[:], float(SLOT), None, ALU.mult))
                link(v.tensor_tensor(placed[:], banks[RANK][0:P, 0:T * EXPERTS].rearrange("p (t e) -> p t e", t=T),
                                     base[0:P].unsqueeze(1).to_broadcast(wide), ALU.add))
                link(v.tensor_tensor(placed[:], placed[:], chosen[:], ALU.mult))
                link(v.tensor_reduce(place[:], placed[:], AX.X, ALU.add))
                v.tensor_copy(keep.place[:], place[:]).then_inc(place_ok, 1)
                link(v.tensor_tensor(passed[:], slot_no[:].unsqueeze(2).to_broadcast([1, SLOTS + 1, EXPERTS]),
                                     ends[0:1].unsqueeze(1).to_broadcast([1, SLOTS + 1, EXPERTS]), ALU.is_ge))
                evens = passed[:, :, 1:7:2]
                odds = passed[:, :, 0:7:2]
                link(v.tensor_reduce(tables[:, 0], evens, AX.X, ALU.add))
                link(v.tensor_reduce(tables[:, 1], odds, AX.X, ALU.add))
                link(v.tensor_scalar(tables[:, 0], tables[:, 0], 1.0, None, ALU.add))
                link(v.tensor_tensor(tables[:, 2], tables[:, 1], tables[:, 0], ALU.subtract))
                link(v.tensor_scalar(tables[:, 2], tables[:, 2], 1.0, None, ALU.add))
                link(v.tensor_reduce(tables[:, 3], passed[:, :, 0:EXPERTS - 1], AX.X, ALU.add))
                link(v.tensor_copy(keep.slot_tables[:], tables[:]))
                link(v.tensor_copy(keep.slot_ends[:], ends[0:1]))


def experts(b, keep):
    nc, a = b.nc, b.a
    FB = FF // 128
    with ExitStack() as ctx:
        w1 = b.sb(ctx, "w1", [128, 2, C, FF])
        w2 = b.sb(ctx, "w2", [128, 2, FB, D])
        b2 = b.sb(ctx, "b2", [128, 2, D])
        b1_rows = b.sb(ctx, "b1_rows", [EXPERTS * FB, 128])
        b1 = b.sb(ctx, "b1", [128, EXPERTS, FB])
        b1_turned = b.sem(ctx, "b1_turned")
        b1_ok = b.sem(ctx, "b1_ok")
        b1_now = b.sb(ctx, "b1_now", [128, FB])
        b1_now_ok = b.sem(ctx, "b1_now_ok")
        pool_y = keep.y_all
        hid = pool_y[:, 0:FF]
        rows = pool_y[:, FF:FF + D]
        rows_t = pool_y[:, FF + D:FF + 2 * D].rearrange("p (c n) -> p c n", c=C)
        done = pool_y[:, FF + 2 * D:FF + 3 * D]
        hid_t = b.sb(ctx, "hid_t", [128, FB, SLOT])
        up = b.ps(ctx, "up", [128, 2, 512])
        turned = b.ps(ctx, "hid_turned", [128, 4, 512])
        down = b.ps(ctx, "down", [128, 512])
        x_turned = b.ps(ctx, "x_turned", [128, 512])
        b1_in = b.sem(ctx, "b1_in")
        rows_in = b.sem(ctx, "rows_in")
        w1_in = [b.sem(ctx, f"w1_in{u}") for u in range(2)]
        w2_in = [b.sem(ctx, f"w2_in{u}") for u in range(2)]
        x_turned_ok = b.sem(ctx, "x_turned_ok")
        rows_t_ok = b.sem(ctx, "rows_t_ok")
        up_ok = b.sem(ctx, "up_ok")
        hid_ok = b.sem(ctx, "hid_ok")
        turned_ok = b.sem(ctx, "hid_turned_ok")
        gelu_ok = b.sem(ctx, "gelu_ok")
        down_ok = b.sem(ctx, "down_ok")
        done_ok = b.sem(ctx, "done_ok")
        done_out = b.sem(ctx, "done_out")
        slots_in = keep.slots_in.rearrange("(s p) d -> s p d", p=SLOT)
        slots_out = keep.slots_out.rearrange("(s p) d -> s p d", p=SLOT)

        def table(eng, row, k):
            return eng.value_load(keep.slot_tables[0:1, row, bass.ds(k, 1)], min_val=0, max_val=(4, 4, 1, EXPERTS - 1)[row])

        with nc.Block() as block:

            @block.sync
            def _(sp):
                def load(e, u):
                    sp.dma_start(w1[:, u], a["L0_ffn_W1"][bass.ds(e, 1)].rearrange("a (c p) f -> p (a c) f", p=128)).then_inc(w1_in[u], 16)
                    sp.dma_start(w2[:, u], a["L0_ffn_W2"][bass.ds(e, 1)].rearrange("a (f p) d -> p (a f) d", p=128)).then_inc(w2_in[u], 16)
                    sp.dma_start(b2[:, u], a["L0_ffn_b2"][bass.ds(e, 1)].to_broadcast([128, D])).then_inc(w2_in[u], 16)

                load(0, 0)
                load(1, 1)
                with sp.Fori(1, EXPERTS // 2) as i:
                    for u in range(2):
                        end = sp.value_load(keep.slot_ends[0:1, bass.ds(2 * i + u - 2, 1)], min_val=0, max_val=SLOTS)
                        sp.wait_ge(done_ok, end)
                        load(2 * i + u, u)

            @block.gpsimd
            def _(pool):
                pool.dma_start(b1_rows[:], a["L0_ffn_b1"].rearrange("e (f p) -> (e f) p", p=128)).then_inc(b1_in, 16)
                pool.dma_start(rows, slots_in[0]).then_inc(rows_in, 16)
                def load(k):
                    pool.wait_ge(x_turned_ok, k)
                    pool.dma_start(rows, slots_in[bass.ds(k, 1)].rearrange("a p d -> p (a d)")).then_inc(rows_in, 16)

                def store(k):
                    pool.wait_ge(done_ok, k + 1)
                    pool.dma_start(slots_out[bass.ds(k, 1)].rearrange("a p d -> p (a d)"), done).then_inc(done_out, 16)

                load(1)
                with pool.Fori(2, SLOTS + 1) as k:
                    load(k)
                    store(k - 2)
                store(SLOTS - 1)
                pool.wait_ge(done_out, 16 * SLOTS)

            @block.tensor
            def _(pe):
                def turn_x(k):
                    pe.wait_ge(rows_in, 16 * (k + 1))
                    pe.wait_ge(rows_t_ok, k)
                    for c in range(C):
                        ins = pe.transpose(x_turned[:, SLOT * c:SLOT * c + SLOT], rows[:, 128 * c:128 * c + 128], keep.ident[:])
                    ins.then_inc(x_turned_ok, 1)

                def product_up(k):
                    even, odd, half = (table(pe, r, k) for r in range(3))
                    pe.wait_ge(w1_in[0], 16 * even)
                    pe.wait_ge(w1_in[1], 16 * odd)
                    pe.wait_ge(rows_t_ok, k + 1)
                    w = w1[:, bass.ds(half, 1)].rearrange("p a c f -> p (a c) f")
                    for f in range(4):
                        if f >= 2:
                            pe.wait_ge(hid_ok, 4 * k + f - 1)
                        else:
                            pe.wait_ge(hid_ok, 4 * k)
                        for c in range(C):
                            ins = pe.matmul(up[:, f % 2], rows_t[:, c], w[:, c, 512 * f:512 * f + 512],
                                            start=(c == 0), stop=(c == C - 1))
                        ins.then_inc(up_ok, 1)

                def turn_hid(k):
                    for f in range(4):
                        pe.wait_ge(hid_ok, 4 * k + f + 1)
                        pe.wait_ge(gelu_ok, 4 * k)
                        for n in range(4):
                            ins = pe.transpose(turned[:, f, 128 * n:128 * n + 128],
                                               hid[:, 512 * f + 128 * n:512 * f + 128 * n + 128], keep.ident[:])
                        ins.then_inc(turned_ok, 1)

                def product_down(k):
                    even, odd, half = (table(pe, r, k) for r in range(3))
                    pe.wait_ge(w2_in[0], 32 * even)
                    pe.wait_ge(w2_in[1], 32 * odd)
                    pe.wait_ge(gelu_ok, 4 * k + 4)
                    pe.wait_ge(done_ok, k)
                    pe.wait_ge(b1_ok, 1)
                    w = w2[:, bass.ds(half, 1)].rearrange("p a f d -> p (a f) d")
                    for f in range(FB):
                        ins = pe.matmul(down[:], hid_t[:, f], w[:, f], start=(f == 0), stop=(f == FB - 1))
                    ins.then_inc(down_ok, 1)

                pe.wait_ge(b1_in, 16)
                pe.transpose(down[:, 0:128], b1_rows[:], keep.ident[:]).then_inc(b1_turned, 1)
                turn_x(0)
                product_up(0)
                turn_x(1)
                turn_hid(0)
                with pe.Fori(1, SLOTS) as k:
                    product_up(k)
                    turn_x(k + 1)
                    product_down(k - 1)
                    turn_hid(k)
                product_down(SLOTS - 1)

            @block.scalar
            def _(act):
                with act.Fori(0, SLOTS) as k:
                    act.wait_ge(b1_now_ok, k + 1)
                    for f in range(FB):
                        if f % 4 == 0:
                            act.wait_ge(turned_ok, 4 * k + f // 4 + 1)
                            act.wait_ge(down_ok, k)
                        ins = act.activation(hid_t[:, f], turned[:, f // 4, 128 * (f % 4):128 * (f % 4) + 128],
                                             ACT.Gelu_apprx_tanh,
                                             bias=b1_now[:, f:f + 1])
                        if f % 4 == 3:
                            ins.then_inc(gelu_ok, 1)

            @block.vector
            def _(v):
                def turned_in(k):
                    v.wait_ge(x_turned_ok, k + 1)
                    v.wait_ge(up_ok, 4 * k)
                    v.tensor_copy(rows_t, x_turned[:].rearrange("p (c n) -> p c n", c=C)).then_inc(rows_t_ok, 1)

                def hidden(k):
                    for f in range(4):
                        v.wait_ge(up_ok, 4 * k + f + 1)
                        v.wait_ge(turned_ok, 4 * k)
                        v.tensor_copy(hid[:, 512 * f:512 * f + 512], up[:, f % 2]).then_inc(hid_ok, 1)
                    e = table(v, 3, k)
                    v.wait_ge(gelu_ok, 4 * k)
                    v.tensor_scalar(b1_now[:], b1[:, bass.ds(e, 1)].rearrange("p a f -> p (a f)"), 1.0, None, ALU.mult
                                    ).then_inc(b1_now_ok, 1)

                def finish(k):
                    half = table(v, 2, k)
                    v.wait_ge(down_ok, k + 1)
                    v.wait_ge(done_out, 16 * k)
                    v.tensor_tensor(done, down[:], b2[:, bass.ds(half, 1)].rearrange("p a d -> p (a d)"), ALU.add
                                    ).then_inc(done_ok, 1)

                v.wait_ge(b1_turned, 1)
                v.tensor_copy(b1[:].rearrange("p e f -> p (e f)"), down[:, 0:128]).then_inc(b1_ok, 1)
                turned_in(0)
                v.wait_ge(b1_ok, 1)
                hidden(0)
                turned_in(1)
                with v.Fori(1, SLOTS) as k:
                    hidden(k)
                    turned_in(k + 1)
                    finish(k - 1)
                finish(SLOTS - 1)


def gat_inputs(b, keep):
    nc, a = b.nc, b.a
    with ExitStack() as ctx:
        got = b.sb(ctx, "got", [P, T, D])
        y_t = b.sb(ctx, "y2_t", [128, C, NODES])
        w_s = b.sb(ctx, "w_s", [128, C, HEADS, HD])
        w_b = b.sb(ctx, "w_b", [P, HEADS, HD])
        a_w = b.sb(ctx, "a_w", [P, HEADS, 2, HD])
        a_b = b.sb(ctx, "a_b", [P, HEADS])
        prod = b.sb(ctx, "prod", [P, HEADS, HD])
        stats = b.sb(ctx, "gat_stats", [P, T, 6])
        mv = b.sb(ctx, "gat_mv", [P, T, 2])
        var = b.sb(ctx, "gat_var", [P, T])
        rstd = b.sb(ctx, "gat_rstd", [P, T])
        halves_t = b.sb(ctx, "halves_t", [2 * HEADS, NODES])
        banks = Banks(b, ctx, "gat_banks")
        w_in = b.sem(ctx, "gat_w_in")
        got_in = b.sem(ctx, "got_in")
        var_ok = b.sem(ctx, "gat_var_ok")
        rstd_ok = b.sem(ctx, "gat_rstd_ok")
        y2_ok = b.sem(ctx, "y2_ok")
        y2_t_ok = b.sem(ctx, "y2_t_ok")
        halves_ok = b.sem(ctx, "halves_ok")
        halves_t_ok = b.sem(ctx, "halves_t_ok")
        halves_out = b.sem(ctx, "halves_out")
        step = b.sem(ctx, "gat_step")
        N = C * len(QUADS)
        with nc.Block() as block:

            @block.sync
            def _(sp):
                sp.dma_start(keep.worth[:], keep.worth_rows.rearrange("(t p) n -> p t n", p=P)).then_inc(keep.worth_in, 16)
                for c in range(C):
                    sp.dma_start(w_s[:, c], a["L1_gnn_Ws"][:, 128 * c:128 * c + 128, :].rearrange("h p e -> p h e")).then_inc(w_in, 16)
                sp.dma_start(w_b[:].rearrange("p h e -> p (h e)"),
                             a["L1_gnn_Wb"].rearrange("(a h) e -> a (h e)", a=1).to_broadcast([P, D])).then_inc(w_in, 16)
                sp.dma_start(a_w[:].rearrange("p h k e -> p (h k e)"),
                             a["L1_gnn_a_w"].rearrange("(a h) e -> a (h e)", a=1).to_broadcast([P, 2 * D])).then_inc(w_in, 16)
                sp.dma_start(a_b[:], a["L1_gnn_a_b"].unsqueeze(0).to_broadcast([P, HEADS])).then_inc(w_in, 16)
                sp.wait_ge(halves_t_ok, len(QUADS))
                sp.dma_start(keep.halves, halves_t[:]).then_inc(halves_out, 16)
                sp.wait_ge(halves_out, 16)

            @block.gpsimd
            def _(pool):
                for t in range(T):
                    pool.indirect_dma_start(out=got[:, t], out_offset=None, in_=keep.slots_out,
                                            in_offset=bass.IndirectOffsetOnAxis(ap=keep.place[:, t:t + 1], axis=0)).then_inc(got_in, 16)
                for t in range(T):
                    pool.wait_ge(var_ok, t + 1)
                    variance_root(pool, rstd[:, t:t + 1], var[:, t:t + 1], keep.minus_half[0:P, 0:1]).then_inc(rstd_ok, 1)

            @block.tensor
            def _(pe):
                pe.wait_ge(y2_ok, T)
                turn_rows(pe, banks, 0, keep.y, keep.ident)
                pe.wait_ge(w_in, 16 * (C + 3))
                pe.wait_ge(y2_t_ok, 1)
                for t in range(T):
                    banks.wait_free(pe, N + t)
                    for c in range(C):
                        ins = pe.matmul(banks[N + t][0:P, :], y_t[:, c, P * t:P * t + P], w_s[:, c].rearrange("p h e -> p (h e)"),
                                        start=(c == 0), stop=(c == C - 1))
                    banks.filled(ins, N + t)
                for q, (t0, n) in enumerate(QUADS):
                    pe.wait_ge(halves_ok, t0 + n)
                    banks.wait_free(pe, N + T + q)
                    for t in range(n):
                        ins = pe.transpose(banks[N + T + q][0:2 * HEADS, P * t:P * t + P], keep.halves_p[:, t0 + t], keep.ident[0:P, 0:P])
                    banks.filled(ins, N + T + q)

            @block.scalar
            def _(act):
                turned_out(act, banks, 0, y_t)
                for j in range(N - BANKS, N):
                    banks.wait_emptied(act, j)
                act.sem_inc(y2_t_ok, 1)
                for q, (t0, n) in enumerate(QUADS):
                    banks.wait_full(act, N + T + q)
                    act.activation(halves_t[:, P * t0:P * (t0 + n)], banks[N + T + q][0:2 * HEADS, 0:P * n], ACT.Copy).then_inc(halves_t_ok, 1)

            @block.vector
            def _(v):
                link = Steps(v, step)
                v.wait_ge(got_in, 16 * T)
                for t in range(T):
                    r = keep.res[:, t]
                    link(v.scalar_tensor_tensor(r, got[:, t], keep.gate[:, t:t + 1], r, ALU.mult, ALU.add))
                    link(v.bn_stats(stats[:, t], r))
                    link(v.bn_aggr(mv[:, t], stats[:, t]))
                    v.tensor_scalar(var[:, t:t + 1], mv[:, t, 1:2], EPS, None, ALU.add).then_inc(var_ok, 1)
                    v.wait_ge(rstd_ok, t + 1)
                    v.tensor_scalar(keep.y[:, t], r, mv[:, t, 0:1], rstd[:, t:t + 1], ALU.subtract, ALU.mult).then_inc(y2_ok, 1)
                link(v.memset(keep.w[:, :, :, HD:HD + 1], 1.0))
                v.wait_ge(w_in, 16 * (C + 3))
                for t in range(T):
                    w = keep.w[:, t, :, 0:HD]
                    banks.wait_full(v, N + t)
                    link(v.tensor_tensor(w, banks[N + t][0:P, :].rearrange("p (h e) -> p h e", h=HEADS), w_b[:], ALU.add))
                    banks.release(v, N + t)
                    for k in range(2):
                        link(v.tensor_tensor(prod[:], w, a_w[:, :, k], ALU.mult))
                        link(v.tensor_reduce(keep.halves_p[:, t, HEADS * k:HEADS * k + HEADS], prod[:], AX.X, ALU.add))
                    v.tensor_tensor(keep.halves_p[:, t, 0:HEADS], keep.halves_p[:, t, 0:HEADS], a_b[:], ALU.add).then_inc(halves_ok, 1)


def gat_max(b, keep):
    nc = b.nc
    with ExitStack() as ctx:
        src = b.sb(ctx, "src_halves", [P, HEADS, NODES])
        absent = b.sb(ctx, "absent_tiles", [P, 2, NODES], BF16)
        masked = b.sb(ctx, "masked", [P, 2, NODES])
        top = b.sb(ctx, "gat_top", [P, T, HEADS])
        low = b.sb(ctx, "gat_low", [P, T, HEADS])
        shifts = b.sb(ctx, "shifts", [P, T, 2, HEADS])
        shifts_t = b.sb(ctx, "shifts_t", [2 * HEADS, NODES])
        banks = Banks(b, ctx, "max_banks", 3)
        src_in = [b.sem(ctx, f"src_in{h}") for h in range(HEADS)]
        absent_in = [b.sem(ctx, f"absent_in{u}") for u in range(2)]
        top_ok = b.sem(ctx, "top_ok")
        shifts_ok = b.sem(ctx, "shifts_ok")
        shifts_t_ok = b.sem(ctx, "shifts_t_ok")
        shifts_out = b.sem(ctx, "shifts_out")
        step = b.sem(ctx, "max_step")
        with nc.Block() as block:

            @block.sync
            def _(sp):
                sp.dma_start(absent[:, 0], keep.absent[0:P, :]).then_inc(absent_in[0], 16)
                for h in range(HEADS):
                    sp.dma_start(src[:, h], keep.halves[HEADS + h:HEADS + h + 1, :].to_broadcast([P, NODES])).then_inc(src_in[h], 16)
                for t in range(1, T):
                    if t >= 2:
                        sp.wait_ge(top_ok, HEADS * (t - 1))
                    sp.dma_start(absent[:, t % 2], keep.absent[P * t:P * t + P, :]).then_inc(absent_in[t % 2], 16)
                sp.wait_ge(shifts_t_ok, len(QUADS))
                sp.dma_start(keep.shifts, shifts_t[:]).then_inc(shifts_out, 16)
                sp.wait_ge(shifts_out, 16)
                sp.wait_ge(keep.worth_in, 16)

            @block.tensor
            def _(pe):
                pe.wait_ge(shifts_ok, 1)
                for q, (t0, n) in enumerate(QUADS):
                    for t in range(n):
                        ins = pe.transpose(banks[q][0:2 * HEADS, P * t:P * t + P],
                                           shifts[:, t0 + t].rearrange("p k h -> p (k h)"), keep.ident[0:P, 0:P])
                    banks.filled(ins, q)

            @block.scalar
            def _(act):
                for q, (t0, n) in enumerate(QUADS):
                    banks.wait_full(act, q)
                    act.activation(shifts_t[:, P * t0:P * (t0 + n)], banks[q][0:2 * HEADS, 0:P * n], ACT.Copy).then_inc(shifts_t_ok, 1)

            @block.vector
            def _(v):
                link = Steps(v, step)
                for t in range(T):
                    v.wait_ge(absent_in[t % 2], 16 * (t // 2 + 1))
                    for h in range(HEADS):
                        if t == 0:
                            v.wait_ge(src_in[h], 16)
                        if HEADS * t + h >= 2:
                            v.wait_ge(top_ok, HEADS * t + h - 1)
                        v.tensor_tensor_reduce(out=masked[:, h % 2], in0=absent[:, t % 2], in1=src[:, h], scale=1.0, scalar=LOWEST,
                                               op0=ALU.add, op1=ALU.max, accum_out=top[:, t, h:h + 1]).then_inc(top_ok, 1)
                v.wait_ge(top_ok, T * HEADS)
                own = keep.halves_p[:, :, 0:HEADS]
                link(v.tensor_tensor(top[:], top[:], own, ALU.add))
                link(v.scalar_tensor_tensor(top[:], top[:], SLOPE, top[:], ALU.mult, ALU.max))
                link(v.tensor_tensor(shifts[:, :, 0], top[:], own, ALU.subtract))
                link(v.scalar_tensor_tensor(shifts[:, :, 1], own, -SLOPE, top[:], ALU.mult, ALU.add))
                v.tensor_scalar(keep.minus_src[:, :, 0], keep.halves_p[:, :, HEADS:2 * HEADS], -1.0, None, ALU.mult)
                v.tensor_scalar(keep.minus_src[:, :, 1], keep.halves_p[:, :, HEADS:2 * HEADS], -SLOPE, None, ALU.mult)
                v.sem_inc(shifts_ok, 1)


def gat(b, keep):
    nc = b.nc
    HALF = T // 2
    WIDE = HD + 1
    with ExitStack() as ctx:
        rows = b.sb(ctx, "shift_rows", [P, 2, 2, NODES])
        far = b.sb(ctx, "far", [P, 3, NODES])
        weight = b.sb(ctx, "weight", [P, 2, NODES])
        share = b.sb(ctx, "gat_share", [P, T])
        mean = b.sb(ctx, "gat_mean", [P, T, HD])
        minus_now = b.sb(ctx, "minus_now", [P, T, 2, 2])
        minus_ok = b.sem(ctx, "minus_ok")
        sums = b.ps(ctx, "gat_sums", [128, 2, 2, 512])
        rows_in = [b.sem(ctx, f"shift_rows_in{u}") for u in range(2)]
        far_ok = b.sem(ctx, "far_ok")
        near_ok = b.sem(ctx, "near_ok2")
        worthy_ok = b.sem(ctx, "worthy_ok")
        weight_ok = b.sem(ctx, "weight_ok")
        summed = b.sem(ctx, "gat_summed")
        head_ok = b.sem(ctx, "head_ok")
        step = b.sem(ctx, "gat_v_step")
        U = 2 * T

        def n3(j):
            return j % 3

        with nc.Block() as block:

            @block.sync
            def _(sp):
                def load(h, u):
                    for k in range(2):
                        sp.dma_start(rows[:, u, k], keep.shifts[bass.ds(HEADS * k + h, 1), :].to_broadcast([P, NODES])).then_inc(rows_in[u], 16)

                load(0, 0)
                load(1, 1)
                with sp.Fori(1, HEADS // 2) as i:
                    for u in range(2):
                        sp.wait_ge(near_ok, U * i + T * (u - 1))
                        load(2 * i + u, u)

            @block.scalar
            def _(act):
                act.sem_inc(weight_ok, 2)
                with act.Fori(0, HEADS // 2) as i:
                    act.wait_ge(minus_ok, i + 1)
                    for j in range(U + 2):
                        n = U * i + j
                        if j < U:
                            u, s = divmod(j, T)
                            if s == 0:
                                act.wait_ge(rows_in[u], 32 * i + 32)
                            act.wait_ge(weight_ok, n)
                            act.activation(far[:, n3(j)], rows[:, u, 1], ACT.Identity, bias=minus_now[:, s, 1, u:u + 1]).then_inc(far_ok, 1)
                        if j >= 2:
                            act.wait_ge(worthy_ok, n - 1)
                            act.wait_ge(summed, n - 1)
                            act.activation(weight[:, j % 2], far[:, n3(j - 2)], ACT.Exp, scale=-1.0).then_inc(weight_ok, 1)

            @block.tensor
            def _(pe):
                pe.sem_inc(summed, 2)
                with pe.Fori(0, HEADS // 2) as i:
                    for j in range(U):
                        u, s = divmod(j, T)
                        n = U * i + j
                        if s == 0:
                            pe.wait_ge(head_ok, 2 * i + u)
                        pe.wait_ge(weight_ok, n + 3)
                        for t in range(T):
                            ins = pe.matmul(sums[0:P, u, t // HALF, WIDE * (t % HALF):WIDE * (t % HALF) + WIDE],
                                            weight[:, j % 2, P * t:P * t + P],
                                            keep.w[:, s, bass.ds(2 * i + u, 1), :].rearrange("p a e -> p (a e)"),
                                            start=(s == 0 and t % HALF == 0), stop=(s == T - 1), skip_group_check=True)
                        ins.then_inc(summed, 1)

            @block.vector
            def _(v):
                v.sem_inc(head_ok, 1)
                with v.Fori(0, HEADS // 2) as i:
                    link = Steps(v, step, base=12 * i)
                    v.wait_ge(far_ok, U * i)
                    v.wait_ge(near_ok, U * i)
                    v.tensor_scalar(minus_now[:], keep.minus_src[:, :, :, bass.ds(2 * i, 2)], 1.0, None, ALU.mult
                                    ).then_inc(minus_ok, 1)

                    def finish(u):
                        h = 2 * i + u
                        v.wait_ge(summed, 2 + T * h + T)
                        for k in range(2):
                            part = sums[0:P, u, k, 0:WIDE * HALF].rearrange("p (t e) -> p t e", t=HALF)
                            link(v.tensor_scalar(share[:, HALF * k:HALF * k + HALF], part[:, :, HD], 1e-30, None, ALU.max))
                        link(v.reciprocal(share[:], share[:]))
                        for k in range(2):
                            part = sums[0:P, u, k, 0:WIDE * HALF].rearrange("p (t e) -> p t e", t=HALF)
                            link(v.tensor_tensor(mean[:, HALF * k:HALF * k + HALF], part[:, :, 0:HD],
                                                 share[:, HALF * k:HALF * k + HALF].unsqueeze(2).to_broadcast([P, HALF, HD]), ALU.mult))
                        to = keep.res[:, :, bass.ds(HD * h, HD)]
                        link(v.tensor_tensor(to, mean[:], to, ALU.add))
                        v.sem_inc(head_ok, 1)

                    for j in range(U + 1):
                        n = U * i + j
                        if j < U:
                            u, s = divmod(j, T)
                            v.wait_ge(far_ok, n + 1)
                            to = far[:, n3(j)]
                            v.scalar_tensor_tensor(to, rows[:, u, 0], minus_now[:, s, 0, u:u + 1], to, ALU.add, ALU.min
                                                   ).then_inc(near_ok, 1)
                        if j >= 1:
                            v.wait_ge(near_ok, n)
                            to = far[:, n3(j - 1)]
                            v.tensor_tensor(to, to, keep.worth[:, (j - 1) % T], ALU.add).then_inc(worthy_ok, 1)
                        if j == T + 4:
                            finish(0)
                    finish(1)
                    assert link.n == 12


def last_mlp(b, keep):
    nc, a = b.nc, b.a
    G = 160
    HI = G - 128
    L = 7
    MARKS, OUT0, OP = 64, 128, 29
    COLS2 = 2 * NODES
    W5 = 500
    K = COLS2 // W5
    ROUND = 1.5 * 2 ** 23
    with ExitStack() as ctx:
        w_rows = b.sb(ctx, "m_rows", [128, L, G])
        w_rows_hi = b.sb(ctx, "m_rows_hi", [HI, L, G])
        w_t = b.sb(ctx, "m_t", [128, L, G])
        w_t_hi = b.sb(ctx, "m_t_hi", [HI, L, G])
        w_first = b.sb(ctx, "m_first", [3, G])
        w_last = b.sb(ctx, "m_last", [128, 2])
        bias = b.sb(ctx, "m_bias", [128, 2, L])
        bias_last = b.sb(ctx, "m_bias_last", [P, 1])
        marks = b.sb(ctx, "marks", [P, T, 4, 16])
        weigh = b.sb(ctx, "weigh", [P, 16])
        sixteen = b.sb(ctx, "sixteen", [P, 16])
        high = b.sb(ctx, "high", [P, T, 4])
        seen = b.sb(ctx, "seen", [P, T, 4])
        feats = b.sb(ctx, "feats", [P, T, 2, 3])
        feats_t = b.sb(ctx, "feats_t", [3, 2, NODES])
        lo = b.sb(ctx, "h_lo", [128, 2, COLS2])
        hi = b.sb(ctx, "h_hi", [HI, 2, COLS2])
        asked = b.sb(ctx, "asked", [P, T, 2])
        mask = b.sb(ctx, "mask", [P, T])
        result = b.sb(ctx, "result", [P, 2, T])
        hot = b.sb(ctx, "hot", [P, T, 2, 16])
        stats = b.sb(ctx, "m_stats", [P, T, 6])
        mv = b.sb(ctx, "m_mv", [P, T, 2])
        var = b.sb(ctx, "m_var", [P, T])
        rstd = b.sb(ctx, "m_rstd", [P, T])
        banks = Banks(b, ctx, "m_banks")
        w_in = b.sem(ctx, "m_w_in")
        const_ok = b.sem(ctx, "m_const_ok")
        var_ok = b.sem(ctx, "m_var_ok")
        rstd_ok = b.sem(ctx, "m_rstd_ok")
        feats_ok = b.sem(ctx, "feats_ok")
        feats_t_ok = b.sem(ctx, "feats_t_ok")
        w_t_ok = b.sem(ctx, "m_t_ok")
        lo_ok = b.sem(ctx, "lo_ok")
        hi_ok = b.sem(ctx, "hi_ok")
        out_ok = b.sem(ctx, "rows_ok")
        out_sent = b.sem(ctx, "out_sent")
        step = b.sem(ctx, "m_step")
        astep = b.sem(ctx, "m_a_step")
        W = L - 2
        F0 = 2 * W
        M0 = F0 + 2 * len(QUADS)
        LAST = M0 + 2 * K * (W + 1)
        with nc.Block() as block:

            @block.sync
            def _(sp):
                slow = dict(allow_slow_non_contiguous=True)
                w = a["L1_ffn_W"]
                sp.dma_start(w_rows[:], w[:, 0:128, :].rearrange("l e d -> e l d")).then_inc(w_in, 16)
                sp.dma_start(w_rows_hi[:], w[:, 128:G, :].rearrange("l e d -> e l d")).then_inc(w_in, 16)
                sp.dma_start(w_first[0:2], w[0, :, 0:2].rearrange("e d -> d e"), **slow).then_inc(w_in, 16)
                sp.dma_start(w_first[2:3], w[0, :, 30:31].rearrange("e d -> d e"), **slow).then_inc(w_in, 16)
                sp.dma_start(w_last[:, 0:1], w[L - 1, 2, 0:128].unsqueeze(1), **slow).then_inc(w_in, 16)
                sp.dma_start(w_last[0:HI, 1:2], w[L - 1, 2, 128:G].unsqueeze(1), **slow).then_inc(w_in, 16)
                bb = a["L1_ffn_b"]
                sp.dma_start(bias[:, 0], bb[:, 0:128].rearrange("l e -> e l"), **slow).then_inc(w_in, 16)
                sp.dma_start(bias[0:HI, 1], bb[:, 128:G].rearrange("l e -> e l"), **slow).then_inc(w_in, 16)
                sp.dma_start(bias_last[:], bb[L - 1:L, 2:3].to_broadcast([P, 1]), **slow).then_inc(w_in, 16)
                for q, (t0, n) in enumerate(QUADS):
                    sp.wait_ge(out_ok, q + 1)
                    sp.dma_start(b.out.rearrange("(t p) d -> p t d", p=P)[:, t0:t0 + n], keep.res[:, t0:t0 + n]).then_inc(out_sent, 16)
                sp.wait_ge(out_sent, 16 * len(QUADS))

            @block.gpsimd
            def _(pool):
                iota = dict(channel_multiplier=0, allow_small_or_imprecise_dtypes=True)
                pool.iota(weigh[:], [[-1, 16]], base=16, **iota).then_inc(const_ok, 1)
                pool.iota(sixteen[:], [[1, 16]], base=0, **iota).then_inc(const_ok, 1)
                pool.wait_ge(var_ok, 1)
                variance_root(pool, rstd[:], var[:], keep.minus_half[0:P, 0:T]).then_inc(rstd_ok, 1)

            @block.tensor
            def _(pe):
                pe.wait_ge(w_in, 16 * 9)
                for l in range(W):
                    banks.wait_free(pe, 2 * l)
                    pe.transpose(banks[2 * l][:, 0:128], w_rows[:, l + 1, 0:128], keep.ident[:])
                    ins = pe.transpose(banks[2 * l][:, 128:G], w_rows_hi[:, l + 1, 0:128], keep.ident[0:HI, 0:HI])
                    banks.filled(ins, 2 * l)
                    banks.wait_free(pe, 2 * l + 1)
                    pe.transpose(banks[2 * l + 1][0:HI, 0:128], w_rows[:, l + 1, 128:G], keep.ident[:])
                    ins = pe.transpose(banks[2 * l + 1][0:HI, 128:G], w_rows_hi[:, l + 1, 128:G], keep.ident[0:HI, 0:HI])
                    banks.filled(ins, 2 * l + 1)
                pe.wait_ge(feats_ok, 1)
                for p in range(2):
                    for q, (t0, n) in enumerate(QUADS):
                        j = F0 + 3 * p + q
                        banks.wait_free(pe, j)
                        for t in range(n):
                            ins = pe.transpose(banks[j][0:3, P * t:P * t + P], feats[:, t0 + t, p], keep.ident[0:P, 0:P])
                        banks.filled(ins, j)
                f = feats_t[:].rearrange("f p n -> f (p n)")
                pe.wait_ge(feats_t_ok, 2 * len(QUADS))
                pe.wait_ge(w_t_ok, 2 * W)
                for l in range(W + 1):
                    for k in range(K):
                        c = slice(W5 * k, W5 * k + W5)
                        if l:
                            pe.wait_ge(lo_ok, K * (l - 1) + k + 1)
                            pe.wait_ge(hi_ok, K * (l - 1) + k + 1)
                        for part, (e0, e1) in enumerate(((0, 128), (128, G))):
                            j = M0 + 2 * (K * l + k) + part
                            banks.wait_free(pe, j)
                            to = banks[j][0:e1 - e0, 0:W5]
                            if l == 0:
                                ins = pe.matmul(to, w_first[:, e0:e1], f[:, c], start=True, stop=True)
                            else:
                                pe.matmul(to, w_t[:, l, e0:e1], lo[:, (l - 1) % 2, c], start=True, stop=False)
                                ins = pe.matmul(to, w_t_hi[:, l, e0:e1], hi[:, (l - 1) % 2, c], start=False, stop=True)
                            banks.filled(ins, j)
                pe.wait_ge(lo_ok, K * (W + 1))
                pe.wait_ge(hi_ok, K * (W + 1))
                banks.wait_free(pe, LAST)
                for p in range(2):
                    for t in range(T):
                        c = slice(NODES * p + P * t, NODES * p + P * t + P)
                        to = banks[LAST][0:P, T * p + t:T * p + t + 1]
                        pe.matmul(to, lo[:, W % 2, c], w_last[:, 0:1], start=True, stop=False)
                        ins = pe.matmul(to, hi[:, W % 2, c], w_last[0:HI, 1:2], start=False, stop=True)
                banks.filled(ins, LAST)

            @block.scalar
            def _(act):
                link = Steps(act, astep)
                for l in range(W):
                    for j, to, rows in ((2 * l, w_t[:, l + 1], 128), (2 * l + 1, w_t_hi[:, l + 1], HI)):
                        banks.wait_full(act, j)
                        act.activation(to, banks[j][0:rows, 0:G], ACT.Copy).then_inc(w_t_ok, 1)
                        act.wait_ge(w_t_ok, j + 1)
                        banks.release(act, j)
                for p in range(2):
                    for q, (t0, n) in enumerate(QUADS):
                        j = F0 + 3 * p + q
                        banks.wait_full(act, j)
                        act.activation(feats_t[:, p, P * t0:P * (t0 + n)], banks[j][0:3, 0:P * n], ACT.Copy).then_inc(feats_t_ok, 1)
                        act.wait_ge(feats_t_ok, 3 * p + q + 1)
                        banks.release(act, j)
                act.wait_ge(w_in, 16 * 9)
                for l in range(W + 1):
                    for k in range(K):
                        j = M0 + 2 * (K * l + k)
                        banks.wait_full(act, j)
                        act.activation(lo[:, l % 2, W5 * k:W5 * k + W5], banks[j][:, 0:W5], ACT.Relu,
                                       bias=bias[:, 0, l:l + 1]).then_inc(lo_ok, 1)
                        act.wait_ge(lo_ok, K * l + k + 1)
                        banks.release(act, j)

            @block.vector
            def _(v):
                link = Steps(v, step)
                for t in range(T):
                    ins = v.bn_stats(stats[:, t], keep.res[:, t])
                link(ins)
                for t in range(T):
                    ins = v.bn_aggr(mv[:, t], stats[:, t])
                link(ins)
                v.tensor_scalar(var[:], mv[:, :, 1], EPS, None, ALU.add).then_inc(var_ok, 1)
                v.wait_ge(rstd_ok, 1)
                for t in range(T):
                    ins = v.tensor_scalar(keep.y[:, t], keep.res[:, t], mv[:, t, 0:1], rstd[:, t:t + 1], ALU.subtract, ALU.mult)
                link(ins)
                v.wait_ge(const_ok, 2)
                for t in range(T):
                    ins = v.scalar_tensor_tensor(marks[:, t], keep.y[:, t, MARKS:MARKS + 64].rearrange("p (m k) -> p m k", m=4), 0.5,
                                                 weigh[:].unsqueeze(1).to_broadcast([P, 4, 16]), ALU.is_gt, ALU.mult)
                link(ins)
                link(v.tensor_reduce(high[:], marks[:], AX.X, ALU.max))
                link(v.tensor_scalar(seen[:], high[:], 0.0, None, ALU.is_gt))
                link(v.tensor_scalar(high[:], high[:], -1.0, 16.0, ALU.mult, ALU.add))
                link(v.tensor_tensor(high[:], high[:], seen[:], ALU.mult))
                for p in range(2):
                    v.tensor_copy(feats[:, :, p, 0:2], high[:, :, p:4:2])
                    ins = v.tensor_copy(feats[:, :, p, 2], keep.y[:, :, OP])
                ins.then_inc(feats_ok, 1)
                link(v.tensor_scalar(asked[:], keep.y[:, :, 0:2], 0.5, None, ALU.is_ge))
                link(v.tensor_tensor(mask[:], asked[:, :, 0], asked[:, :, 1], ALU.mult))
                link(v.tensor_scalar(mask[:], mask[:], 2.0, None, ALU.mult))
                link(v.tensor_tensor(keep.res[:], keep.res[:], keep.y, ALU.add))
                v.wait_ge(w_in, 16 * 9)
                for l in range(W + 1):
                    for k in range(K):
                        j = M0 + 2 * (K * l + k) + 1
                        banks.wait_full(v, j)
                        v.tensor_scalar(hi[:, l % 2, W5 * k:W5 * k + W5], banks[j][0:HI, 0:W5], bias[0:HI, 1, l:l + 1], 0.0,
                                        ALU.add, ALU.max).then_inc(hi_ok, 1)
                        v.wait_ge(hi_ok, K * l + k + 1)
                        banks.release(v, j)
                banks.wait_full(v, LAST)
                link(v.tensor_scalar(result[:].rearrange("p a t -> p (a t)"), banks[LAST][0:P, 0:2 * T], bias_last[:, 0:1], 0.0,
                                     ALU.add, ALU.max))
                link(v.tensor_scalar(result[:], result[:], 15.0, ROUND, ALU.min, ALU.add))
                link(v.tensor_scalar(result[:], result[:], ROUND, None, ALU.subtract))
                for p in range(2):
                    link(v.tensor_tensor(hot[:, :, p], sixteen[:].unsqueeze(1).to_broadcast([P, T, 16]),
                                         result[:, p].unsqueeze(2).to_broadcast([P, T, 16]), ALU.is_equal))
                flat = hot[:].rearrange("p t a k -> p t (a k)")
                link(v.tensor_tensor(flat, flat, mask[:].unsqueeze(2).to_broadcast([P, T, 32]), ALU.mult))
                for q, (t0, n) in enumerate(QUADS):
                    to = keep.res[:, t0:t0 + n, OUT0:OUT0 + 32]
                    v.tensor_tensor(to, to, flat[:, t0:t0 + n], ALU.add).then_inc(out_ok, 1)


class Keep:
    pass


def program(nc, a, out, upto=99):
    with ExitStack() as ctx:
        b = Build(nc, a, out, ctx)
        keep = Keep()
        keep.edges = nc.dram_tensor("edge_lists", [2, EDGES + GROUP], F32).ap()
        keep.ident = b.sb(ctx, "ident", [128, 128])
        keep.ones = b.sb(ctx, "ones", [128, 128])
        keep.minus_half = b.sb(ctx, "minus_half", [128, T])
        keep.node_no = b.sb(ctx, "node_no", [128, NODES], I16)
        keep.tile_base = b.sb(ctx, "tile_base", [128, GROUPS])
        keep.group_offset = b.sb(ctx, "group_offset", [1, GROUPS], I32)
        keep.group_tile = b.sb(ctx, "group_tile", [1, GROUPS], I32)
        keep.x_in = b.sem(ctx, "x_in")
        keep.w_in = b.sem(ctx, "w_in")
        keep.y_all = b.sb(ctx, "y", [128, T * D])
        keep.y = keep.y_all[0:P].rearrange("p (t d) -> p t d", t=T)
        keep.x = keep.y
        keep.res = b.sb(ctx, "res", [P, T, D])
        keep.worth_rows = nc.dram_tensor("worth_rows", [NODES, NODES], F32).ap()
        keep.slots_in = nc.dram_tensor("slots_in", [(SLOTS + 1) * SLOT, D], F32).ap()
        keep.slots_out = nc.dram_tensor("slots_out", [SLOTS * SLOT, D], F32).ap()
        keep.place = b.sb(ctx, "place", [P, T], mybir.dt.uint32)
        keep.gate = b.sb(ctx, "gate", [P, T])
        keep.slot_tables = b.sb(ctx, "slot_tables_i", [1, 4, SLOTS + 1], I32)
        keep.slot_ends = b.sb(ctx, "slot_ends_i", [1, EXPERTS], I32)
        keep.absent = nc.dram_tensor("absent_rows", [NODES, NODES], BF16).ap()
        with ExitStack() as stage:
            keep.count = b.sb(stage, "count", [P, T + 1, NODES])
            with ExitStack() as weights:
                keep.w_rows = b.sb(weights, "w_rows", [128, 2, C, D])
                index_edges(b, keep)
                if upto > 1:
                    count_edges(b, keep)
                if upto > 2:
                    sage(b, keep)
        if upto > 3:
            with ExitStack() as stage:
                keep.o = b.sb(stage, "o", [P, T, D])
                attention(b, keep)
                if upto > 4:
                    routing(b, keep)
        if upto > 5:
            experts(b, keep)
        if upto > 6:
            with ExitStack() as stage:
                keep.worth_in = b.sem(ctx, "worth_in")
                keep.halves = nc.dram_tensor("halves_rows", [2 * HEADS, NODES], F32).ap()
                keep.shifts = nc.dram_tensor("shifts_rows", [2 * HEADS, NODES], F32).ap()
                keep.w = b.sb(stage, "w", [P, T, HEADS, HD + 1])
                keep.halves_p = b.sb(stage, "halves", [P, T, 2 * HEADS])
                keep.minus_src = b.sb(stage, "minus_src", [P, T, 2, HEADS])
                keep.worth = b.sb(stage, "worth", [P, T, NODES])
                gat_inputs(b, keep)
                if upto > 7:
                    gat_max(b, keep)
                    gat(b, keep)
        if upto > 8:
            last_mlp(b, keep)


def kernel(**inputs):
    import numpy as np
    import concourse.bacc as bacc
    from concourse.bass_utils import run_bass_kernel_spmd

    nc = bacc.Bacc("TRN2", target_bir_lowering=False, num_devices=1)
    arrays, args = {}, {}
    for name, value in inputs.items():
        arrays[f"in_{name}"] = value = np.ascontiguousarray(value)
        args[name] = nc.dram_tensor(f"in_{name}", value.shape, mybir.dt.from_np(value.dtype), kind="ExternalInput").ap()
    out = nc.dram_tensor("out", [NODES, D], F32, kind="ExternalOutput").ap()
    program(nc, args, out)
    return run_bass_kernel_spmd(nc, [arrays], core_ids=[0]).results[0]["out"]
```

```python
from contextlib import ExitStack

import concourse.bass as bass
from concourse import mybir

ALU = mybir.AluOpType
ACT = mybir.ActivationFunctionType
AX = mybir.AxisListType
F32 = mybir.dt.float32
BF16 = mybir.dt.bfloat16
I32 = mybir.dt.int32
I16 = mybir.dt.int16

NODES = 1250
EDGES = 20000
D = 512
P = 125
T = NODES // P
C = D // 128
EPS = 1e-5

RING = 3
CHUNKS = 6
GROUP = 128 * CHUNKS
GROUPS = -(-((EDGES + T * (GROUP - 1)) // GROUP) // 2) * 2
NOWHERE = 5000.0
EXPERTS = 8
FF = 4 * D
HEADS = 8
HD = D // HEADS
SLOPE = 0.2
LOWEST = -1e20
NEVER = 1e30
SLOT = 128
SLOTS = (NODES + EXPERTS * (SLOT - 1)) // SLOT
BANKS = 8
QUADS = [(0, 4), (4, 4), (8, 2)]
COLS = [(0, 512), (512, 512), (1024, 226)]


class Steps:

    def __init__(self, eng, sem, base=0):
        self.eng, self.sem, self.base, self.n = eng, sem, base, 0

    def __call__(self, ins):
        self.n += 1
        ins.then_inc(self.sem, 1)
        self.eng.wait_ge(self.sem, self.base + self.n)


class Build:
    def __init__(self, nc, a, out, ctx):
        self.nc, self.a, self.out, self.ctx = nc, a, out, ctx
        self.full = [self.sem(ctx, f"bank_full{i}") for i in range(BANKS)]
        self.free = [self.sem(ctx, f"bank_free{i}") for i in range(BANKS)]
        self.filled, self.emptied = [0] * BANKS, [0] * BANKS
        self.var_ok, self.rstd_ok, self.rooted = self.sem(ctx, "var_ok"), self.sem(ctx, "rstd_ok"), 0
        self.v_steps = Steps(None, self.sem(ctx, "vector_steps"))

    def steps_of(self, v):
        self.v_steps.eng = v
        return self.v_steps

    def roots(self, n):
        before, self.rooted = self.rooted, self.rooted + n
        return self.var_ok, self.rstd_ok, before

    def sb(self, ctx, name, shape, dt=F32):
        return ctx.enter_context(self.nc.sbuf_tensor(name, shape, dt))

    def ps(self, ctx, name, shape, dt=F32):
        return ctx.enter_context(self.nc.psum_tensor(name, shape, dt))

    def sem(self, ctx, name):
        return self.ctx.enter_context(self.nc.semaphore(name))


def index_edges(b, keep):
    nc, a = b.nc, b.a
    with ExitStack() as ctx:
        src_i = b.sb(ctx, "src_i", [P, EDGES // P], I32)
        dst_i = b.sb(ctx, "dst_i", [P, EDGES // P], I32)
        src_f = b.sb(ctx, "src_f", [P, EDGES // P])
        dst_f = b.sb(ctx, "dst_f", [P, EDGES // P])
        pad = b.sb(ctx, "pad", [2, GROUP])
        bounds = b.sb(ctx, "bounds", [P, T])
        below = b.sb(ctx, "below", [P, T, EDGES // P])
        part = b.sb(ctx, "part", [P, T])
        J = -(-EDGES // GROUP)
        steps_j = b.sb(ctx, "steps_j", [128, J])
        group_no = b.sb(ctx, "group_no", [128, GROUPS])
        more = b.sb(ctx, "more", [128, T, J])
        lo = b.sb(ctx, "lo", [128, T + 1])
        length = b.sb(ctx, "length", [128, T])
        n_groups = b.sb(ctx, "n_groups", [128, T])
        ends = b.sb(ctx, "ends", [128, T + 1])
        first = b.sb(ctx, "first", [128, T])
        past = b.sb(ctx, "past", [128, GROUPS, T])
        tile_of = b.sb(ctx, "tile_of", [128, GROUPS])
        shift = b.sb(ctx, "shift", [128, GROUPS])
        offset = b.sb(ctx, "offset", [128, GROUPS])
        counts = b.ps(ctx, "counts", [128, T])
        edges_in = b.sem(ctx, "edges_in")
        const_ok = b.sem(ctx, "const_ok")
        ident_ok = b.sem(ctx, "ident_ok")
        lists_ok = b.sem(ctx, "lists_ok")
        zeros = b.sb(ctx, "zeros", [128, D])
        zeros_ok = b.sem(ctx, "zeros_ok")
        zeros_out = b.sem(ctx, "zeros_out")
        lists_out = b.sem(ctx, "lists_out")
        parts_ok = b.sem(ctx, "parts_ok")
        counts_ok = b.sem(ctx, "counts_ok")
        with nc.Block() as block:

            @block.sync
            def _(sp):
                sp.dma_start(dst_i[:], a["dst"].rearrange("(p e) -> p e", p=P)).then_inc(edges_in, 16)
                sp.dma_start(src_i[:], a["src"].rearrange("(p e) -> p e", p=P)).then_inc(edges_in, 16)
                sp.dma_start(keep.x, a["x"].rearrange("(t p) d -> p t d", p=P)).then_inc(keep.x_in, 16)
                for w, name in enumerate(("L0_gnn_W_self", "L0_gnn_W_neigh")):
                    sp.dma_start(keep.w_rows[:, w], a[name].rearrange("(k p) d -> p k d", p=128)).then_inc(keep.w_in, 16)
                sp.wait_ge(zeros_ok, 1)
                sp.dma_start(keep.slots_in.rearrange("(s p) d -> p s d", p=SLOT),
                             zeros[:].unsqueeze(1).to_broadcast([128, SLOTS + 1, D])).then_inc(zeros_out, 16)
                sp.wait_ge(lists_ok, 2)
                sp.wait_ge(const_ok, 1)
                sp.dma_start(keep.edges[0, 0:EDGES].rearrange("(p e) -> p e", p=P), src_f[:]).then_inc(lists_out, 16)
                sp.dma_start(keep.edges[1, 0:EDGES].rearrange("(p e) -> p e", p=P), dst_f[:]).then_inc(lists_out, 16)
                sp.dma_start(keep.edges[:, EDGES:EDGES + GROUP], pad[:]).then_inc(lists_out, 16)
                sp.wait_ge(lists_out, 48)
                sp.wait_ge(zeros_out, 16)

            @block.gpsimd
            def _(pool):
                pool.memset(zeros[:], 0.0).then_inc(zeros_ok, 1)
                pool.memset(pad[:], NOWHERE).then_inc(const_ok, 1)
                pool.iota(bounds[:], [[P, T]], base=P, channel_multiplier=0,
                          allow_small_or_imprecise_dtypes=True).then_inc(const_ok, 1)
                pool.memset(keep.ones[:], 1.0).then_inc(const_ok, 1)
                pool.memset(keep.minus_half[:], -0.5)
                pool.iota(steps_j[:], [[GROUP, J]], base=0, channel_multiplier=0,
                          allow_small_or_imprecise_dtypes=True).then_inc(const_ok, 1)
                pool.iota(group_no[:], [[1, GROUPS]], base=0, channel_multiplier=0,
                          allow_small_or_imprecise_dtypes=True).then_inc(const_ok, 1)
                pool.iota(keep.node_no[:], [[1, NODES]], base=0, channel_multiplier=0).then_inc(const_ok, 1)
                pool.memset(keep.ident[:], 0.0).then_inc(ident_ok, 1)
                pool.wait_ge(ident_ok, 1)
                pool.affine_select(out=keep.ident[:], in_=keep.ident[:], compare_op=ALU.not_equal, fill=1.0,
                                   base=0, pattern=[[-1, 128]], channel_multiplier=1).then_inc(ident_ok, 1)
                pool.memset(keep.count[:], 0.0).then_inc(ident_ok, 1)

            @block.tensor
            def _(pe):
                pe.wait_ge(parts_ok, 1)
                pe.wait_ge(const_ok, 6)
                pe.matmul(counts[:], keep.ones[0:P, :], part[:], start=True, stop=True).then_inc(counts_ok, 1)

            @block.vector
            def _(v):
                v.wait_ge(edges_in, 32)
                v.tensor_copy(dst_f[:], dst_i[:]).then_inc(lists_ok, 1)
                v.tensor_copy(src_f[:], src_i[:]).then_inc(lists_ok, 1)
                v.wait_ge(lists_ok, 2)
                v.wait_ge(const_ok, 6)
                link = b.steps_of(v)
                link(v.tensor_tensor(below[:], dst_f[:].unsqueeze(1).to_broadcast([P, T, EDGES // P]),
                                     bounds[:].unsqueeze(2).to_broadcast([P, T, EDGES // P]), ALU.is_lt))
                v.tensor_reduce(part[:], below[:], AX.X, ALU.add).then_inc(parts_ok, 1)
                link(v.memset(lo[:, 0:1], 0.0))
                link(v.memset(ends[:, 0:1], 0.0))
                v.wait_ge(counts_ok, 1)
                link(v.tensor_copy(lo[:, 1:T + 1], counts[:]))
                link(v.tensor_tensor(length[:], lo[:, 1:T + 1], lo[:, 0:T], ALU.subtract))
                link(v.tensor_tensor(more[:], length[:].unsqueeze(2).to_broadcast([128, T, J]),
                                     steps_j[:].unsqueeze(1).to_broadcast([128, T, J]), ALU.is_gt))
                link(v.tensor_reduce(n_groups[:], more[:], AX.X, ALU.add))
                link(v.tensor_tensor_scan(ends[:, 1:T + 1], keep.ones[:, 0:T], n_groups[:], 0.0, ALU.mult, ALU.add))
                link(v.scalar_tensor_tensor(first[:], ends[:, 0:T], -float(GROUP), lo[:, 0:T], ALU.mult, ALU.add))
                link(v.tensor_tensor(past[:], group_no[:].unsqueeze(2).to_broadcast([128, GROUPS, T]),
                                     ends[:, 1:T + 1].unsqueeze(1).to_broadcast([128, GROUPS, T]), ALU.is_ge))
                link(v.tensor_reduce(tile_of[:], past[:], AX.X, ALU.add))
                link(v.tensor_scalar(keep.tile_base[:], tile_of[:], float(P), None, ALU.mult))
                link(v.tensor_scalar(shift[:], past[:, :, 0], -1.0, 1.0, ALU.mult, ALU.add))
                link(v.tensor_scalar(offset[:], shift[:], first[:, 0:1], None, ALU.mult))
                for t in range(1, T):
                    link(v.tensor_tensor(shift[:], past[:, :, t - 1], past[:, :, t], ALU.subtract))
                    link(v.scalar_tensor_tensor(offset[:], shift[:], first[:, t:t + 1], offset[:], ALU.mult, ALU.add))
                link(v.scalar_tensor_tensor(offset[:], group_no[:], float(GROUP), offset[:], ALU.mult, ALU.add))
                link(v.tensor_scalar(offset[:], offset[:], float(EDGES), 0.0, ALU.min, ALU.max))
                link(v.tensor_copy(keep.group_offset[:], offset[0:1, :]))
                link(v.tensor_copy(keep.group_tile[:], tile_of[0:1, :]))


def count_edges(b, keep):
    nc = b.nc
    with ExitStack() as ctx:
        ends = b.sb(ctx, "edge_ends", [128, 2, 2, CHUNKS])
        near = b.sb(ctx, "near", [128, 2, CHUNKS])
        hot_src = b.sb(ctx, "hot_src", [128, RING, NODES], BF16)
        hot_dst = b.sb(ctx, "hot_dst", [128, RING, P], BF16)
        sums = b.ps(ctx, "sums", [128, 2, 2048])
        ends_in = [b.sem(ctx, f"ends_in{u}") for u in range(2)]
        near_ok = b.sem(ctx, "near_ok")
        hot_ok = b.sem(ctx, "hot_ok")
        hot_free = b.sem(ctx, "hot_free")
        sums_added = b.sem(ctx, "sums_added")
        with nc.Block() as block:

            @block.sync
            def _(sp):
                def load(m, u):
                    at = sp.value_load(keep.group_offset[0:1, bass.ds(m, 1)], min_val=0, max_val=EDGES)
                    sp.dma_start(ends[:, u], keep.edges[:, bass.ds(at, GROUP)].rearrange("e (p c) -> p e c", p=128)
                                 ).then_inc(ends_in[u], 16)

                load(0, 0)
                load(1, 1)
                with sp.Fori(1, GROUPS // 2) as i:
                    for u in range(2):
                        sp.wait_ge(hot_ok, CHUNKS * (2 * i + u - 1))
                        load(2 * i + u, u)

            @block.vector
            def _(v):
                v.sem_inc(hot_free, RING)

                def hots(m, u, k):
                    v.wait_ge(ends_in[u], 16 * k + 16)
                    v.tensor_scalar(near[:, u], ends[:, u, 1], keep.tile_base[:, bass.ds(m, 1)], None,
                                    ALU.subtract).then_inc(near_ok, 1)
                    v.wait_ge(near_ok, m + 1)
                    for c in range(CHUNKS):
                        v.wait_ge(hot_free, CHUNKS * m + c + 1)
                        n = c % RING
                        v.tensor_scalar(hot_dst[:, n], keep.node_no[:, 0:P], near[:, u, c:c + 1], None, ALU.is_equal)
                        v.tensor_scalar(hot_src[:, n], keep.node_no[:], ends[:, u, 0, c:c + 1], None,
                                        ALU.is_equal).then_inc(hot_ok, 1)

                def add(m, u):
                    v.wait_ge(hot_free, RING + CHUNKS * (m + 1))
                    row = v.value_load(keep.group_tile[0:1, bass.ds(m, 1)], min_val=0, max_val=T)
                    v.wait_ge(sums_added, m)
                    to = keep.count[:, bass.ds(row, 1), :].rearrange("p a n -> p (a n)")
                    v.tensor_tensor(to, sums[0:P, u, 0:NODES], to, ALU.add).then_inc(sums_added, 1)

                hots(0, 0, 0)
                with v.Fori(0, GROUPS // 2 - 1) as i:
                    hots(2 * i + 1, 1, i)
                    add(2 * i, 0)
                    hots(2 * i + 2, 0, i + 1)
                    add(2 * i + 1, 1)
                hots(GROUPS - 1, 1, GROUPS // 2 - 1)
                add(GROUPS - 2, 0)
                add(GROUPS - 1, 1)

            @block.tensor
            def _(pe):
                def group(m, u):
                    for c in range(CHUNKS):
                        pe.wait_ge(hot_ok, CHUNKS * m + c + 1)
                        n = c % RING
                        for c0, w in COLS:
                            ins = pe.matmul(sums[0:P, u, c0:c0 + w], hot_dst[:, n], hot_src[:, n, c0:c0 + w],
                                            start=(c == 0), stop=(c == CHUNKS - 1))
                        ins.then_inc(hot_free, 1)

                group(0, 0)
                group(1, 1)
                with pe.Fori(1, GROUPS // 2) as i:
                    for u in range(2):
                        pe.wait_ge(sums_added, 2 * i + u - 1)
                        group(2 * i + u, u)


class Banks:

    def __init__(self, b, ctx, name, ring=BANKS):
        self.b, self.ring = b, ring
        self.at = b.ps(ctx, name, [128, ring, 512])
        self.full0, self.free0 = list(b.filled), list(b.emptied)

    def __getitem__(self, j):
        return self.at[:, j % self.ring]

    def wait_emptied(self, eng, j):
        i = j % self.ring
        eng.wait_ge(self.b.free[i], self.free0[i] + j // self.ring + 1)

    def wait_free(self, pe, j):
        if j >= self.ring:
            self.wait_emptied(pe, j - self.ring)

    def wait_full(self, eng, j):
        i = j % self.ring
        eng.wait_ge(self.b.full[i], self.full0[i] + j // self.ring + 1)

    def filled(self, ins, j):
        self.b.filled[j % self.ring] += 1
        ins.then_inc(self.b.full[j % self.ring], 1)

    def emptied(self, ins, j):
        self.b.emptied[j % self.ring] += 1
        ins.then_inc(self.b.free[j % self.ring], 1)

    def release(self, eng, j):
        self.b.emptied[j % self.ring] += 1
        eng.sem_inc(self.b.free[j % self.ring], 1)


def variance_root(pool, rstd, var, minus_half):
    return pool.tensor_tensor(rstd, var, minus_half, ALU.pow)


def sage(b, keep):
    nc, a = b.nc, b.a
    with ExitStack() as ctx:
        w_t = b.sb(ctx, "w_t", [128, 2, C, D])
        xt = b.sb(ctx, "xt", [128, T * D])
        xn_t = xt[:, 0:C * NODES].rearrange("p (c n) -> p c n", c=C)
        x_again = xt[0:P, :].rearrange("p (t d) -> p t d", t=T)
        from_src = b.sb(ctx, "from_src", [P, 2, T, P])
        absent = b.sb(ctx, "absent", [P, 2, NODES], BF16)
        tiny = b.sb(ctx, "tiny", [P, 1])
        logs = b.sb(ctx, "logs", [P, 2, T, P])
        worth = b.sb(ctx, "worth_part", [P, 2, T, P])
        tiny_ok = b.sem(ctx, "tiny_ok")
        logs_ok = b.sem(ctx, "logs_ok")
        worth_ok = b.sem(ctx, "worth_ok")
        worth_out = [b.sem(ctx, f"worth_out{u}") for u in range(2)]
        row3 = b.sb(ctx, "sage_rows", [P, 3, D])
        stats = b.sb(ctx, "stats", [P, T, 3, 6])
        mv = b.sb(ctx, "mv", [P, T, 3, 2])
        var = b.sb(ctx, "var", [P, T, 3])
        rstd = b.sb(ctx, "rstd", [P, T, 3])
        degree = b.sb(ctx, "degree", [P, T])
        rdeg = b.sb(ctx, "rdeg", [P, T])
        banks = Banks(b, ctx, "sage_banks")
        rows_in = b.sem(ctx, "sage_rows_in")
        x_again_in = b.sem(ctx, "x_again_in")
        var_ok, rstd_ok, roots = b.roots(1 + 2 * T)
        xn_ok = b.sem(ctx, "xn_ok")
        wt_ok = b.sem(ctx, "wt_ok")
        xnt_ok = b.sem(ctx, "xnt_ok")
        z_ok = b.sem(ctx, "z_ok")
        from_ok = b.sem(ctx, "from_ok")
        agg_ok = b.sem(ctx, "agg_ok")
        absent_ok = b.sem(ctx, "absent_ok")
        absent_out = [b.sem(ctx, f"absent_out{u}") for u in range(2)]
        step = b.sem(ctx, "sage_step")

        W0 = 0
        X0 = W0 + 2 * C
        Z0 = X0 + C * len(QUADS)
        S0 = Z0 + T
        E0 = S0 + T
        def turn_job(t, q):
            return E0 + (q if t == 0 else 3 + 4 * (t - 1) + q)
        def sum_job(t):
            return E0 + (3 + 4 * t + 3 if t < T - 1 else 3 + 4 * (T - 1))

        with nc.Block() as block:

            @block.sync
            def _(sp):
                for k, name in enumerate(("L0_gnn_bias", "L0_gnn_gamma", "L0_gnn_beta")):
                    sp.dma_start(row3[:, k], a[name].unsqueeze(0).to_broadcast([P, D])).then_inc(rows_in, 16)
                for t in range(T):
                    sp.wait_ge(absent_ok, t + 1)
                    sp.dma_start(keep.absent[t * P:(t + 1) * P, :], absent[:, t % 2]).then_inc(absent_out[t % 2], 16)
                banks.wait_full(sp, S0 + T - 1)
                sp.dma_start(x_again, a["x"].rearrange("(t p) d -> p t d", p=P)).then_inc(x_again_in, 16)
                for t in range(T):
                    sp.wait_ge(worth_ok, 2 * t + 2)
                    sp.dma_start(keep.worth_rows.rearrange("(s p) n -> p s n", p=P)[:, :, P * t:P * t + P], worth[:, t % 2]
                                 ).then_inc(worth_out[t % 2], 16)
                for u in range(2):
                    sp.wait_ge(absent_out[u], 16 * T // 2)
                    sp.wait_ge(worth_out[u], 16 * T // 2)

            @block.tensor
            def _(pe):
                pe.wait_ge(keep.w_in, 32)
                for w in range(2):
                    for c in range(C):
                        j = W0 + w * C + c
                        banks.wait_free(pe, j)
                        for k in range(C):
                            ins = pe.transpose(banks[j][:, 128 * k:128 * k + 128],
                                               keep.w_rows[:, w, k, 128 * c:128 * c + 128], keep.ident[:])
                        banks.filled(ins, j)
                for q, (t0, n) in enumerate(QUADS):
                    pe.wait_ge(xn_ok, t0 + n)
                    for c in range(C):
                        j = X0 + C * q + c
                        banks.wait_free(pe, j)
                        for t in range(n):
                            ins = pe.transpose(banks[j][:, P * t:P * t + P],
                                               keep.y[:, t0 + t, 128 * c:128 * c + 128], keep.ident[0:P, 0:P])
                        banks.filled(ins, j)
                pe.wait_ge(wt_ok, 2 * C)
                pe.wait_ge(xnt_ok, C * len(QUADS))
                for w, first in ((1, Z0), (0, S0)):
                    for t in range(T):
                        banks.wait_free(pe, first + t)
                        for c in range(C):
                            ins = pe.matmul(banks[first + t][0:P, :], xn_t[:, c, P * t:P * t + P], w_t[:, w, c],
                                            start=(c == 0), stop=(c == C - 1))
                        banks.filled(ins, first + t)

                def turn(t):
                    for q, (s0, n) in enumerate(QUADS):
                        j = turn_job(t, q)
                        banks.wait_free(pe, j)
                        for s in range(n):
                            ins = pe.transpose(banks[j][0:P, P * s:P * s + P],
                                               keep.count[:, t, P * (s0 + s):P * (s0 + s) + P], keep.ident[0:P, 0:P])
                        banks.filled(ins, j)

                turn(0)
                pe.wait_ge(z_ok, T)
                for t in range(T):
                    if t + 1 < T:
                        turn(t + 1)
                    pe.wait_ge(from_ok, 3 * t + 3)
                    j = sum_job(t)
                    banks.wait_free(pe, j)
                    for s in range(T):
                        ins = pe.matmul(banks[j][0:P, :], from_src[:, t % 2, s], keep.y[:, s],
                                        start=(s == 0), stop=(s == T - 1))
                    banks.filled(ins, j)

            @block.scalar
            def _(act):
                def evacuate(j, to, of, done):
                    banks.wait_full(act, j)
                    banks.emptied(act.activation(to, of, ACT.Copy), j)

                for j in range(2 * C):
                    banks.wait_full(act, W0 + j)
                    act.activation(w_t[:, j // C, j % C], banks[W0 + j][:, :], ACT.Copy).then_inc(wt_ok, 1)
                    act.wait_ge(wt_ok, j + 1)
                    banks.release(act, W0 + j)
                for q, (t0, n) in enumerate(QUADS):
                    for c in range(C):
                        j = X0 + C * q + c
                        banks.wait_full(act, j)
                        act.activation(xn_t[:, c, P * t0:P * (t0 + n)], banks[j][:, 0:P * n], ACT.Copy).then_inc(xnt_ok, 1)
                        act.wait_ge(xnt_ok, C * q + c + 1)
                        banks.release(act, j)
                for t in range(T):
                    banks.wait_full(act, Z0 + t)
                    act.activation(keep.y[:, t], banks[Z0 + t][0:P, :], ACT.Copy).then_inc(z_ok, 1)
                    act.wait_ge(z_ok, t + 1)
                    banks.release(act, Z0 + t)

                act.wait_ge(tiny_ok, 1)
                for t in range(T):
                    for q, (s0, n) in enumerate(QUADS):
                        j = turn_job(t, q)
                        banks.wait_full(act, j)
                        if t >= 2:
                            banks.wait_full(act, sum_job(t - 2))
                            act.wait_ge(worth_ok, 2 * t - 2)
                        act.activation(from_src[:, t % 2, s0:s0 + n],
                                       banks[j][0:P, 0:P * n].rearrange("p (s d) -> p s d", s=n), ACT.Copy).then_inc(from_ok, 1)
                        act.wait_ge(from_ok, 3 * t + q + 1)
                        banks.release(act, j)
                    act.activation(logs[:, t % 2], from_src[:, t % 2], ACT.Ln, bias=tiny[:]).then_inc(logs_ok, 1)

            @block.gpsimd
            def _(pool):
                pool.memset(tiny[:], 1e-19).then_inc(tiny_ok, 1)
                pool.wait_ge(var_ok, roots + 1)
                variance_root(pool, rstd[:, :, 0], var[:, :, 0], keep.minus_half[0:P, 0:T]).then_inc(rstd_ok, 1)
                for t in range(T + 1):
                    if t < T:
                        pool.wait_ge(from_ok, 3 * t + 3)
                        if t >= 2:
                            pool.wait_ge(worth_out[t % 2], 16 * (t // 2))
                        pool.tensor_scalar(worth[:, t % 2], from_src[:, t % 2], 0.0, NEVER, ALU.is_equal, ALU.mult).then_inc(worth_ok, 1)
                        pool.wait_ge(worth_ok, 2 * t + 1)
                        pool.wait_ge(logs_ok, t + 1)
                        pool.tensor_tensor(worth[:, t % 2], worth[:, t % 2], logs[:, t % 2], ALU.subtract).then_inc(worth_ok, 1)
                    if t >= 1:
                        for k in (1, 2):
                            pool.wait_ge(var_ok, roots + 2 * (t - 1) + k + 1)
                            variance_root(pool, rstd[:, t - 1, k:k + 1], var[:, t - 1, k:k + 1],
                                          keep.minus_half[0:P, 0:1]).then_inc(rstd_ok, 1)

            @block.vector
            def _(v):
                link = b.steps_of(v)
                v.wait_ge(keep.x_in, 16)
                for t in range(T):
                    ins = v.bn_stats(stats[:, t, 0], keep.y[:, t])
                link(ins)
                for t in range(T):
                    ins = v.bn_aggr(mv[:, t, 0], stats[:, t, 0])
                link(ins)
                v.tensor_scalar(var[:, :, 0], mv[:, :, 0, 1], EPS, None, ALU.add).then_inc(var_ok, 1)
                v.wait_ge(rstd_ok, roots + 1)
                for t in range(T):
                    v.tensor_scalar(keep.y[:, t], keep.y[:, t], mv[:, t, 0, 0:1], rstd[:, t, 0:1],
                                    ALU.subtract, ALU.mult).then_inc(xn_ok, 1)
                for t in range(T):
                    if t >= 2:
                        v.wait_ge(absent_out[t % 2], 16 * (t // 2))
                    v.tensor_scalar(absent[:, t % 2], keep.count[:, t], 0.0, -3e38, ALU.is_equal, ALU.mult).then_inc(absent_ok, 1)
                    link(v.tensor_reduce(degree[:, t:t + 1], keep.count[:, t], AX.X, ALU.add))
                link(v.tensor_scalar(degree[:], degree[:], 1.0, None, ALU.max))
                link(v.reciprocal(rdeg[:], degree[:]))
                v.wait_ge(rows_in, 48)
                for t in range(T):
                    banks.wait_full(v, S0 + t)
                    link(v.tensor_tensor(keep.res[:, t], banks[S0 + t][0:P, :], row3[:, 0], ALU.add))
                    banks.release(v, S0 + t)
                for t in range(T):
                    r = keep.res[:, t]
                    j = sum_job(t)
                    banks.wait_full(v, j)
                    link(v.scalar_tensor_tensor(r, banks[j][0:P, :], rdeg[:, t:t + 1], r, ALU.mult, ALU.add))
                    banks.release(v, j)

                    def normed(k, to):
                        link(v.bn_stats(stats[:, t, k], r))
                        link(v.bn_aggr(mv[:, t, k], stats[:, t, k]))
                        v.tensor_scalar(var[:, t, k:k + 1], mv[:, t, k, 1:2], EPS, None, ALU.add).then_inc(var_ok, 1)
                        v.wait_ge(rstd_ok, roots + 2 * t + k + 1)
                        link(v.tensor_scalar(to, r, mv[:, t, k, 0:1], rstd[:, t, k:k + 1], ALU.subtract, ALU.mult))

                    normed(1, r)
                    link(v.tensor_tensor(r, r, row3[:, 1], ALU.mult))
                    link(v.tensor_tensor(r, r, row3[:, 2], ALU.add))
                    if t == 0:
                        v.wait_ge(x_again_in, 16)
                    link(v.tensor_tensor(r, r, x_again[:, t], ALU.add))
                    normed(2, x_again[:, t])
                banks.wait_full(v, sum_job(T - 1))
                v.tensor_copy(keep.y, x_again)


def turn_rows(pe, banks, first, rows, ident):
    for q, (t0, n) in enumerate(QUADS):
        for c in range(C):
            j = first + C * q + c
            banks.wait_free(pe, j)
            for t in range(n):
                ins = pe.transpose(banks[j][:, P * t:P * t + P], rows[:, t0 + t, 128 * c:128 * c + 128], ident[0:P, 0:P])
            banks.filled(ins, j)


def turned_out(act, banks, first, cols):
    for q, (t0, n) in enumerate(QUADS):
        for c in range(C):
            j = first + C * q + c
            banks.wait_full(act, j)
            banks.emptied(act.activation(cols[:, c, P * t0:P * (t0 + n)], banks[j][:, 0:P * n], ACT.Copy), j)


def attention(b, keep):
    nc, a = b.nc, b.a
    H, HD = 8, 64
    PAIRS = H // 2
    U = 2 * T
    with ExitStack() as ctx:
        y_t = b.sb(ctx, "y_t", [128, C, NODES])
        vals = b.sb(ctx, "vals", [P, T, H, HD])
        w_v = b.sb(ctx, "w_v", [128, C, D])
        bv = b.sb(ctx, "bv", [P, D])
        bq = b.sb(ctx, "bq", [128, 2, PAIRS])
        w_qk = b.sb(ctx, "w_qk", [128, 2, C, 128])
        v_in = b.sem(ctx, "v_in")
        bqk_in = b.sem(ctx, "bqk_in")
        w_qk_in = b.sem(ctx, "w_qk_in")
        sources = [a["L0_ffn_" + n].rearrange("(c p) n -> p c n", p=128) for n in ("Wq", "Wk")]
        with ExitStack() as stage:
            banks = Banks(b, stage, "value_banks")
            with nc.Block() as block:

                @block.sync
                def _(sp):
                    sp.dma_start(w_v[:], a["L0_ffn_Wv"].rearrange("(c p) n -> p c n", p=128)).then_inc(v_in, 16)
                    sp.dma_start(bv[:], a["L0_ffn_bv"].unsqueeze(0).to_broadcast([P, D])).then_inc(v_in, 16)
                    for k, n in enumerate(("bq", "bk")):
                        sp.dma_start(bq[:, k], a["L0_ffn_" + n].rearrange("(i p) -> p i", p=128),
                                     allow_slow_non_contiguous=True).then_inc(bqk_in, 16)
                    for k in range(2):
                        sp.dma_start(w_qk[:, k], sources[k][:, :, 0:128]).then_inc(w_qk_in, 16)

                @block.tensor
                def _(pe):
                    turn_rows(pe, banks, 0, keep.y, keep.ident)
                    first = C * len(QUADS)
                    pe.wait_ge(v_in, 32)
                    for j in range(first - BANKS, first):
                        banks.wait_emptied(pe, j)
                    for t in range(T):
                        j = first + t
                        banks.wait_free(pe, j)
                        for c in range(C):
                            ins = pe.matmul(banks[j][0:P, :], y_t[:, c, P * t:P * t + P], w_v[:, c],
                                            start=(c == 0), stop=(c == C - 1))
                        banks.filled(ins, j)

                @block.scalar
                def _(act):
                    turned_out(act, banks, 0, y_t)

                @block.vector
                def _(v):
                    v.wait_ge(v_in, 32)
                    for t in range(T):
                        j = C * len(QUADS) + t
                        banks.wait_full(v, j)
                        banks.emptied(v.tensor_tensor(vals[:, t].rearrange("p h d -> p (h d)"), banks[j][0:P, :], bv[:], ALU.add), j)

        with ExitStack() as stage:
            S, HALF = HD ** -0.5, T // 2
            KEPT = 8
            q_t = b.sb(stage, "q_t", [128, 2, NODES])
            k_t = b.sb(stage, "k_t", [128, NODES])
            zeros_ok = b.sem(stage, "q_zeros_ok")
            probs = b.sb(stage, "probs", [P, 2, NODES])
            probs_t = b.sb(stage, "probs_t", [P, 4, T, P])
            mixed_t = b.sb(stage, "mixed_t", [128, 2, P])
            top = b.sb(stage, "top", [P, 2])
            shift = b.sb(stage, "neg_max", [P, 2])
            bq_now = b.sb(stage, "bq_now", [128, 1])
            total = b.sb(stage, "total", [P, KEPT])
            share = b.sb(stage, "share", [P, 2, 2])
            vals_now = b.sb(stage, "vals_now", [P, T, 2, HD])
            vals_ok = b.sem(stage, "vals_ok")
            scores = b.ps(stage, "scores", [128, 2, 3 * 512])
            turned = b.ps(stage, "turned", [128, 512])
            mixed = b.ps(stage, "mixed", [128, 512])
            bq_ok = b.sem(stage, "bq_ok")
            proj_ok = b.sem(stage, "proj_ok")
            q_ok = b.sem(stage, "q_ok")
            k_ok = b.sem(stage, "k_ok")
            scores_ok = b.sem(stage, "scores_ok")
            max_ok = b.sem(stage, "max_ok")
            shift_ok = b.sem(stage, "shift_ok")
            probs_ok = b.sem(stage, "probs_ok")
            turned_ok = [b.sem(stage, f"turned_ok{q}") for q in range(3)]
            copied = [b.sem(stage, f"copied{q}") for q in range(3)]
            mixed_ok = b.sem(stage, "mixed_ok")
            mixed_out = b.sem(stage, "mixed_out")
            back_ok = b.sem(stage, "back_ok")
            share_ok = b.sem(stage, "share_ok")
            back_out = b.sem(stage, "back_out")
            STEPS = U + 6

            def turning(j):
                return j - 2 if 2 <= j < U + 2 else None

            def mixing(j):
                return divmod(j - 4, 2) if 4 <= j < U + 4 else (None, 0)

            def turns_back(j):
                return (j - 6) // 2 if j >= 6 and j % 2 == 0 else None

            with nc.Block() as block:

                @block.gpsimd
                def _(pool):
                    for h in range(2):
                        pool.memset(q_t[HD * (1 - h):HD * (2 - h), h], 0.0).then_inc(zeros_ok, 1)

                @block.sync
                def _(sp):
                    with sp.Fori(1, PAIRS) as i:
                        sp.wait_ge(proj_ok, 6 * i)
                        for k in range(2):
                            sp.dma_start(w_qk[:, k], sources[k][:, :, bass.ds(128 * i, 128)]).then_inc(w_qk_in, 16)

                @block.tensor
                def _(pe):
                    def project(x):
                        c0, w = COLS[x % 3]
                        for c in range(C):
                            ins = pe.matmul(scores[:, x // 3, c0:c0 + w], w_qk[:, 1 - x // 3, c], y_t[:, c, c0:c0 + w],
                                            start=(c == 0), stop=(c == C - 1))
                        ins.then_inc(proj_ok, 1)

                    def turn(i, j, q):
                        k = turning(j)
                        if k is None:
                            return
                        n = U * i + k
                        if q == 0:
                            pe.wait_ge(probs_ok, n + 3)
                            pe.wait_ge(copied[2], n + 1)
                            pe.wait_ge(back_out, T * i + max(0, (j - 5) // 2) + 1)
                        else:
                            pe.wait_ge(copied[q - 1], n + 2)
                        s0, m = QUADS[q]
                        for s in range(m):
                            ins = pe.transpose(turned[0:P, P * s:P * s + P], probs[:, k % 2, P * (s0 + s):P * (s0 + s) + P],
                                               keep.ident[0:P, 0:P])
                        ins.then_inc(turned_ok[q], 1)

                    def mix(i, j, s0, s1):
                        t, half = mixing(j)
                        if t is None:
                            return
                        m = T * i + t
                        if s0 == 0:
                            if half == 0:
                                pe.wait_ge(mixed_out, m + 1)
                                pe.wait_ge(copied[0], 2 * m + 3)
                                pe.wait_ge(copied[1], 2 * m + 3)
                            else:
                                pe.wait_ge(copied[2], 2 * m + 3)
                        for s in range(HALF * half + s0, HALF * half + s1):
                            for h in range(2):
                                rows = slice(HD * h, HD * h + HD)
                                ins = pe.matmul(mixed[rows, 0:P], vals_now[:, s, h], probs_t[:, (2 * t + h) % 4, s],
                                                start=(s == 0), stop=(s == T - 1), tile_position=(0, HD * h))
                        if half and s1 == HALF:
                            ins.then_inc(mixed_ok, 1)

                    def turn_back(i, j):
                        t = turns_back(j)
                        if t is None:
                            return
                        m = T * i + t
                        pe.wait_ge(mixed_out, m + 2)
                        pe.wait_ge(copied[2], U * i + min(j - 2, U - 1) + 2)
                        pe.wait_ge(back_out, m + 1)
                        pe.transpose(turned[0:P, 0:128], mixed_t[:, t % 2], keep.ident[:]).then_inc(back_ok, 1)

                    def steps(i, last=False):
                        for j in range(STEPS):
                            if mixing(j) == (0, 0):
                                pe.wait_ge(vals_ok, i + 1)
                            if j < U:
                                if j == 0:
                                    pe.wait_ge(k_ok, 3 * i + 3)
                                    pe.wait_ge(q_ok, 6 * i + 2)
                                if j == 1:
                                    pe.wait_ge(q_ok, 6 * i + 6)
                                pe.wait_ge(probs_ok, U * i + j + 1)
                                t, h = divmod(j, 2)
                            elif not last:
                                x = j - U
                                if x == 0:
                                    pe.wait_ge(w_qk_in, 32 * i + 64)
                                pe.wait_ge(probs_ok, U * i + U - 2 + x // 3 + 3)
                            for part, (c0, w) in enumerate(COLS):
                                if j < U:
                                    ins = pe.matmul(scores[0:P, h, c0:c0 + w], q_t[:, h, P * t:P * t + P], k_t[:, c0:c0 + w],
                                                    start=True, stop=True)
                                elif part == 0 and not last:
                                    project(x)
                                turn(i, j, part)
                                mix(i, j, max(0, 2 * part - 1), 2 * part + 1)
                            if j < U:
                                ins.then_inc(scores_ok, 1)
                            turn_back(i, j)

                    pe.sem_inc(mixed_ok, 2)
                    pe.sem_inc(back_ok, 2)
                    pe.sem_inc(turned_ok[2], 2)
                    pe.wait_ge(zeros_ok, 2)
                    pe.wait_ge(w_qk_in, 32)
                    for x in range(6):
                        project(x)
                    with pe.Fori(0, PAIRS - 1) as i:
                        steps(i)
                    steps(PAIRS - 1, last=True)

                @block.scalar
                def _(act):
                    def queries(p, x):
                        c0, w = COLS[x]
                        if x == 0:
                            act.wait_ge(bq_ok, p + 1)
                        act.wait_ge(proj_ok, 6 * p + 3 + x + 1)
                        for h in range(2):
                            rows = slice(HD * h, HD * h + HD)
                            act.activation(q_t[rows, h, c0:c0 + w], scores[rows, 1, c0:c0 + w], ACT.Identity,
                                           bias=bq_now[rows, :]).then_inc(q_ok, 1)

                    def copy(i, j, q):
                        k = turning(j)
                        if k is None:
                            return
                        n = U * i + k
                        if q == 0:
                            act.wait_ge(mixed_ok, T * i + k // 2 + 1)
                            act.wait_ge(turned_ok[0], n + 1)
                        else:
                            act.wait_ge(turned_ok[2], n + 3)
                        s0, m = QUADS[q]
                        act.activation(probs_t[:, k % 4, s0:s0 + m], turned[0:P, 0:P * m].rearrange("p (s d) -> p s d", s=m),
                                       ACT.Copy).then_inc(copied[q], 1)

                    def steps(i, last=False):
                        for j in range(STEPS):
                            copy(i, j, 0)
                            if 1 <= j <= U:
                                k = j - 1
                                n = U * i + k
                                act.wait_ge(shift_ok, n + 1)
                                act.wait_ge(turned_ok[2], n + 1)
                                act.activation(probs[:, k % 2], scores[0:P, k % 2, 0:NODES], ACT.Exp, bias=shift[:, k % 2:k % 2 + 1],
                                               scale=S, accum_out=total[:, k % KEPT:k % KEPT + 1]).then_inc(probs_ok, 1)
                            copy(i, j, 2)
                            if not last and j >= U + 3:
                                queries(i + 1, j - U - 3)

                    act.sem_inc(probs_ok, 2)
                    act.sem_inc(copied[0], 1)
                    act.sem_inc(copied[2], 1)
                    for x in range(3):
                        queries(0, x)
                    with act.Fori(0, PAIRS - 1) as i:
                        steps(i)
                    steps(PAIRS - 1, last=True)

                @block.vector
                def _(v):
                    def prepare(p):
                        v.tensor_scalar(bq_now[:], bq[:, 0, bass.ds(p, 1)], 1.0, None, ALU.mult).then_inc(bq_ok, 1)

                    def keys(p, x):
                        c0, w = COLS[x]
                        v.wait_ge(proj_ok, 6 * p + x + 1)
                        v.tensor_scalar(k_t[:, c0:c0 + w], scores[:, 0, c0:c0 + w], bq[:, 1, bass.ds(p, 1)], None,
                                        ALU.add).then_inc(k_ok, 1)

                    def steps(i, last=False):
                        for j in range(STEPS):
                            if j == 3:
                                v.wait_ge(mixed_ok, T * i + 2)
                                v.tensor_scalar(vals_now[:].rearrange("p s h d -> p s (h d)"),
                                                vals[:, :, bass.ds(2 * i, 2), :].rearrange("p s h d -> p s (h d)"),
                                                1.0, None, ALU.mult).then_inc(vals_ok, 1)
                            t = turns_back(j)
                            if t is not None:
                                m = T * i + t
                                v.wait_ge(mixed_ok, m + 3)
                                v.wait_ge(back_ok, m + 1)
                                v.tensor_copy(mixed_t[:, t % 2], mixed[:, 0:P]).then_inc(mixed_out, 1)
                            if 1 <= j <= U:
                                k = j - 1
                                n = U * i + k
                                at = slice(k % 2, k % 2 + 1)
                                v.wait_ge(scores_ok, n + 1)
                                v.tensor_reduce(top[:, at], scores[0:P, k % 2, 0:NODES], AX.X, ALU.max).then_inc(max_ok, 1)
                                v.wait_ge(max_ok, n + 1)
                                v.wait_ge(probs_ok, n + 1)
                                v.tensor_scalar(shift[:, at], top[:, at], -S, None, ALU.mult).then_inc(shift_ok, 1)
                            k = turning(j)
                            if k is not None:
                                s0, m = QUADS[1]
                                v.wait_ge(mixed_ok, T * i + k // 2 + 1)
                                v.wait_ge(turned_ok[1], U * i + k + 1)
                                v.tensor_copy(probs_t[:, k % 4, s0:s0 + m],
                                              turned[0:P, 0:P * m].rearrange("p (s d) -> p s d", s=m)).then_inc(copied[1], 1)
                            if not last and j == U - 1:
                                v.wait_ge(q_ok, 6 * i + 6)
                                prepare(i + 1)
                            if not last and U <= j < U + 3:
                                keys(i + 1, j - U)
                            t = turns_back(j)
                            if t is not None:
                                m = T * i + t
                                k = (2 * t) % KEPT
                                v.reciprocal(share[:, t % 2], total[:, k:k + 2]).then_inc(share_ok, 1)
                                v.wait_ge(share_ok, m + 1)
                                v.wait_ge(back_ok, m + 3)
                                for h in range(2):
                                    ins = v.tensor_scalar(keep.o[:, t, bass.ds(HD * (2 * i + h), HD)], turned[0:P, HD * h:HD * h + HD],
                                                          share[:, t % 2, h:h + 1], None, ALU.mult)
                                ins.then_inc(back_out, 1)

                    v.sem_inc(copied[1], 1)
                    v.sem_inc(mixed_out, 1)
                    v.sem_inc(back_out, 1)
                    v.wait_ge(bqk_in, 32)
                    prepare(0)
                    for x in range(3):
                        keys(0, x)
                    with v.Fori(0, PAIRS - 1) as i:
                        steps(i)
                    steps(PAIRS - 1, last=True)


def load_w1(b, keep, sp, e, half):
    sp.dma_start(keep.w1[:, half], b.a["L0_ffn_W1"][bass.ds(e, 1)].rearrange("a (c p) f -> p (a c) f", p=128)
                 ).then_inc(keep.w1_in[half], 16)


def routing(b, keep):
    nc, a = b.nc, b.a
    with ExitStack() as ctx:
        o_t = b.sb(ctx, "o_t", [128, C, NODES])
        t_t = b.sb(ctx, "t_t", [128, C, NODES])
        w_o = b.sb(ctx, "w_o", [128, C, D])
        rows = b.sb(ctx, "route_rows", [P, 3, D])
        gate_w = b.sb(ctx, "gate_w", [128, C, EXPERTS])
        gate_b = b.sb(ctx, "gate_b", [P, EXPERTS])
        earlier = b.sb(ctx, "earlier", [P, P])
        expert_no = b.sb(ctx, "expert_no", [P, EXPERTS])
        slot_no = b.sb(ctx, "slot_no", [1, SLOTS + 1])
        J = -(-NODES // SLOT)
        slot_steps = b.sb(ctx, "slot_steps", [128, J])
        stats = b.sb(ctx, "route_stats", [P, T, 6])
        mv = b.sb(ctx, "route_mv", [P, T, 2])
        var = b.sb(ctx, "route_var", [P, T])
        rstd = b.sb(ctx, "route_rstd", [P, T])
        logits = b.sb(ctx, "logits", [P, T, EXPERTS])
        best = b.sb(ctx, "best", [P, T])
        exps = b.sb(ctx, "exps", [P, T, EXPERTS])
        chosen = b.sb(ctx, "chosen", [P, T, EXPERTS])
        before = b.sb(ctx, "before", [P, T + 1, EXPERTS])
        place = b.sb(ctx, "place_f", [P, T])
        placed = b.sb(ctx, "placed", [P, T, EXPERTS])
        counts = b.sb(ctx, "expert_counts", [128, EXPERTS])
        over = b.sb(ctx, "over", [128, EXPERTS, J])
        n_slots = b.sb(ctx, "n_slots", [128, EXPERTS])
        ends = b.sb(ctx, "slot_ends", [128, EXPERTS])
        base = b.sb(ctx, "slot_base", [128, EXPERTS])
        passed = b.sb(ctx, "passed", [1, SLOTS + 1, EXPERTS])
        tables = b.sb(ctx, "slot_tables", [1, 4, SLOTS + 1])
        banks = Banks(b, ctx, "route_banks")
        w_in = b.sem(ctx, "route_w_in")
        const_ok = b.sem(ctx, "route_const_ok")
        o_t_ok = b.sem(ctx, "o_t_ok")
        var_ok, rstd_ok, roots = b.roots(T)
        t_ok = b.sem(ctx, "t_ok")
        shifted_ok = b.sem(ctx, "shifted_ok")
        exps_ok = b.sem(ctx, "exps_ok")
        chosen_ok = b.sem(ctx, "chosen_ok")
        place_ok = b.sem(ctx, "place_ok")
        sent = b.sem(ctx, "tokens_sent")
        N = C * len(QUADS)
        PROJ, TURN, GATE, RANK = N, N + T, 2 * N + T, 2 * N + T + 1
        with nc.Block() as block:

            @block.sync
            def _(sp):
                sp.dma_start(w_o[:], a["L0_ffn_Wo"].rearrange("(c p) n -> p c n", p=128)).then_inc(w_in, 16)
                for k, n in enumerate(("bo", "ln1_g", "ln1_b")):
                    sp.dma_start(rows[:, k], a["L0_ffn_" + n].unsqueeze(0).to_broadcast([P, D])).then_inc(w_in, 16)
                sp.dma_start(gate_w[:], a["L0_ffn_gate_W"].rearrange("(c p) n -> p c n", p=128)).then_inc(w_in, 16)
                sp.dma_start(gate_b[:], a["L0_ffn_gate_b"].unsqueeze(0).to_broadcast([P, EXPERTS])).then_inc(w_in, 16)
                sp.dma_start(keep.b1_rows[:], a["L0_ffn_b1"].rearrange("e (f p) -> (e f) p", p=128)).then_inc(keep.b1_in, 16)
                sp.sem_inc(keep.w1_in[1], 16)
                for e in range(2):
                    load_w1(b, keep, sp, e, e)

            @block.gpsimd
            def _(pool):
                iota = dict(base=0, channel_multiplier=0, allow_small_or_imprecise_dtypes=True)
                pool.iota(expert_no[:], [[1, EXPERTS]], **iota).then_inc(const_ok, 1)
                pool.iota(slot_no[:], [[1, SLOTS + 1]], **iota).then_inc(const_ok, 1)
                pool.iota(slot_steps[:], [[SLOT, J]], **iota).then_inc(const_ok, 1)
                pool.memset(earlier[:], 1.0).then_inc(const_ok, 1)
                pool.wait_ge(const_ok, 4)
                pool.affine_select(out=earlier[:], in_=earlier[:], compare_op=ALU.is_gt, fill=0.0, base=0,
                                   pattern=[[1, P]], channel_multiplier=-1).then_inc(const_ok, 1)
                for t in range(T):
                    pool.wait_ge(var_ok, roots + t + 1)
                    variance_root(pool, rstd[:, t:t + 1], var[:, t:t + 1], keep.minus_half[0:P, 0:1]).then_inc(rstd_ok, 1)
                pool.wait_ge(place_ok, 1)
                for t in range(T):
                    pool.indirect_dma_start(out=keep.slots_in, out_offset=bass.IndirectOffsetOnAxis(ap=keep.place[:, t:t + 1], axis=0),
                                            in_=keep.y[:, t], in_offset=None).then_inc(sent, 16)
                pool.wait_ge(sent, 16 * T)

            @block.tensor
            def _(pe):
                turn_rows(pe, banks, 0, keep.o, keep.ident)
                pe.wait_ge(w_in, 96)
                pe.wait_ge(o_t_ok, 1)
                for t in range(T):
                    j = PROJ + t
                    banks.wait_free(pe, j)
                    for c in range(C):
                        ins = pe.matmul(banks[j][0:P, :], o_t[:, c, P * t:P * t + P], w_o[:, c], start=(c == 0), stop=(c == C - 1))
                    banks.filled(ins, j)
                pe.wait_ge(t_ok, T)
                turn_rows(pe, banks, TURN, keep.y, keep.ident)
                pe.wait_ge(o_t_ok, 2)
                banks.wait_free(pe, GATE)
                for t in range(T):
                    for c in range(C):
                        ins = pe.matmul(banks[GATE][0:P, EXPERTS * t:EXPERTS * t + EXPERTS], t_t[:, c, P * t:P * t + P],
                                        gate_w[:, c], start=(c == 0), stop=(c == C - 1))
                banks.filled(ins, GATE)
                pe.wait_ge(chosen_ok, 1)
                pe.wait_ge(const_ok, 5)
                banks.wait_free(pe, RANK)
                flat = "p t e -> p (t e)"
                pe.matmul(banks[RANK][0:P, 0:T * EXPERTS], earlier[:], chosen[:].rearrange(flat), start=True, stop=False)
                ins = pe.matmul(banks[RANK][0:P, 0:T * EXPERTS], keep.ones[0:P, 0:P], before[:, 0:T].rearrange(flat),
                                start=False, stop=True)
                banks.filled(ins, RANK)
                banks.wait_free(pe, RANK + 1)
                ins = pe.matmul(banks[RANK + 1][:, 0:EXPERTS], keep.ones[0:P, :], before[:, T], start=True, stop=True)
                banks.filled(ins, RANK + 1)

            @block.scalar
            def _(act):
                turned_out(act, banks, 0, o_t)
                for j in range(N - BANKS, N):
                    banks.wait_emptied(act, j)
                act.sem_inc(o_t_ok, 1)
                turned_out(act, banks, TURN, t_t)
                for j in range(TURN + N - BANKS, TURN + N):
                    banks.wait_emptied(act, j)
                act.sem_inc(o_t_ok, 1)
                act.wait_ge(shifted_ok, 1)
                act.activation(exps[:], exps[:], ACT.Exp).then_inc(exps_ok, 1)

            @block.vector
            def _(v):
                link = b.steps_of(v)
                v.wait_ge(w_in, 96)
                for t in range(T):
                    y = keep.y[:, t]
                    j = PROJ + t
                    banks.wait_full(v, j)
                    link(v.tensor_tensor(y, banks[j][0:P, :], y, ALU.add))
                    banks.release(v, j)
                    link(v.tensor_tensor(y, y, rows[:, 0], ALU.add))
                    link(v.bn_stats(stats[:, t], y))
                    link(v.bn_aggr(mv[:, t], stats[:, t]))
                    v.tensor_scalar(var[:, t:t + 1], mv[:, t, 1:2], EPS, None, ALU.add).then_inc(var_ok, 1)
                    v.wait_ge(rstd_ok, roots + t + 1)
                    link(v.tensor_scalar(y, y, mv[:, t, 0:1], rstd[:, t:t + 1], ALU.subtract, ALU.mult))
                    link(v.tensor_tensor(y, y, rows[:, 1], ALU.mult))
                    v.tensor_tensor(y, y, rows[:, 2], ALU.add).then_inc(t_ok, 1)
                wide = [P, T, EXPERTS]
                banks.wait_full(v, GATE)
                link(v.tensor_tensor(logits[:], banks[GATE][0:P, 0:T * EXPERTS].rearrange("p (t e) -> p t e", t=T),
                                     gate_b[:].unsqueeze(1).to_broadcast(wide), ALU.add))
                banks.release(v, GATE)
                link(v.tensor_reduce(best[:], logits[:], AX.X, ALU.max))
                v.tensor_tensor(exps[:], logits[:], best[:].unsqueeze(2).to_broadcast(wide), ALU.subtract).then_inc(shifted_ok, 1)
                link(v.tensor_tensor(chosen[:], logits[:], best[:].unsqueeze(2).to_broadcast(wide), ALU.is_equal))
                v.wait_ge(const_ok, 5)
                link(v.scalar_tensor_tensor(chosen[:], chosen[:], -float(EXPERTS), expert_no[:].unsqueeze(1).to_broadcast(wide),
                                            ALU.mult, ALU.add))
                link(v.tensor_reduce(best[:], chosen[:], AX.X, ALU.min))
                link(v.tensor_scalar(best[:], best[:], float(EXPERTS), None, ALU.add))
                link(v.tensor_tensor(chosen[:], expert_no[:].unsqueeze(1).to_broadcast(wide),
                                     best[:].unsqueeze(2).to_broadcast(wide), ALU.is_equal))
                link(v.memset(before[:, 0], 0.0))
                for t in range(T - 1):
                    link(v.tensor_tensor(before[:, t + 1], before[:, t], chosen[:, t], ALU.add))
                v.tensor_tensor(before[:, T], before[:, T - 1], chosen[:, T - 1], ALU.add).then_inc(chosen_ok, 1)
                v.wait_ge(exps_ok, 1)
                link(v.tensor_reduce(keep.gate[:], exps[:], AX.X, ALU.add))
                link(v.reciprocal(keep.gate[:], keep.gate[:]))
                banks.wait_full(v, RANK + 1)
                link(v.tensor_copy(counts[:], banks[RANK + 1][:, 0:EXPERTS]))
                link(v.tensor_tensor(over[:], counts[:].unsqueeze(2).to_broadcast([128, EXPERTS, J]),
                                     slot_steps[:].unsqueeze(1).to_broadcast([128, EXPERTS, J]), ALU.is_gt))
                link(v.tensor_reduce(n_slots[:], over[:], AX.X, ALU.add))
                link(v.tensor_tensor_scan(ends[:], keep.ones[:, 0:EXPERTS], n_slots[:], 0.0, ALU.mult, ALU.add))
                link(v.tensor_tensor(base[:], ends[:], n_slots[:], ALU.subtract))
                link(v.tensor_scalar(base[:], base[:], float(SLOT), None, ALU.mult))
                link(v.tensor_tensor(placed[:], banks[RANK][0:P, 0:T * EXPERTS].rearrange("p (t e) -> p t e", t=T),
                                     base[0:P].unsqueeze(1).to_broadcast(wide), ALU.add))
                link(v.tensor_tensor(placed[:], placed[:], chosen[:], ALU.mult))
                link(v.tensor_reduce(place[:], placed[:], AX.X, ALU.add))
                v.tensor_copy(keep.place[:], place[:]).then_inc(place_ok, 1)
                link(v.tensor_tensor(passed[:], slot_no[:].unsqueeze(2).to_broadcast([1, SLOTS + 1, EXPERTS]),
                                     ends[0:1].unsqueeze(1).to_broadcast([1, SLOTS + 1, EXPERTS]), ALU.is_ge))
                evens = passed[:, :, 1:7:2]
                odds = passed[:, :, 0:7:2]
                link(v.tensor_reduce(tables[:, 0], evens, AX.X, ALU.add))
                link(v.tensor_reduce(tables[:, 1], odds, AX.X, ALU.add))
                link(v.tensor_scalar(tables[:, 0], tables[:, 0], 1.0, None, ALU.add))
                link(v.tensor_tensor(tables[:, 2], tables[:, 1], tables[:, 0], ALU.subtract))
                link(v.tensor_scalar(tables[:, 2], tables[:, 2], 1.0, None, ALU.add))
                link(v.tensor_reduce(tables[:, 3], passed[:, :, 0:EXPERTS - 1], AX.X, ALU.add))
                link(v.tensor_copy(keep.slot_tables[:], tables[:]))
                link(v.tensor_copy(keep.slot_ends[:], ends[0:1]))


def experts(b, keep):
    nc, a = b.nc, b.a
    FB = FF // 128
    with ExitStack() as ctx:
        w1, w1_in, b1_rows, b1_in = keep.w1, keep.w1_in, keep.b1_rows, keep.b1_in
        w2 = b.sb(ctx, "w2", [128, 2, FB, D])
        b1 = b.sb(ctx, "b1", [128, EXPERTS, FB])
        b1_now = b.sb(ctx, "b1_now", [128, FB])

        def cut(free, *sizes):
            ends = [sum(sizes[:i + 1]) for i in range(len(sizes))]
            return [free[:, end - size:end] for end, size in zip(ends, sizes)]

        hid, rows_t, *rest = cut(keep.y_all, FF, D, *[D] * 4)
        rows_t = rows_t.rearrange("p (c n) -> p c n", c=C)
        rows, done = rest[:2], rest[2:]
        hid_t, b2 = cut(keep.o_all, FB * SLOT, 2 * D)
        hid_t = hid_t.rearrange("p (f n) -> p f n", f=FB)
        b2 = b2.rearrange("p (a d) -> p a d", a=2)
        up = b.ps(ctx, "up", [128, 2, 512])
        turned = b.ps(ctx, "hid_turned", [128, 4, 512])
        down = b.ps(ctx, "down", [128, 512])
        x_turned = b.ps(ctx, "x_turned", [128, 512])
        b1_turned = b.sem(ctx, "b1_turned")
        b1_ok = b.sem(ctx, "b1_ok")
        b1_now_ok = b.sem(ctx, "b1_now_ok")
        rows_in = [b.sem(ctx, f"rows_in{u}") for u in range(2)]
        w2_in = [b.sem(ctx, f"w2_in{u}") for u in range(2)]
        x_turned_ok = b.sem(ctx, "x_turned_ok")
        rows_t_ok = b.sem(ctx, "rows_t_ok")
        up_ok = b.sem(ctx, "up_ok")
        hid_ok = b.sem(ctx, "hid_ok")
        turned_ok = b.sem(ctx, "hid_turned_ok")
        gelu_ok = b.sem(ctx, "gelu_ok")
        down_ok = b.sem(ctx, "down_ok")
        done_ok = b.sem(ctx, "done_ok")
        done_out = [b.sem(ctx, f"done_out{u}") for u in range(2)]
        slots_in = keep.slots_in.rearrange("(s p) d -> s p d", p=SLOT)
        slots_out = keep.slots_out.rearrange("(s p) d -> s p d", p=SLOT)

        def table(eng, row, k):
            return eng.value_load(keep.slot_tables[0:1, row, bass.ds(k, 1)], min_val=0, max_val=(4, 4, 1, EXPERTS - 1)[row])

        with nc.Block() as block:

            @block.sync
            def _(sp):
                def load_w2(e, u):
                    sp.dma_start(w2[:, u], a["L0_ffn_W2"][bass.ds(e, 1)].rearrange("a (f p) d -> p (a f) d", p=128)).then_inc(w2_in[u], 16)
                    sp.dma_start(b2[:, u], a["L0_ffn_b2"][bass.ds(e, 1)].to_broadcast([128, D])).then_inc(w2_in[u], 16)

                sp.sem_inc(w2_in[1], 32)
                for u in range(2):
                    sp.wait_ge(rows_in[u], 16)
                load_w2(0, 0)
                load_w2(1, 1)
                with sp.Fori(1, EXPERTS // 2) as i:
                    for u in range(2):
                        end = sp.value_load(keep.slot_ends[0:1, bass.ds(2 * i + u - 2, 1)], min_val=0, max_val=SLOTS)
                        sp.wait_ge(up_ok, 4 * end + 4)
                        load_w1(b, keep, sp, 2 * i + u, u)
                        sp.wait_ge(done_ok, end + 1)
                        load_w2(2 * i + u, u)

            @block.tensor
            def _(pe):
                def turn_x(k, u, nth):
                    pe.wait_ge(rows_in[u], 16 * nth)
                    pe.wait_ge(rows_t_ok, k)
                    for c in range(C):
                        ins = pe.transpose(x_turned[:, SLOT * c:SLOT * c + SLOT], rows[u][:, 128 * c:128 * c + 128], keep.ident[:])
                    ins.then_inc(x_turned_ok, 1)

                def product_up(k):
                    even, odd, half = (table(pe, r, k) for r in range(3))
                    pe.wait_ge(w1_in[0], 16 * even)
                    pe.wait_ge(w1_in[1], 16 * odd + 16)
                    pe.wait_ge(rows_t_ok, k + 1)
                    w = w1[:, bass.ds(half, 1)].rearrange("p a c f -> p (a c) f")
                    for f in range(4):
                        if f >= 2:
                            pe.wait_ge(hid_ok, 4 * k + f - 1)
                        else:
                            pe.wait_ge(hid_ok, 4 * k)
                        for c in range(C):
                            ins = pe.matmul(up[:, f % 2], rows_t[:, c], w[:, c, 512 * f:512 * f + 512],
                                            start=(c == 0), stop=(c == C - 1))
                        ins.then_inc(up_ok, 1)

                def turn_hid(k):
                    for f in range(4):
                        pe.wait_ge(hid_ok, 4 * k + f + 1)
                        pe.wait_ge(gelu_ok, 4 * k)
                        for n in range(4):
                            ins = pe.transpose(turned[:, f, 128 * n:128 * n + 128],
                                               hid[:, 512 * f + 128 * n:512 * f + 128 * n + 128], keep.ident[:])
                        ins.then_inc(turned_ok, 1)

                def product_down(k):
                    even, odd, half = (table(pe, r, k) for r in range(3))
                    pe.wait_ge(w2_in[0], 32 * even)
                    pe.wait_ge(w2_in[1], 32 * odd + 32)
                    pe.wait_ge(gelu_ok, 4 * k + 4)
                    pe.wait_ge(done_ok, k + 1)
                    pe.wait_ge(b1_ok, 1)
                    w = w2[:, bass.ds(half, 1)].rearrange("p a f d -> p (a f) d")
                    for f in range(FB):
                        ins = pe.matmul(down[:], hid_t[:, f], w[:, f], start=(f == 0), stop=(f == FB - 1))
                    ins.then_inc(down_ok, 1)

                pe.sem_inc(up_ok, 4)
                pe.sem_inc(down_ok, 1)
                pe.wait_ge(b1_in, 16)
                pe.transpose(down[:, 0:128], b1_rows[:], keep.ident[:]).then_inc(b1_turned, 1)
                turn_x(0, 0, 1)
                product_up(0)
                turn_x(1, 1, 1)
                turn_hid(0)
                with pe.Fori(0, SLOTS // 2) as i:
                    for u in range(2):
                        k = 2 * i + 1 + u
                        product_up(k)
                        turn_x(k + 1, u, i + 2)
                        product_down(k - 1)
                        turn_hid(k)
                product_down(SLOTS - 1)

            @block.scalar
            def _(act):
                def load(k, u):
                    act.wait_ge(x_turned_ok, k - 1)
                    act.dma_start(rows[u], slots_in[bass.ds(k, 1)].rearrange("a p d -> p (a d)")).then_inc(rows_in[u], 16)

                def store(k, u):
                    act.wait_ge(done_ok, k + 2)
                    act.dma_start(slots_out[bass.ds(k, 1)].rearrange("a p d -> p (a d)"), done[u]).then_inc(done_out[u], 16)

                def gelu(k):
                    act.wait_ge(b1_now_ok, k + 1)
                    for f in range(FB):
                        if f % 4 == 0:
                            act.wait_ge(turned_ok, 4 * k + f // 4 + 1)
                            act.wait_ge(down_ok, k + 1)
                        ins = act.activation(hid_t[:, f], turned[:, f // 4, 128 * (f % 4):128 * (f % 4) + 128],
                                             ACT.Gelu_apprx_tanh,
                                             bias=b1_now[:, f:f + 1])
                        if f % 4 == 3:
                            ins.then_inc(gelu_ok, 1)

                for k in range(2):
                    act.sem_inc(done_out[k], 16)
                    act.dma_start(rows[k], slots_in[k]).then_inc(rows_in[k], 16)
                load(2, 0)
                gelu(0)
                load(3, 1)
                with act.Fori(0, (SLOTS - 3) // 2) as i:
                    for u in range(2):
                        k = 2 * i + 1 + u
                        gelu(k)
                        store(k - 1, u)
                        load(k + 3, u)
                for k in range(SLOTS - 2, SLOTS):
                    gelu(k)
                    store(k - 1, (k - 1) % 2)
                store(SLOTS - 1, (SLOTS - 1) % 2)
                act.wait_ge(done_out[0], 16 * (SLOTS // 2 + 2))
                act.wait_ge(done_out[1], 16 * (SLOTS // 2 + 1))

            @block.vector
            def _(v):
                def turned_in(k):
                    v.wait_ge(x_turned_ok, k + 1)
                    v.wait_ge(up_ok, 4 * k + 4)
                    v.tensor_copy(rows_t, x_turned[:].rearrange("p (c n) -> p c n", c=C)).then_inc(rows_t_ok, 1)

                def hidden(k):
                    for f in range(4):
                        v.wait_ge(up_ok, 4 * k + f + 5)
                        v.wait_ge(turned_ok, 4 * k)
                        v.tensor_copy(hid[:, 512 * f:512 * f + 512], up[:, f % 2]).then_inc(hid_ok, 1)
                    e = table(v, 3, k)
                    v.wait_ge(gelu_ok, 4 * k)
                    v.tensor_scalar(b1_now[:], b1[:, bass.ds(e, 1)].rearrange("p a f -> p (a f)"), 1.0, None, ALU.mult
                                    ).then_inc(b1_now_ok, 1)

                def finish(k, u, nth):
                    half = table(v, 2, k)
                    v.wait_ge(down_ok, k + 2)
                    v.wait_ge(done_out[u], 16 * nth)
                    v.tensor_tensor(done[u], down[:], b2[:, bass.ds(half, 1)].rearrange("p a d -> p (a d)"), ALU.add
                                    ).then_inc(done_ok, 1)

                v.sem_inc(done_ok, 1)
                v.wait_ge(b1_turned, 1)
                v.tensor_copy(b1[:].rearrange("p e f -> p (e f)"), down[:, 0:128]).then_inc(b1_ok, 1)
                turned_in(0)
                v.wait_ge(b1_ok, 1)
                hidden(0)
                turned_in(1)
                with v.Fori(0, SLOTS // 2) as i:
                    for u in range(2):
                        k = 2 * i + 1 + u
                        hidden(k)
                        turned_in(k + 1)
                        finish(k - 1, u, i + 1)
                finish(SLOTS - 1, (SLOTS - 1) % 2, SLOTS // 2 + 1)


def gat_inputs(b, keep):
    nc, a = b.nc, b.a
    with ExitStack() as ctx:
        got = b.sb(ctx, "got", [P, T, D])
        y_t = b.sb(ctx, "y2_t", [128, C, NODES])
        w_s = b.sb(ctx, "w_s", [128, C, HEADS, HD])
        w_b = b.sb(ctx, "w_b", [P, HEADS, HD])
        a_w = b.sb(ctx, "a_w", [P, HEADS, 2, HD])
        a_b = b.sb(ctx, "a_b", [P, HEADS])
        prod = b.sb(ctx, "prod", [P, HEADS, HD])
        stats = b.sb(ctx, "gat_stats", [P, T, 6])
        mv = b.sb(ctx, "gat_mv", [P, T, 2])
        var = b.sb(ctx, "gat_var", [P, T])
        rstd = b.sb(ctx, "gat_rstd", [P, T])
        halves_t = b.sb(ctx, "halves_t", [2 * HEADS, NODES])
        banks = Banks(b, ctx, "gat_banks")
        w_in = b.sem(ctx, "gat_w_in")
        got_in = b.sem(ctx, "got_in")
        var_ok, rstd_ok, roots = b.roots(T)
        y2_ok = b.sem(ctx, "y2_ok")
        y2_t_ok = b.sem(ctx, "y2_t_ok")
        halves_ok = b.sem(ctx, "halves_ok")
        halves_t_ok = b.sem(ctx, "halves_t_ok")
        halves_out = b.sem(ctx, "halves_out")
        N = C * len(QUADS)
        with nc.Block() as block:

            @block.sync
            def _(sp):
                for c in range(C):
                    sp.dma_start(w_s[:, c], a["L1_gnn_Ws"][:, 128 * c:128 * c + 128, :].rearrange("h p e -> p h e")).then_inc(w_in, 16)
                sp.dma_start(w_b[:].rearrange("p h e -> p (h e)"),
                             a["L1_gnn_Wb"].rearrange("(a h) e -> a (h e)", a=1).to_broadcast([P, D])).then_inc(w_in, 16)
                sp.dma_start(a_w[:].rearrange("p h k e -> p (h k e)"),
                             a["L1_gnn_a_w"].rearrange("(a h) e -> a (h e)", a=1).to_broadcast([P, 2 * D])).then_inc(w_in, 16)
                sp.dma_start(a_b[:], a["L1_gnn_a_b"].unsqueeze(0).to_broadcast([P, HEADS])).then_inc(w_in, 16)
                sp.dma_start(keep.worth[:], keep.worth_rows.rearrange("(t p) n -> p t n", p=P)).then_inc(keep.worth_in, 16)
                sp.wait_ge(halves_t_ok, len(QUADS))
                sp.dma_start(keep.halves, halves_t[:]).then_inc(halves_out, 16)
                sp.wait_ge(halves_out, 16)

            @block.gpsimd
            def _(pool):
                for t in range(T):
                    pool.indirect_dma_start(out=got[:, t], out_offset=None, in_=keep.slots_out,
                                            in_offset=bass.IndirectOffsetOnAxis(ap=keep.place[:, t:t + 1], axis=0)).then_inc(got_in, 16)
                for t in range(T):
                    pool.wait_ge(var_ok, roots + t + 1)
                    variance_root(pool, rstd[:, t:t + 1], var[:, t:t + 1], keep.minus_half[0:P, 0:1]).then_inc(rstd_ok, 1)

            @block.tensor
            def _(pe):
                pe.wait_ge(y2_ok, T)
                turn_rows(pe, banks, 0, keep.y, keep.ident)
                pe.wait_ge(w_in, 16 * (C + 3))
                pe.wait_ge(y2_t_ok, 1)
                for t in range(T):
                    banks.wait_free(pe, N + t)
                    for c in range(C):
                        ins = pe.matmul(banks[N + t][0:P, :], y_t[:, c, P * t:P * t + P], w_s[:, c].rearrange("p h e -> p (h e)"),
                                        start=(c == 0), stop=(c == C - 1))
                    banks.filled(ins, N + t)
                for q, (t0, n) in enumerate(QUADS):
                    pe.wait_ge(halves_ok, t0 + n)
                    banks.wait_free(pe, N + T + q)
                    for t in range(n):
                        ins = pe.transpose(banks[N + T + q][0:2 * HEADS, P * t:P * t + P], keep.halves_p[:, t0 + t], keep.ident[0:P, 0:P])
                    banks.filled(ins, N + T + q)

            @block.scalar
            def _(act):
                turned_out(act, banks, 0, y_t)
                for j in range(N - BANKS, N):
                    banks.wait_emptied(act, j)
                act.sem_inc(y2_t_ok, 1)
                for q, (t0, n) in enumerate(QUADS):
                    banks.wait_full(act, N + T + q)
                    act.activation(halves_t[:, P * t0:P * (t0 + n)], banks[N + T + q][0:2 * HEADS, 0:P * n], ACT.Copy).then_inc(halves_t_ok, 1)

            @block.vector
            def _(v):
                link = b.steps_of(v)
                v.wait_ge(got_in, 16 * T)
                for t in range(T):
                    r = keep.res[:, t]
                    link(v.scalar_tensor_tensor(r, got[:, t], keep.gate[:, t:t + 1], r, ALU.mult, ALU.add))
                    link(v.bn_stats(stats[:, t], r))
                    link(v.bn_aggr(mv[:, t], stats[:, t]))
                    v.tensor_scalar(var[:, t:t + 1], mv[:, t, 1:2], EPS, None, ALU.add).then_inc(var_ok, 1)
                    v.wait_ge(rstd_ok, roots + t + 1)
                    v.tensor_scalar(keep.y[:, t], r, mv[:, t, 0:1], rstd[:, t:t + 1], ALU.subtract, ALU.mult).then_inc(y2_ok, 1)
                link(v.memset(keep.w[:, :, :, HD:HD + 1], 1.0))
                v.wait_ge(w_in, 16 * (C + 3))
                for t in range(T):
                    w = keep.w[:, t, :, 0:HD]
                    banks.wait_full(v, N + t)
                    link(v.tensor_tensor(w, banks[N + t][0:P, :].rearrange("p (h e) -> p h e", h=HEADS), w_b[:], ALU.add))
                    banks.release(v, N + t)
                    for k in range(2):
                        link(v.tensor_tensor(prod[:], w, a_w[:, :, k], ALU.mult))
                        link(v.tensor_reduce(keep.halves_p[:, t, HEADS * k:HEADS * k + HEADS], prod[:], AX.X, ALU.add))
                    v.tensor_tensor(keep.halves_p[:, t, 0:HEADS], keep.halves_p[:, t, 0:HEADS], a_b[:], ALU.add).then_inc(halves_ok, 1)


def gat_max(b, keep):
    nc = b.nc
    with ExitStack() as ctx:
        src = b.sb(ctx, "src_halves", [P, HEADS, NODES])
        absent = b.sb(ctx, "absent_tiles", [P, 2, NODES], BF16)
        masked = b.sb(ctx, "masked", [P, 2, NODES])
        top = b.sb(ctx, "gat_top", [P, T, HEADS])
        low = b.sb(ctx, "gat_low", [P, T, HEADS])
        shifts = b.sb(ctx, "shifts", [P, T, 2, HEADS])
        shifts_t = b.sb(ctx, "shifts_t", [2 * HEADS, NODES])
        banks = Banks(b, ctx, "max_banks", 3)
        src_in = [b.sem(ctx, f"src_in{h}") for h in range(HEADS)]
        absent_in = [b.sem(ctx, f"absent_in{u}") for u in range(2)]
        top_ok = b.sem(ctx, "top_ok")
        shifts_ok = b.sem(ctx, "shifts_ok")
        shifts_t_ok = b.sem(ctx, "shifts_t_ok")
        shifts_out = b.sem(ctx, "shifts_out")
        with nc.Block() as block:

            @block.sync
            def _(sp):
                sp.dma_start(absent[:, 0], keep.absent[0:P, :]).then_inc(absent_in[0], 16)
                for h in range(HEADS):
                    sp.dma_start(src[:, h], keep.halves[HEADS + h:HEADS + h + 1, :].to_broadcast([P, NODES])).then_inc(src_in[h], 16)
                for t in range(1, T):
                    if t >= 2:
                        sp.wait_ge(top_ok, HEADS * (t - 1))
                    sp.dma_start(absent[:, t % 2], keep.absent[P * t:P * t + P, :]).then_inc(absent_in[t % 2], 16)
                sp.wait_ge(shifts_t_ok, len(QUADS))
                sp.dma_start(keep.shifts, shifts_t[:]).then_inc(shifts_out, 16)
                sp.wait_ge(shifts_out, 16)
                sp.wait_ge(keep.worth_in, 16)

            @block.tensor
            def _(pe):
                pe.wait_ge(shifts_ok, 1)
                for q, (t0, n) in enumerate(QUADS):
                    for t in range(n):
                        ins = pe.transpose(banks[q][0:2 * HEADS, P * t:P * t + P],
                                           shifts[:, t0 + t].rearrange("p k h -> p (k h)"), keep.ident[0:P, 0:P])
                    banks.filled(ins, q)

            @block.scalar
            def _(act):
                for q, (t0, n) in enumerate(QUADS):
                    banks.wait_full(act, q)
                    act.activation(shifts_t[:, P * t0:P * (t0 + n)], banks[q][0:2 * HEADS, 0:P * n], ACT.Copy).then_inc(shifts_t_ok, 1)

            @block.vector
            def _(v):
                link = b.steps_of(v)
                for t in range(T):
                    v.wait_ge(absent_in[t % 2], 16 * (t // 2 + 1))
                    for h in range(HEADS):
                        if t == 0:
                            v.wait_ge(src_in[h], 16)
                        if HEADS * t + h >= 2:
                            v.wait_ge(top_ok, HEADS * t + h - 1)
                        v.tensor_tensor_reduce(out=masked[:, h % 2], in0=absent[:, t % 2], in1=src[:, h], scale=1.0, scalar=LOWEST,
                                               op0=ALU.add, op1=ALU.max, accum_out=top[:, t, h:h + 1]).then_inc(top_ok, 1)
                v.wait_ge(top_ok, T * HEADS)
                own = keep.halves_p[:, :, 0:HEADS]
                link(v.tensor_tensor(top[:], top[:], own, ALU.add))
                link(v.scalar_tensor_tensor(top[:], top[:], SLOPE, top[:], ALU.mult, ALU.max))
                link(v.tensor_tensor(shifts[:, :, 0], top[:], own, ALU.subtract))
                link(v.scalar_tensor_tensor(shifts[:, :, 1], own, -SLOPE, top[:], ALU.mult, ALU.add))
                v.tensor_scalar(keep.minus_src[:, :, 0], keep.halves_p[:, :, HEADS:2 * HEADS], -1.0, None, ALU.mult)
                v.tensor_scalar(keep.minus_src[:, :, 1], keep.halves_p[:, :, HEADS:2 * HEADS], -SLOPE, None, ALU.mult)
                v.sem_inc(shifts_ok, 1)


def gat(b, keep):
    nc = b.nc
    HALF = T // 2
    WIDE = HD + 1
    RING = 5
    AHEAD = 3
    LATE = 7
    U = 2 * T
    TURNS = HEADS // 2
    with ExitStack() as ctx:
        rows = b.sb(ctx, "shift_rows", [P, 2, 2, NODES])
        far = b.sb(ctx, "far", [P, RING, NODES])
        weight = b.sb(ctx, "weight", [P, 2, NODES])
        share = b.sb(ctx, "gat_share", [P, T])
        mean = b.sb(ctx, "gat_mean", [P, T, HD])
        minus_now = b.sb(ctx, "minus_now", [P, 2, T, 2])
        w_now = b.sb(ctx, "w_now", [P, 2, T, WIDE])
        sums_t = b.sb(ctx, "sums_t", [WIDE, NODES])
        sums = b.ps(ctx, "gat_sums", [128, 2, 3 * 512])
        back = b.ps(ctx, "sums_back", [128, 2, 512])
        w_now_ok = b.sem(ctx, "w_now_ok")
        sums_out = b.sem(ctx, "sums_out")
        back_ok = b.sem(ctx, "sums_back_ok")
        rows_in = [b.sem(ctx, f"shift_rows_in{u}") for u in range(2)]
        minus_ok = b.sem(ctx, "minus_ok")
        far_ok = b.sem(ctx, "far_ok")
        near_ok = b.sem(ctx, "near_ok2")
        worthy_ok = b.sem(ctx, "worthy_ok")
        weight_ok = b.sem(ctx, "weight_ok")
        summed = b.sem(ctx, "gat_summed")
        head_ok = b.sem(ctx, "head_ok")
        step = b.sem(ctx, "gat_v_step")

        with nc.Block() as block:

            @block.sync
            def _(sp):
                def load(h, u):
                    for k in range(2):
                        sp.dma_start(rows[:, u, k], keep.shifts[bass.ds(HEADS * k + h, 1), :].to_broadcast([P, NODES])).then_inc(rows_in[u], 16)

                load(0, 0)
                load(1, 1)
                w = b.a["L1_ffn_W"]
                sp.dma_start(keep.m_rows[:], w[:, 0:128, :].rearrange("l e d -> e l d")).then_inc(keep.m_in, 16)
                sp.dma_start(keep.m_rows_hi[:], w[:, 128:, :].rearrange("l e d -> e l d")).then_inc(keep.m_in, 16)
                with sp.Fori(1, TURNS) as i:
                    for u in range(2):
                        sp.wait_ge(near_ok, U * i + T * (u - 1))
                        load(2 * i + u, u)

            @block.scalar
            def _(act):
                def line(i, j):
                    u, s = divmod(j, T)
                    if s == 0:
                        act.wait_ge(rows_in[u], 32 * i + 32)
                        act.wait_ge(minus_ok, 2 * i + u + 1)
                    act.activation(far[:, j % RING], rows[:, u, 1], ACT.Identity, bias=minus_now[:, u, s, 1:2]).then_inc(far_ok, 1)

                def values(h, u):
                    act.activation(w_now[:, u], keep.w[:, :, bass.ds(h, 1), :].rearrange("p t a e -> p t (a e)"), ACT.Copy
                                   ).then_inc(w_now_ok, 1)

                def take(i, u):
                    h = 2 * i + u
                    act.wait_ge(summed, 2 + T * h + T)
                    act.wait_ge(back_ok, h + 1)
                    act.activation(sums_t[:], sums[0:WIDE, u, 0:NODES], ACT.Copy).then_inc(sums_out, 1)

                def weights(i, steps):
                    for j in steps:
                        n = U * i + j
                        if n_left(i, j) > AHEAD:
                            act.wait_ge(weight_ok, n + AHEAD - RING + 3)
                            ahead, j_ahead = divmod(j + AHEAD, U)
                            line(i + ahead, j_ahead)
                        act.wait_ge(worthy_ok, n + 1)
                        act.wait_ge(summed, n + 1)
                        act.activation(weight[:, j % 2], far[:, j % RING], ACT.Exp, scale=-1.0).then_inc(weight_ok, 1)
                        if j in (T + 2, U + 2):
                            u = j // T - 1
                            take(i, u)
                            if n_left(i, j) > T:
                                values(2 * i + 2 + u, u)

                def n_left(i, j):
                    return U * (TURNS - i) - j if isinstance(i, int) else U

                act.sem_inc(weight_ok, 2)
                for u in range(2):
                    values(u, u)
                for j in range(AHEAD):
                    line(0, j)
                weights(0, range(LATE))
                with act.Fori(0, TURNS - 1) as i:
                    weights(i, range(LATE, U + LATE))
                weights(TURNS - 1, range(LATE, U))
                take(TURNS - 1, 1)

            @block.tensor
            def _(pe):
                def turn_back(i, u):
                    h = 2 * i + u
                    pe.wait_ge(sums_out, h + 3)
                    pe.wait_ge(head_ok, h + 1)
                    for t in range(T):
                        ins = pe.transpose(back[0:P, t // HALF, WIDE * (t % HALF):WIDE * (t % HALF) + WIDE],
                                           sums_t[:, P * t:P * t + P], keep.ident[0:WIDE, 0:WIDE])
                    ins.then_inc(back_ok, 1)

                def products(i, steps):
                    for j in steps:
                        u, s = divmod(j % U, T)
                        n = U * i + j
                        if s == 0:
                            h = 2 * i + j // T
                            pe.wait_ge(sums_out, h + 1)
                            pe.wait_ge(w_now_ok, h + 1)
                        pe.wait_ge(weight_ok, n + 3)
                        for c0, w in COLS:
                            ins = pe.matmul(sums[0:WIDE, u, c0:c0 + w], w_now[:, u, s], weight[:, j % 2, c0:c0 + w],
                                            start=(s == 0), stop=(s == T - 1))
                        ins.then_inc(summed, 1)
                        if j in (T + 3, U + 3):
                            turn_back(i, j // T - 1)

                pe.sem_inc(summed, 2)
                pe.sem_inc(sums_out, 2)
                pe.sem_inc(back_ok, 1)
                products(0, range(LATE))
                with pe.Fori(0, TURNS - 1) as i:
                    products(i, range(LATE, U + LATE))
                products(TURNS - 1, range(LATE, U))
                turn_back(TURNS - 1, 1)

            @block.vector
            def _(v):
                def minus(h, u):
                    v.tensor_scalar(minus_now[:, u], keep.minus_src[:, :, :, bass.ds(h, 1)].rearrange("p t k a -> p t (k a)"),
                                    1.0, None, ALU.mult).then_inc(minus_ok, 1)

                def near(i, j):
                    u, s = divmod(j, T)
                    v.wait_ge(far_ok, U * i + j + 1)
                    to = far[:, j % RING]
                    v.scalar_tensor_tensor(to, rows[:, u, 0], minus_now[:, u, s, 0:1], to, ALU.add, ALU.min).then_inc(near_ok, 1)

                def unit(i, j, last=False):
                    n = U * i + j
                    if not last:
                        if j + 1 < U:
                            near(i, j + 1)
                        else:
                            near(i + 1, j + 1 - U)
                    v.wait_ge(near_ok, n + 1)
                    to = far[:, j % RING]
                    v.tensor_tensor(to, to, keep.worth[:, j % T], ALU.add).then_inc(worthy_ok, 1)

                def finish(i, u, link):
                    h = 2 * i + u
                    v.wait_ge(back_ok, h + 2)
                    for k in range(2):
                        part = back[0:P, k, 0:WIDE * HALF].rearrange("p (t e) -> p t e", t=HALF)
                        link(v.tensor_scalar(share[:, HALF * k:HALF * k + HALF], part[:, :, HD], 1e-30, None, ALU.max))
                    link(v.reciprocal(share[:], share[:]))
                    for k in range(2):
                        part = back[0:P, k, 0:WIDE * HALF].rearrange("p (t e) -> p t e", t=HALF)
                        link(v.tensor_tensor(mean[:, HALF * k:HALF * k + HALF], part[:, :, 0:HD],
                                             share[:, HALF * k:HALF * k + HALF].unsqueeze(2).to_broadcast([P, HALF, HD]), ALU.mult))
                    to = keep.res[:, :, bass.ds(HD * h, HD)]
                    link(v.tensor_tensor(to, mean[:], to, ALU.add))
                    v.sem_inc(head_ok, 1)

                def both(i, link, last=False):
                    for j in range(LATE, U if last else U + LATE):
                        if j in (T + LATE - 1, U + LATE - 1):
                            finish(i, j // T - 1, link)
                        if j == T + LATE and not last:
                            v.wait_ge(far_ok, U * i + T)
                            v.wait_ge(near_ok, U * i + T)
                            minus(2 * i + 2, 0)
                        if j == U + LATE - 1:
                            minus(2 * i + 3, 1)
                        unit(i, j, last and j == U - 1)
                    if last:
                        finish(i, 1, link)

                v.sem_inc(head_ok, 1)
                minus(0, 0)
                minus(1, 1)
                near(0, 0)
                for j in range(LATE):
                    unit(0, j)
                PER_TURN = 12
                with v.Fori(0, TURNS - 1) as i:
                    link = Steps(v, step, base=PER_TURN * i)
                    both(i, link)
                    assert link.n == PER_TURN
                both(TURNS - 1, Steps(v, step, base=PER_TURN * (TURNS - 1)), last=True)


def last_mlp(b, keep):
    nc, a = b.nc, b.a
    G = 160
    HI = G - 128
    L = 7
    MARKS, OUT0, OP = 64, 128, 29
    COLS2 = 2 * NODES
    BLOCKS = 128 // HI
    WIDE = COLS2 // BLOCKS
    PIECES = ((0, (WIDE + 1) // 2), ((WIDE + 1) // 2, WIDE // 2))
    ROUND = 1.5 * 2 ** 23
    with ExitStack() as ctx:
        w_rows, w_rows_hi = keep.m_rows, keep.m_rows_hi
        again = b.sb(ctx, "m_again", [128, L, BLOCKS, HI])
        again_hi = b.sb(ctx, "m_again_hi", [HI, L, BLOCKS, HI])
        w_t = b.sb(ctx, "m_t", [128, L, G])
        w_from_hi = b.sb(ctx, "m_from_hi", [128, L, BLOCKS, 128])
        w_hi_hi = b.sb(ctx, "m_hi_hi", [128, L, BLOCKS, HI])
        block_of = b.sb(ctx, "block_of", [128, BLOCKS])
        w_last_hi = b.sb(ctx, "m_last_hi", [128, BLOCKS])
        w_first = b.sb(ctx, "m_first", [3, G])
        w_last = b.sb(ctx, "m_last", [128, 2])
        bias = b.sb(ctx, "m_bias", [128, 2, L])
        bias_last = b.sb(ctx, "m_bias_last", [P, 1])
        marks = b.sb(ctx, "marks", [P, T, 4, 16])
        weigh = b.sb(ctx, "weigh", [P, 16])
        sixteen = b.sb(ctx, "sixteen", [P, 16])
        high = b.sb(ctx, "high", [P, T, 4])
        seen = b.sb(ctx, "seen", [P, T, 4])
        feats = b.sb(ctx, "feats", [P, T, 2, 3])
        feats_t = b.sb(ctx, "feats_t", [3, 2, NODES])
        lo = b.sb(ctx, "h_lo", [128, 2, COLS2])
        hi = b.sb(ctx, "h_hi", [128, 2, WIDE])
        asked = b.sb(ctx, "asked", [P, T, 2])
        mask = b.sb(ctx, "mask", [P, T])
        result = b.sb(ctx, "result", [P, 2, T])
        hot = b.sb(ctx, "hot", [P, T, 2, 16])
        stats = b.sb(ctx, "m_stats", [P, T, 6])
        mv = b.sb(ctx, "m_mv", [P, T, 2])
        var = b.sb(ctx, "m_var", [P, T])
        rstd = b.sb(ctx, "m_rstd", [P, T])
        banks = Banks(b, ctx, "m_banks")
        w_in = b.sem(ctx, "m_w_in")
        const_ok = b.sem(ctx, "m_const_ok")
        var_ok, rstd_ok, roots = b.roots(1)
        feats_ok = b.sem(ctx, "feats_ok")
        feats_t_ok = b.sem(ctx, "feats_t_ok")
        w_t_ok = b.sem(ctx, "m_t_ok")
        w_hi_ok = b.sem(ctx, "m_hi_ok")
        again_ok = b.sem(ctx, "again_ok")
        layer_a = b.sem(ctx, "layer_a")
        layer_v = b.sem(ctx, "layer_v")
        sum_ok = b.sem(ctx, "sum_ok")
        out_ok = b.sem(ctx, "rows_ok")
        out_sent = b.sem(ctx, "out_sent")
        W = L - 2
        F0 = 2 * W
        M0 = F0 + 2 * len(QUADS)
        LAST = M0 + (BLOCKS + 1) * len(PIECES) * (W + 1)

        def job(l, x, block):
            return M0 + (BLOCKS + 1) * (len(PIECES) * l + x) + block

        def done(l, x):
            return len(PIECES) * l + x + 1

        N_IN = 5 + 2 * BLOCKS
        with nc.Block() as stage:

            @stage.sync
            def _(sp):
                slow = dict(allow_slow_non_contiguous=True)
                w = a["L1_ffn_W"]
                sp.dma_start(w_first[0:2], w[0, :, 0:2].rearrange("e d -> d e"), **slow).then_inc(w_in, 16)
                sp.dma_start(w_first[2:3], w[0, :, 30:31].rearrange("e d -> d e"), **slow).then_inc(w_in, 16)
                sp.dma_start(w_last[:, 0:1], w[L - 1, 2, 0:128].unsqueeze(1), **slow).then_inc(w_in, 16)
                bb = a["L1_ffn_b"]
                sp.dma_start(bias[:, 0], bb[:, 0:128].rearrange("l e -> e l"), **slow).then_inc(w_in, 16)
                for block in range(BLOCKS):
                    rows = slice(HI * block, HI * block + HI)
                    sp.dma_start(w_last[rows, 1:2], w[L - 1, 2, 128:G].unsqueeze(1), **slow).then_inc(w_in, 16)
                    sp.dma_start(bias[rows, 1], bb[:, 128:G].rearrange("l e -> e l"), **slow).then_inc(w_in, 16)
                sp.dma_start(bias_last[:], bb[L - 1:L, 2:3].to_broadcast([P, 1]), **slow).then_inc(w_in, 16)
                rows_of = b.out.rearrange("(t p) d -> p t d", p=P)
                sp.wait_ge(sum_ok, 1)
                for c in (slice(0, OUT0), slice(OUT0 + 32, D)):
                    sp.dma_start(rows_of[:, :, c], keep.res[:, :, c]).then_inc(out_sent, 16)
                sp.wait_ge(out_ok, 1)
                c = slice(OUT0, OUT0 + 32)
                sp.dma_start(rows_of[:, :, c], keep.res[:, :, c]).then_inc(out_sent, 16)
                sp.wait_ge(out_sent, 48)

            @stage.gpsimd
            def _(pool):
                iota = dict(channel_multiplier=0, allow_small_or_imprecise_dtypes=True)
                pool.iota(weigh[:], [[-1, 16]], base=16, **iota).then_inc(const_ok, 1)
                pool.iota(sixteen[:], [[1, 16]], base=0, **iota).then_inc(const_ok, 1)
                pool.wait_ge(var_ok, roots + 1)
                variance_root(pool, rstd[:], var[:], keep.minus_half[0:P, 0:T]).then_inc(rstd_ok, 1)
                pool.wait_ge(feats_ok, 1)
                pool.tensor_tensor(keep.res[:], keep.res[:], keep.y, ALU.add).then_inc(sum_ok, 1)

            @stage.tensor
            def _(pe):
                pe.wait_ge(keep.m_in, 32)
                pe.wait_ge(again_ok, 1)
                for l in range(W):
                    banks.wait_free(pe, 2 * l)
                    pe.transpose(banks[2 * l][:, 0:128], w_rows[:, l + 1, 0:128], keep.ident[:])
                    ins = pe.transpose(banks[2 * l][:, 128:G], w_rows_hi[:, l + 1, 0:128], keep.ident[0:HI, 0:HI])
                    banks.filled(ins, 2 * l)
                    banks.wait_free(pe, 2 * l + 1)
                    pe.transpose(banks[2 * l + 1][:, 0:128], again[:, l + 1].rearrange("e b d -> e (b d)"), keep.ident[:])
                    ins = pe.transpose(banks[2 * l + 1][:, 128:G], again_hi[:, l + 1].rearrange("e b d -> e (b d)"),
                                       keep.ident[0:HI, 0:HI])
                    banks.filled(ins, 2 * l + 1)
                pe.wait_ge(feats_ok, 1)
                for p in range(2):
                    for q, (t0, n) in enumerate(QUADS):
                        j = F0 + 3 * p + q
                        banks.wait_free(pe, j)
                        for t in range(n):
                            ins = pe.transpose(banks[j][0:3, P * t:P * t + P], feats[:, t0 + t, p], keep.ident[0:P, 0:P])
                        banks.filled(ins, j)
                f = feats_t[:].rearrange("f p n -> f (p n)")
                pe.wait_ge(feats_t_ok, 2 * len(QUADS))
                pe.wait_ge(w_t_ok, W)
                pe.wait_ge(w_hi_ok, 2 * W + 1)
                pe.wait_ge(w_in, 16 * N_IN)
                for l in range(W + 1):
                    for x, (c0, n) in enumerate(PIECES):
                        if l:
                            pe.wait_ge(layer_a, 3 * done(l - 1, x))
                            pe.wait_ge(layer_v, 2 * done(l - 1, x))
                        h = hi[:, (l - 1) % 2, c0:c0 + n]
                        for block in range(BLOCKS):
                            c = slice(WIDE * block + c0, WIDE * block + c0 + n)
                            j = job(l, x, block)
                            banks.wait_free(pe, j)
                            to = banks[j][:, 0:n]
                            if l == 0:
                                ins = pe.matmul(to, w_first[:, 0:128], f[:, c], start=True, stop=True)
                            else:
                                pe.matmul(to, w_t[:, l, 0:128], lo[:, (l - 1) % 2, c], start=True, stop=False)
                                ins = pe.matmul(to, w_from_hi[:, l, block], h, start=False, stop=True)
                            banks.filled(ins, j)
                        j = job(l, x, BLOCKS)
                        banks.wait_free(pe, j)
                        for block in range(BLOCKS):
                            c = slice(WIDE * block + c0, WIDE * block + c0 + n)
                            to = banks[j][HI * block:HI * block + HI, 0:n]
                            if l == 0:
                                ins = pe.matmul(to, w_first[:, 128:G], f[:, c], start=True, stop=True, tile_position=(0, HI * block))
                            else:
                                pe.matmul(to, w_t[:, l, 128:G], lo[:, (l - 1) % 2, c], start=True, stop=False,
                                          tile_position=(0, HI * block), skip_group_check=True)
                        if l:
                            ins = pe.matmul(banks[j][:, 0:n], w_hi_hi[:, l].rearrange("p b e -> p (b e)"), h, start=False, stop=True,
                                            skip_group_check=True)
                        banks.filled(ins, j)
                pe.wait_ge(layer_a, 3 * done(W, 1))
                pe.wait_ge(layer_v, 2 * done(W, 1))
                banks.wait_free(pe, LAST)
                PER = 2 * T // BLOCKS
                for t in range(2 * T):
                    pe.matmul(banks[LAST][0:P, t:t + 1], lo[:, W % 2, P * t:P * t + P], w_last[:, 0:1],
                              start=(t == 0), stop=False, skip_group_check=True)
                for r in range(PER):
                    ins = pe.matmul(banks[LAST][0:P, r:2 * T:PER], hi[:, W % 2, P * r:P * r + P], w_last_hi[:],
                                    start=False, stop=True, skip_group_check=True)
                banks.filled(ins, LAST)

            @stage.scalar
            def _(act):
                for l in range(W):
                    banks.wait_full(act, 2 * l)
                    act.activation(w_t[:, l + 1], banks[2 * l][:, 0:G], ACT.Copy).then_inc(w_t_ok, 1)
                    act.wait_ge(w_t_ok, l + 1)
                    banks.release(act, 2 * l)
                for p in range(2):
                    for q, (t0, n) in enumerate(QUADS):
                        j = F0 + 3 * p + q
                        banks.wait_full(act, j)
                        act.activation(feats_t[:, p, P * t0:P * (t0 + n)], banks[j][0:3, 0:P * n], ACT.Copy).then_inc(feats_t_ok, 1)
                        act.wait_ge(feats_t_ok, 3 * p + q + 1)
                        banks.release(act, j)
                act.wait_ge(w_in, 16 * N_IN)
                for l in range(W + 1):
                    for x, (c0, n) in enumerate(PIECES):
                        for k, block in enumerate((0, 2, BLOCKS)):
                            j = job(l, x, block)
                            banks.wait_full(act, j)
                            if block < BLOCKS:
                                to = lo[:, l % 2, WIDE * block + c0:WIDE * block + c0 + n]
                            else:
                                to = hi[:, l % 2, c0:c0 + n]
                            act.activation(to, banks[j][:, 0:n], ACT.Relu, bias=bias[:, block // BLOCKS, l:l + 1]).then_inc(layer_a, 1)
                            act.wait_ge(layer_a, 3 * done(l, x) - 2 + k)
                            banks.release(act, j)

            @stage.vector
            def _(v):
                link = b.steps_of(v)
                v.wait_ge(keep.m_in, 32)
                for block in range(BLOCKS):
                    v.tensor_copy(again[:, :, block], w_rows[:, :, 128:G])
                    ins = v.tensor_copy(again_hi[:, :, block], w_rows_hi[:, :, 128:G])
                ins.then_inc(again_ok, 1)
                link(v.memset(block_of[:], 0.0))
                for block in range(BLOCKS):
                    ins = v.memset(block_of[HI * block:HI * block + HI, block:block + 1], 1.0)
                link(ins)
                for t in range(T):
                    ins = v.bn_stats(stats[:, t], keep.res[:, t])
                link(ins)
                for t in range(T):
                    ins = v.bn_aggr(mv[:, t], stats[:, t])
                link(ins)
                v.tensor_scalar(var[:], mv[:, :, 1], EPS, None, ALU.add).then_inc(var_ok, 1)
                v.wait_ge(rstd_ok, roots + 1)
                for t in range(T):
                    ins = v.tensor_scalar(keep.y[:, t], keep.res[:, t], mv[:, t, 0:1], rstd[:, t:t + 1], ALU.subtract, ALU.mult)
                link(ins)
                v.wait_ge(const_ok, 2)
                for t in range(T):
                    ins = v.scalar_tensor_tensor(marks[:, t], keep.y[:, t, MARKS:MARKS + 64].rearrange("p (m k) -> p m k", m=4), 0.5,
                                                 weigh[:].unsqueeze(1).to_broadcast([P, 4, 16]), ALU.is_gt, ALU.mult)
                link(ins)
                link(v.tensor_reduce(high[:], marks[:], AX.X, ALU.max))
                link(v.tensor_scalar(seen[:], high[:], 0.0, None, ALU.is_gt))
                link(v.tensor_scalar(high[:], high[:], -1.0, 16.0, ALU.mult, ALU.add))
                link(v.tensor_tensor(high[:], high[:], seen[:], ALU.mult))
                for p in range(2):
                    v.tensor_copy(feats[:, :, p, 0:2], high[:, :, p:4:2])
                    ins = v.tensor_copy(feats[:, :, p, 2], keep.y[:, :, OP])
                ins.then_inc(feats_ok, 1)
                for l in range(W):
                    j = 2 * l + 1
                    banks.wait_full(v, j)
                    for to, c in ((w_from_hi[:, l + 1], slice(0, 128)), (w_hi_hi[:, l + 1], slice(128, G))):
                        n = c.stop - c.start
                        v.tensor_tensor(to, banks[j][:, c].unsqueeze(1).to_broadcast([128, BLOCKS, n]),
                                        block_of[:].unsqueeze(2).to_broadcast([128, BLOCKS, n]), ALU.mult).then_inc(w_hi_ok, 1)
                    v.wait_ge(w_hi_ok, 2 * l + 2)
                    banks.release(v, j)
                v.wait_ge(w_in, 16 * N_IN)
                v.tensor_scalar(w_last_hi[:], block_of[:], w_last[:, 1:2], None, ALU.mult).then_inc(w_hi_ok, 1)
                link(v.tensor_scalar(asked[:], keep.y[:, :, 0:2], 0.5, None, ALU.is_ge))
                link(v.tensor_tensor(mask[:], asked[:, :, 0], asked[:, :, 1], ALU.mult))
                link(v.tensor_scalar(mask[:], mask[:], 2.0, None, ALU.mult))
                for l in range(W + 1):
                    for x, (c0, n) in enumerate(PIECES):
                        for k, block in enumerate((1, 3)):
                            j = job(l, x, block)
                            banks.wait_full(v, j)
                            v.tensor_scalar(lo[:, l % 2, WIDE * block + c0:WIDE * block + c0 + n], banks[j][:, 0:n],
                                            bias[:, 0, l:l + 1], 0.0, ALU.add, ALU.max).then_inc(layer_v, 1)
                            v.wait_ge(layer_v, 2 * done(l, x) - 1 + k)
                            banks.release(v, j)
                banks.wait_full(v, LAST)
                link(v.tensor_scalar(result[:].rearrange("p a t -> p (a t)"), banks[LAST][0:P, 0:2 * T], bias_last[:, 0:1], 0.0,
                                     ALU.add, ALU.max))
                link(v.tensor_scalar(result[:], result[:], 15.0, ROUND, ALU.min, ALU.add))
                link(v.tensor_scalar(result[:], result[:], ROUND, None, ALU.subtract))
                for p in range(2):
                    link(v.tensor_tensor(hot[:, :, p], sixteen[:].unsqueeze(1).to_broadcast([P, T, 16]),
                                         result[:, p].unsqueeze(2).to_broadcast([P, T, 16]), ALU.is_equal))
                flat = hot[:].rearrange("p t a k -> p t (a k)")
                link(v.tensor_tensor(flat, flat, mask[:].unsqueeze(2).to_broadcast([P, T, 32]), ALU.mult))
                to = keep.res[:, :, OUT0:OUT0 + 32]
                v.wait_ge(sum_ok, 1)
                v.tensor_tensor(to, to, flat, ALU.add).then_inc(out_ok, 1)


class Keep:
    pass


def program(nc, a, out, upto=99):
    with ExitStack() as ctx:
        b = Build(nc, a, out, ctx)
        keep = Keep()
        keep.edges = nc.dram_tensor("edge_lists", [2, EDGES + GROUP], F32).ap()
        keep.ident = b.sb(ctx, "ident", [128, 128])
        keep.ones = b.sb(ctx, "ones", [128, 128])
        keep.minus_half = b.sb(ctx, "minus_half", [128, T])
        keep.node_no = b.sb(ctx, "node_no", [128, NODES], I16)
        keep.tile_base = b.sb(ctx, "tile_base", [128, GROUPS])
        keep.group_offset = b.sb(ctx, "group_offset", [1, GROUPS], I32)
        keep.group_tile = b.sb(ctx, "group_tile", [1, GROUPS], I32)
        keep.x_in = b.sem(ctx, "x_in")
        keep.w_in = b.sem(ctx, "w_in")
        keep.y_all = b.sb(ctx, "y", [128, T * D])
        keep.y = keep.y_all[0:P].rearrange("p (t d) -> p t d", t=T)
        keep.x = keep.y
        keep.res = b.sb(ctx, "res", [P, T, D])
        keep.worth_rows = nc.dram_tensor("worth_rows", [NODES, NODES], F32).ap()
        keep.slots_in = nc.dram_tensor("slots_in", [(SLOTS + 1) * SLOT, D], F32).ap()
        keep.slots_out = nc.dram_tensor("slots_out", [SLOTS * SLOT, D], F32).ap()
        keep.place = b.sb(ctx, "place", [P, T], mybir.dt.uint32)
        keep.gate = b.sb(ctx, "gate", [P, T])
        keep.slot_tables = b.sb(ctx, "slot_tables_i", [1, 4, SLOTS + 1], I32)
        keep.slot_ends = b.sb(ctx, "slot_ends_i", [1, EXPERTS], I32)
        keep.absent = nc.dram_tensor("absent_rows", [NODES, NODES], BF16).ap()
        with ExitStack() as stage:
            keep.count = b.sb(stage, "count", [P, T + 1, NODES])
            with ExitStack() as weights:
                keep.w_rows = b.sb(weights, "w_rows", [128, 2, C, D])
                index_edges(b, keep)
                if upto > 1:
                    count_edges(b, keep)
                if upto > 2:
                    sage(b, keep)
        with ExitStack() as stage:
            keep.o_all = b.sb(stage, "o", [128, T * D])
            keep.o = keep.o_all[0:P].rearrange("p (t d) -> p t d", t=T)
            if upto > 3:
                attention(b, keep)
            keep.w1 = b.sb(stage, "w1", [128, 2, C, FF])
            keep.w1_in = [b.sem(ctx, f"w1_in{u}") for u in range(2)]
            keep.b1_rows = b.sb(stage, "b1_rows", [EXPERTS * FF // 128, 128])
            keep.b1_in = b.sem(ctx, "b1_in")
            if upto > 4:
                routing(b, keep)
            if upto > 5:
                experts(b, keep)
        keep.m_rows = b.sb(ctx, "m_rows", [128, *a["L1_ffn_W"].shape[0::2]])
        keep.m_rows_hi = b.sb(ctx, "m_rows_hi", [a["L1_ffn_W"].shape[1] - 128, *a["L1_ffn_W"].shape[0::2]])
        keep.m_in = b.sem(ctx, "m_in")
        if upto > 6:
            with ExitStack() as stage:
                keep.worth_in = b.sem(ctx, "worth_in")
                keep.halves = nc.dram_tensor("halves_rows", [2 * HEADS, NODES], F32).ap()
                keep.shifts = nc.dram_tensor("shifts_rows", [2 * HEADS, NODES], F32).ap()
                keep.w = b.sb(stage, "w", [P, T, HEADS, HD + 1])
                keep.halves_p = b.sb(stage, "halves", [P, T, 2 * HEADS])
                keep.minus_src = b.sb(stage, "minus_src", [P, T, 2, HEADS])
                keep.worth = b.sb(stage, "worth", [P, T, NODES])
                gat_inputs(b, keep)
                if upto > 7:
                    gat_max(b, keep)
                    gat(b, keep)
        if upto > 8:
            last_mlp(b, keep)


def kernel(**inputs):
    import numpy as np
    import concourse.bacc as bacc
    from concourse.bass_utils import run_bass_kernel_spmd

    nc = bacc.Bacc("TRN2", target_bir_lowering=False, num_devices=1)
    arrays, args = {}, {}
    for name, value in inputs.items():
        arrays[f"in_{name}"] = value = np.ascontiguousarray(value)
        args[name] = nc.dram_tensor(f"in_{name}", value.shape, mybir.dt.from_np(value.dtype), kind="ExternalInput").ap()
    out = nc.dram_tensor("out", [NODES, D], F32, kind="ExternalOutput").ap()
    program(nc, args, out)
    return run_bass_kernel_spmd(nc, [arrays], core_ids=[0]).results[0]["out"]
```

```python
from contextlib import ExitStack

import concourse.bass as bass
from concourse import mybir

ALU = mybir.AluOpType
ACT = mybir.ActivationFunctionType
AX = mybir.AxisListType
F32 = mybir.dt.float32
BF16 = mybir.dt.bfloat16
I32 = mybir.dt.int32
I16 = mybir.dt.int16

NODES = 1250
EDGES = 20000
D = 512
P = 125
T = NODES // P
C = D // 128
EPS = 1e-5

CHUNKS = 6
RING = 2 * CHUNKS
GROUP = 128 * CHUNKS
GROUPS = -(-((EDGES + T * (GROUP - 1)) // GROUP) // 2) * 2
NOWHERE = 5000.0
EXPERTS = 8
FF = 4 * D
HEADS = 8
HD = D // HEADS
SLOPE = 0.2
LOWEST = -1e20
NEVER = 1e30
SLOT = 128
SLOTS = (NODES + EXPERTS * (SLOT - 1)) // SLOT
BANKS = 8
QUADS = [(0, 4), (4, 4), (8, 2)]
COLS = [(0, 512), (512, 512), (1024, 226)]


class Steps:

    def __init__(self, eng, sem, base=0):
        self.eng, self.sem, self.base, self.n = eng, sem, base, 0

    def __call__(self, ins):
        self.n += 1
        ins.then_inc(self.sem, 1)
        self.eng.wait_ge(self.sem, self.base + self.n)


class Build:
    def __init__(self, nc, a, out, ctx):
        self.nc, self.a, self.out, self.ctx = nc, a, out, ctx
        self.full = [self.sem(ctx, f"bank_full{i}") for i in range(BANKS)]
        self.free = [self.sem(ctx, f"bank_free{i}") for i in range(BANKS)]
        self.filled, self.emptied = [0] * BANKS, [0] * BANKS
        self.var_ok, self.rstd_ok, self.rooted = self.sem(ctx, "var_ok"), self.sem(ctx, "rstd_ok"), 0
        self.v_steps = Steps(None, self.sem(ctx, "vector_steps"))

    def steps_of(self, v):
        self.v_steps.eng = v
        return self.v_steps

    def roots(self, n):
        before, self.rooted = self.rooted, self.rooted + n
        return self.var_ok, self.rstd_ok, before

    def sb(self, ctx, name, shape, dt=F32):
        return ctx.enter_context(self.nc.sbuf_tensor(name, shape, dt))

    def ps(self, ctx, name, shape, dt=F32):
        return ctx.enter_context(self.nc.psum_tensor(name, shape, dt))

    def sem(self, ctx, name):
        return self.ctx.enter_context(self.nc.semaphore(name))


def index_edges(b, keep):
    nc, a = b.nc, b.a
    with ExitStack() as ctx:
        src_i = b.sb(ctx, "src_i", [P, EDGES // P], I32)
        dst_i = b.sb(ctx, "dst_i", [P, EDGES // P], I32)
        src_f = b.sb(ctx, "src_f", [P, EDGES // P])
        dst_f = b.sb(ctx, "dst_f", [P, EDGES // P])
        pad = b.sb(ctx, "pad", [2, GROUP])
        bounds = b.sb(ctx, "bounds", [P, T])
        below = b.sb(ctx, "below", [P, T, EDGES // P])
        part = b.sb(ctx, "part", [P, T])
        J = -(-EDGES // GROUP)
        steps_j = b.sb(ctx, "steps_j", [128, J])
        group_no = b.sb(ctx, "group_no", [128, GROUPS])
        more = b.sb(ctx, "more", [128, T, J])
        lo = b.sb(ctx, "lo", [128, T + 1])
        length = b.sb(ctx, "length", [128, T])
        n_groups = b.sb(ctx, "n_groups", [128, T])
        ends = b.sb(ctx, "ends", [128, T + 1])
        first = b.sb(ctx, "first", [128, T])
        past = b.sb(ctx, "past", [128, GROUPS, T])
        tile_of = b.sb(ctx, "tile_of", [128, GROUPS])
        shift = b.sb(ctx, "shift", [128, GROUPS])
        offset = b.sb(ctx, "offset", [128, GROUPS])
        counts = b.ps(ctx, "counts", [128, T])
        edges_in = b.sem(ctx, "edges_in")
        const_ok = b.sem(ctx, "const_ok")
        ident_ok = b.sem(ctx, "ident_ok")
        lists_ok = b.sem(ctx, "lists_ok")
        zeros_ok = b.sem(ctx, "zeros_ok")
        lists_out = b.sem(ctx, "lists_out")
        parts_ok = b.sem(ctx, "parts_ok")
        counts_ok = b.sem(ctx, "counts_ok")
        with nc.Block() as block:

            @block.sync
            def _(sp):
                sp.dma_start(dst_i[:], a["dst"].rearrange("(p e) -> p e", p=P)).then_inc(edges_in, 16)
                sp.dma_start(src_i[:], a["src"].rearrange("(p e) -> p e", p=P)).then_inc(edges_in, 16)
                sp.wait_ge(lists_ok, 2)
                sp.wait_ge(const_ok, 1)
                sp.dma_start(keep.edges[0, 0:EDGES].rearrange("(p e) -> p e", p=P), src_f[:]).then_inc(lists_out, 16)
                sp.dma_start(keep.edges[1, 0:EDGES].rearrange("(p e) -> p e", p=P), dst_f[:]).then_inc(lists_out, 16)
                sp.dma_start(keep.edges[:, EDGES:EDGES + GROUP], pad[:]).then_inc(lists_out, 16)
                sp.dma_start(keep.x, a["x"].rearrange("(t p) d -> p t d", p=P)).then_inc(keep.x_in, 16)
                for w, name in enumerate(("L0_gnn_W_self", "L0_gnn_W_neigh")):
                    sp.dma_start(keep.w_rows[:, w], a[name].rearrange("(k p) d -> p k d", p=128)).then_inc(keep.w_in, 16)
                sp.wait_ge(zeros_ok, 1)
                sp.dma_start(keep.slots_in.rearrange("(s p) d -> p s d", p=SLOT),
                             keep.zeros[:].unsqueeze(1).to_broadcast([128, SLOTS + 1, D])).then_inc(keep.zeros_out, 16)
                sp.wait_ge(lists_out, 48)

            @block.gpsimd
            def _(pool):
                pool.memset(keep.zeros[:], 0.0).then_inc(zeros_ok, 1)
                pool.memset(pad[:], NOWHERE).then_inc(const_ok, 1)
                pool.iota(bounds[:], [[P, T]], base=P, channel_multiplier=0,
                          allow_small_or_imprecise_dtypes=True).then_inc(const_ok, 1)
                pool.memset(keep.ones[:], 1.0).then_inc(const_ok, 1)
                pool.memset(keep.minus_half[:], -0.5)
                pool.iota(steps_j[:], [[GROUP, J]], base=0, channel_multiplier=0,
                          allow_small_or_imprecise_dtypes=True).then_inc(const_ok, 1)
                pool.iota(group_no[:], [[1, GROUPS]], base=0, channel_multiplier=0,
                          allow_small_or_imprecise_dtypes=True).then_inc(const_ok, 1)
                pool.iota(keep.node_no[:], [[1, NODES]], base=0, channel_multiplier=0).then_inc(const_ok, 1)
                pool.memset(keep.ident[:], 0.0).then_inc(ident_ok, 1)
                pool.wait_ge(ident_ok, 1)
                pool.affine_select(out=keep.ident[:], in_=keep.ident[:], compare_op=ALU.not_equal, fill=1.0,
                                   base=0, pattern=[[-1, 128]], channel_multiplier=1).then_inc(ident_ok, 1)
                pool.memset(keep.count[:], 0.0).then_inc(ident_ok, 1)

            @block.tensor
            def _(pe):
                pe.wait_ge(parts_ok, 1)
                pe.wait_ge(const_ok, 6)
                pe.matmul(counts[:], keep.ones[0:P, :], part[:], start=True, stop=True).then_inc(counts_ok, 1)

            @block.vector
            def _(v):
                v.wait_ge(edges_in, 32)
                v.tensor_copy(dst_f[:], dst_i[:]).then_inc(lists_ok, 1)
                v.tensor_copy(src_f[:], src_i[:]).then_inc(lists_ok, 1)
                v.wait_ge(lists_ok, 2)
                v.wait_ge(const_ok, 6)
                link = b.steps_of(v)
                link(v.tensor_tensor(below[:], dst_f[:].unsqueeze(1).to_broadcast([P, T, EDGES // P]),
                                     bounds[:].unsqueeze(2).to_broadcast([P, T, EDGES // P]), ALU.is_lt))
                v.tensor_reduce(part[:], below[:], AX.X, ALU.add).then_inc(parts_ok, 1)
                link(v.memset(lo[:, 0:1], 0.0))
                link(v.memset(ends[:, 0:1], 0.0))
                v.wait_ge(counts_ok, 1)
                link(v.tensor_copy(lo[:, 1:T + 1], counts[:]))
                link(v.tensor_tensor(length[:], lo[:, 1:T + 1], lo[:, 0:T], ALU.subtract))
                link(v.tensor_tensor(more[:], length[:].unsqueeze(2).to_broadcast([128, T, J]),
                                     steps_j[:].unsqueeze(1).to_broadcast([128, T, J]), ALU.is_gt))
                link(v.tensor_reduce(n_groups[:], more[:], AX.X, ALU.add))
                link(v.tensor_tensor_scan(ends[:, 1:T + 1], keep.ones[:, 0:T], n_groups[:], 0.0, ALU.mult, ALU.add))
                link(v.scalar_tensor_tensor(first[:], ends[:, 0:T], -float(GROUP), lo[:, 0:T], ALU.mult, ALU.add))
                link(v.tensor_tensor(past[:], group_no[:].unsqueeze(2).to_broadcast([128, GROUPS, T]),
                                     ends[:, 1:T + 1].unsqueeze(1).to_broadcast([128, GROUPS, T]), ALU.is_ge))
                link(v.tensor_reduce(tile_of[:], past[:], AX.X, ALU.add))
                link(v.tensor_scalar(keep.tile_base[:], tile_of[:], float(P), None, ALU.mult))
                link(v.tensor_scalar(shift[:], past[:, :, 0], -1.0, 1.0, ALU.mult, ALU.add))
                link(v.tensor_scalar(offset[:], shift[:], first[:, 0:1], None, ALU.mult))
                for t in range(1, T):
                    link(v.tensor_tensor(shift[:], past[:, :, t - 1], past[:, :, t], ALU.subtract))
                    link(v.scalar_tensor_tensor(offset[:], shift[:], first[:, t:t + 1], offset[:], ALU.mult, ALU.add))
                link(v.scalar_tensor_tensor(offset[:], group_no[:], float(GROUP), offset[:], ALU.mult, ALU.add))
                link(v.tensor_scalar(offset[:], offset[:], float(EDGES), 0.0, ALU.min, ALU.max))
                link(v.tensor_copy(keep.group_offset[:], offset[0:1, :]))
                link(v.tensor_copy(keep.group_tile[:], tile_of[0:1, :]))


def count_edges(b, keep):
    nc = b.nc
    with ExitStack() as ctx:
        ends = b.sb(ctx, "edge_ends", [128, 2, 2, CHUNKS])
        near = b.sb(ctx, "near", [128, 2, CHUNKS])
        hot_src = b.sb(ctx, "hot_src", [128, RING, NODES], BF16)
        away = b.sb(ctx, "away", [128, CHUNKS, P])
        hot_dst = b.sb(ctx, "hot_dst", [128, 2, CHUNKS, P], BF16)
        sums = b.ps(ctx, "sums", [128, 2, 2048])
        ends_in = [b.sem(ctx, f"ends_in{u}") for u in range(2)]
        near_ok = b.sem(ctx, "near_ok")
        hot_ok = b.sem(ctx, "hot_ok")
        hot_free = b.sem(ctx, "hot_free")
        away_ok = b.sem(ctx, "away_ok")
        dst_ok = b.sem(ctx, "dst_ok")
        moved = b.sb(ctx, "moved", [P, 2, NODES])
        moved_ok = b.sem(ctx, "moved_ok")
        sums_added = b.sem(ctx, "sums_added")
        with nc.Block() as block:

            @block.sync
            def _(sp):
                def load(m, u):
                    at = sp.value_load(keep.group_offset[0:1, bass.ds(m, 1)], min_val=0, max_val=EDGES)
                    sp.dma_start(ends[:, u], keep.edges[:, bass.ds(at, GROUP)].rearrange("e (p c) -> p e c", p=128)
                                 ).then_inc(ends_in[u], 16)

                load(0, 0)
                load(1, 1)
                with sp.Fori(1, GROUPS // 2) as i:
                    for u in range(2):
                        sp.wait_ge(hot_ok, CHUNKS * (2 * i + u - 1))
                        load(2 * i + u, u)
                sp.wait_ge(keep.zeros_out, 16)

            @block.scalar
            def _(act):
                def hots(m, u):
                    act.wait_ge(near_ok, m + 1)
                    act.wait_ge(dst_ok, m)
                    for c in range(CHUNKS):
                        ins = act.activation(away[:, c], keep.node_no[:, 0:P], ACT.Abs, bias=near[:, u, c:c + 1], scale=-1.0)
                    ins.then_inc(away_ok, 1)
                    act.wait_ge(away_ok, m + 1)
                    act.activation(hot_dst[:, u], away[:], ACT.Relu, bias=keep.ones[:, 0:1], scale=-1.0).then_inc(dst_ok, 1)

                def move(m, u):
                    act.wait_ge(hot_free, RING + CHUNKS * (m + 1))
                    act.wait_ge(sums_added, m)
                    act.activation(moved[:, u], sums[0:P, u, 0:NODES], ACT.Copy).then_inc(moved_ok, 1)

                hots(0, 0)
                hots(1, 1)
                move(0, 0)
                with act.Fori(1, GROUPS // 2) as i:
                    for u in range(2):
                        act.wait_ge(hot_free, RING + CHUNKS * (2 * i + u - 1))
                        hots(2 * i + u, u)
                        move(2 * i + u - 1, 1 - u)
                move(GROUPS - 1, 1)

            @block.vector
            def _(v):
                v.sem_inc(hot_free, RING)

                def nears(m, u, k):
                    v.wait_ge(ends_in[u], 16 * k + 16)
                    if not isinstance(m, int) or m >= 2:
                        v.wait_ge(dst_ok, m - 1)
                    v.tensor_scalar(near[:, u], ends[:, u, 1], keep.tile_base[:, bass.ds(m, 1)], None,
                                    ALU.subtract).then_inc(near_ok, 1)

                def hots(m, u, k):
                    for c in range(CHUNKS):
                        if c == CHUNKS - 1 and not (isinstance(m, int) and m == GROUPS - 1):
                            nears(m + 1, 1 - u, k + u)
                        v.wait_ge(hot_free, CHUNKS * m + c + 1)
                        v.tensor_scalar(hot_src[:, CHUNKS * u + c], keep.node_no[:], ends[:, u, 0, c:c + 1], None,
                                        ALU.is_equal).then_inc(hot_ok, 1)

                nears(0, 0, 0)
                hots(0, 0, 0)
                with v.Fori(0, GROUPS // 2 - 1) as i:
                    hots(2 * i + 1, 1, i)
                    hots(2 * i + 2, 0, i + 1)
                hots(GROUPS - 1, 1, GROUPS // 2 - 1)

            @block.gpsimd
            def _(pool):
                pool.sem_inc(sums_added, 1)

                def add(m, u):
                    pool.wait_ge(moved_ok, m + 1)
                    row = pool.value_load(keep.group_tile[0:1, bass.ds(m, 1)], min_val=0, max_val=T)
                    pool.wait_ge(sums_added, m + 1)
                    to = keep.count[:, bass.ds(row, 1), :].rearrange("p a n -> p (a n)")
                    pool.tensor_tensor(to, moved[:, u], to, ALU.add).then_inc(sums_added, 1)

                with pool.Fori(0, GROUPS // 2) as i:
                    for u in range(2):
                        add(2 * i + u, u)

            @block.tensor
            def _(pe):
                def group(m, u):
                    pe.wait_ge(dst_ok, m + 1)
                    for c in range(CHUNKS):
                        pe.wait_ge(hot_ok, CHUNKS * m + c + 1)
                        for c0, w in COLS:
                            ins = pe.matmul(sums[0:P, u, c0:c0 + w], hot_dst[:, u, c], hot_src[:, CHUNKS * u + c, c0:c0 + w],
                                            start=(c == 0), stop=(c == CHUNKS - 1))
                        ins.then_inc(hot_free, 1)

                group(0, 0)
                group(1, 1)
                with pe.Fori(1, GROUPS // 2) as i:
                    for u in range(2):
                        pe.wait_ge(moved_ok, 2 * i + u - 1)
                        group(2 * i + u, u)


class Banks:

    def __init__(self, b, ctx, name, ring=BANKS):
        self.b, self.ring = b, ring
        self.at = b.ps(ctx, name, [128, ring, 512])
        self.full0, self.free0 = list(b.filled), list(b.emptied)

    def __getitem__(self, j):
        return self.at[:, j % self.ring]

    def wait_emptied(self, eng, j):
        i = j % self.ring
        eng.wait_ge(self.b.free[i], self.free0[i] + j // self.ring + 1)

    def wait_free(self, pe, j):
        if j >= self.ring:
            self.wait_emptied(pe, j - self.ring)

    def wait_full(self, eng, j):
        i = j % self.ring
        eng.wait_ge(self.b.full[i], self.full0[i] + j // self.ring + 1)

    def filled(self, ins, j):
        self.b.filled[j % self.ring] += 1
        ins.then_inc(self.b.full[j % self.ring], 1)

    def emptied(self, ins, j):
        self.b.emptied[j % self.ring] += 1
        ins.then_inc(self.b.free[j % self.ring], 1)

    def release(self, eng, j):
        self.b.emptied[j % self.ring] += 1
        eng.sem_inc(self.b.free[j % self.ring], 1)


def variance_root(pool, rstd, var, minus_half):
    return pool.tensor_tensor(rstd, var, minus_half, ALU.pow)


def sage(b, keep):
    nc, a = b.nc, b.a
    with ExitStack() as ctx:
        w_t = b.sb(ctx, "w_t", [128, 2, C, D])
        xt = b.sb(ctx, "xt", [128, T * D])
        xn_t = xt[:, 0:C * NODES].rearrange("p (c n) -> p c n", c=C)
        x_again = xt[0:P, :].rearrange("p (t d) -> p t d", t=T)
        from_src = b.sb(ctx, "from_src", [P, 2, T, P])
        absent = b.sb(ctx, "absent", [P, 2, NODES], BF16)
        tiny = b.sb(ctx, "tiny", [P, 1])
        logs = b.sb(ctx, "logs", [P, 2, T, P])
        worth = b.sb(ctx, "worth_part", [P, 2, T, P])
        tiny_ok = b.sem(ctx, "tiny_ok")
        logs_ok = b.sem(ctx, "logs_ok")
        worth_ok = b.sem(ctx, "worth_ok")
        worth_out = [b.sem(ctx, f"worth_out{u}") for u in range(2)]
        row3 = b.sb(ctx, "sage_rows", [P, 3, D])
        stats = b.sb(ctx, "stats", [P, T, 3, 6])
        mv = b.sb(ctx, "mv", [P, T, 3, 2])
        var = b.sb(ctx, "var", [P, T, 3])
        rstd = b.sb(ctx, "rstd", [P, T, 3])
        degree = b.sb(ctx, "degree", [P, T])
        rdeg = b.sb(ctx, "rdeg", [P, T])
        banks = Banks(b, ctx, "sage_banks")
        rows_in = b.sem(ctx, "sage_rows_in")
        x_again_in = b.sem(ctx, "x_again_in")
        var_ok, rstd_ok, roots = b.roots(1 + 2 * T)
        xn_ok = b.sem(ctx, "xn_ok")
        wt_ok = b.sem(ctx, "wt_ok")
        xnt_ok = b.sem(ctx, "xnt_ok")
        z_ok = b.sem(ctx, "z_ok")
        from_ok = b.sem(ctx, "from_ok")
        absent_ok = b.sem(ctx, "absent_ok")
        absent_out = [b.sem(ctx, f"absent_out{u}") for u in range(2)]
        never_ok = b.sem(ctx, "never_ok")

        W0 = 0
        X0 = W0 + 2 * C
        Z0 = X0 + C * len(QUADS)
        S0 = Z0 + T
        E0 = S0 + T
        def turn_job(t, q):
            return E0 + (q if t == 0 else 3 + 4 * (t - 1) + q)
        def sum_job(t):
            return E0 + (3 + 4 * t + 3 if t < T - 1 else 3 + 4 * (T - 1))

        with nc.Block() as block:

            @block.sync
            def _(sp):
                for k, name in enumerate(("L0_gnn_bias", "L0_gnn_gamma", "L0_gnn_beta")):
                    sp.dma_start(row3[:, k], a[name].unsqueeze(0).to_broadcast([P, D])).then_inc(rows_in, 16)
                for t in range(T):
                    sp.wait_ge(absent_ok, t + 1)
                    sp.dma_start(keep.absent[t * P:(t + 1) * P, :], absent[:, t % 2]).then_inc(absent_out[t % 2], 16)
                banks.wait_full(sp, S0 + T - 1)
                sp.dma_start(x_again, a["x"].rearrange("(t p) d -> p t d", p=P)).then_inc(x_again_in, 16)
                for t in range(T):
                    sp.wait_ge(worth_ok, t + 1)
                    sp.dma_start(keep.worth_rows.rearrange("(s p) n -> p s n", p=P)[:, :, P * t:P * t + P], worth[:, t % 2]
                                 ).then_inc(worth_out[t % 2], 16)
                for u in range(2):
                    sp.wait_ge(absent_out[u], 16 * T // 2)
                    sp.wait_ge(worth_out[u], 16 * T // 2)

            @block.tensor
            def _(pe):
                pe.wait_ge(keep.w_in, 32)
                for w in range(2):
                    for c in range(C):
                        j = W0 + w * C + c
                        banks.wait_free(pe, j)
                        for k in range(C):
                            ins = pe.transpose(banks[j][:, 128 * k:128 * k + 128],
                                               keep.w_rows[:, w, k, 128 * c:128 * c + 128], keep.ident[:])
                        banks.filled(ins, j)
                for q, (t0, n) in enumerate(QUADS):
                    pe.wait_ge(xn_ok, t0 + n)
                    for c in range(C):
                        j = X0 + C * q + c
                        banks.wait_free(pe, j)
                        for t in range(n):
                            ins = pe.transpose(banks[j][:, P * t:P * t + P],
                                               keep.y[:, t0 + t, 128 * c:128 * c + 128], keep.ident[0:P, 0:P])
                        banks.filled(ins, j)
                pe.wait_ge(wt_ok, 2 * C)
                pe.wait_ge(xnt_ok, C * len(QUADS))
                for w, first in ((1, Z0), (0, S0)):
                    for t in range(T):
                        banks.wait_free(pe, first + t)
                        for c in range(C):
                            ins = pe.matmul(banks[first + t][0:P, :], xn_t[:, c, P * t:P * t + P], w_t[:, w, c],
                                            start=(c == 0), stop=(c == C - 1))
                        banks.filled(ins, first + t)

                def turn(t):
                    for q, (s0, n) in enumerate(QUADS):
                        j = turn_job(t, q)
                        banks.wait_free(pe, j)
                        for s in range(n):
                            ins = pe.transpose(banks[j][0:P, P * s:P * s + P],
                                               keep.count[:, t, P * (s0 + s):P * (s0 + s) + P], keep.ident[0:P, 0:P])
                        banks.filled(ins, j)

                turn(0)
                pe.wait_ge(z_ok, T)
                for t in range(T):
                    if t + 1 < T:
                        turn(t + 1)
                    pe.wait_ge(from_ok, 3 * t + 3)
                    j = sum_job(t)
                    banks.wait_free(pe, j)
                    for s in range(T):
                        ins = pe.matmul(banks[j][0:P, :], from_src[:, t % 2, s], keep.y[:, s],
                                        start=(s == 0), stop=(s == T - 1))
                    banks.filled(ins, j)

            @block.scalar
            def _(act):
                def evacuate(j, to, of, done):
                    banks.wait_full(act, j)
                    banks.emptied(act.activation(to, of, ACT.Copy), j)

                for j in range(2 * C):
                    banks.wait_full(act, W0 + j)
                    act.activation(w_t[:, j // C, j % C], banks[W0 + j][:, :], ACT.Copy).then_inc(wt_ok, 1)
                    act.wait_ge(wt_ok, j + 1)
                    banks.release(act, W0 + j)
                for q, (t0, n) in enumerate(QUADS):
                    for c in range(C):
                        j = X0 + C * q + c
                        banks.wait_full(act, j)
                        act.activation(xn_t[:, c, P * t0:P * (t0 + n)], banks[j][:, 0:P * n], ACT.Copy).then_inc(xnt_ok, 1)
                        act.wait_ge(xnt_ok, C * q + c + 1)
                        banks.release(act, j)
                for t in range(T):
                    banks.wait_full(act, Z0 + t)
                    act.activation(keep.y[:, t], banks[Z0 + t][0:P, :], ACT.Copy).then_inc(z_ok, 1)
                    act.wait_ge(z_ok, t + 1)
                    banks.release(act, Z0 + t)

                act.wait_ge(tiny_ok, 1)
                for t in range(T):
                    for q, (s0, n) in enumerate(QUADS):
                        j = turn_job(t, q)
                        banks.wait_full(act, j)
                        if t >= 2:
                            banks.wait_full(act, sum_job(t - 2))
                            act.wait_ge(never_ok, t - 1)
                            act.wait_ge(worth_ok, t - 1)
                        act.activation(from_src[:, t % 2, s0:s0 + n],
                                       banks[j][0:P, 0:P * n].rearrange("p (s d) -> p s d", s=n), ACT.Copy).then_inc(from_ok, 1)
                        act.wait_ge(from_ok, 3 * t + q + 1)
                        banks.release(act, j)
                    act.activation(logs[:, t % 2], from_src[:, t % 2], ACT.Ln, bias=tiny[:]).then_inc(logs_ok, 1)

            @block.gpsimd
            def _(pool):
                pool.memset(tiny[:], 1e-19).then_inc(tiny_ok, 1)
                pool.wait_ge(var_ok, roots + 1)
                variance_root(pool, rstd[:, :, 0], var[:, :, 0], keep.minus_half[0:P, 0:T]).then_inc(rstd_ok, 1)
                for t in range(T + 1):
                    if t < T:
                        pool.wait_ge(never_ok, t + 1)
                        pool.wait_ge(logs_ok, t + 1)
                        pool.tensor_tensor(worth[:, t % 2], worth[:, t % 2], logs[:, t % 2], ALU.subtract).then_inc(worth_ok, 1)
                    if t >= 1:
                        for k in (1, 2):
                            pool.wait_ge(var_ok, roots + 2 * (t - 1) + k + 1)
                            variance_root(pool, rstd[:, t - 1, k:k + 1], var[:, t - 1, k:k + 1],
                                          keep.minus_half[0:P, 0:1]).then_inc(rstd_ok, 1)

            @block.vector
            def _(v):
                link = b.steps_of(v)
                v.wait_ge(keep.x_in, 16)
                for t in range(T):
                    ins = v.bn_stats(stats[:, t, 0], keep.y[:, t])
                link(ins)
                for t in range(T):
                    ins = v.bn_aggr(mv[:, t, 0], stats[:, t, 0])
                link(ins)
                v.tensor_scalar(var[:, :, 0], mv[:, :, 0, 1], EPS, None, ALU.add).then_inc(var_ok, 1)
                v.wait_ge(rstd_ok, roots + 1)
                for t in range(T):
                    v.tensor_scalar(keep.y[:, t], keep.y[:, t], mv[:, t, 0, 0:1], rstd[:, t, 0:1],
                                    ALU.subtract, ALU.mult).then_inc(xn_ok, 1)
                for t in range(T):
                    if t >= 2:
                        v.wait_ge(absent_out[t % 2], 16 * (t // 2))
                    v.tensor_scalar(absent[:, t % 2], keep.count[:, t], 0.0, -3e38, ALU.is_equal, ALU.mult).then_inc(absent_ok, 1)
                    link(v.tensor_reduce(degree[:, t:t + 1], keep.count[:, t], AX.X, ALU.add))
                link(v.tensor_scalar(degree[:], degree[:], 1.0, None, ALU.max))
                link(v.reciprocal(rdeg[:], degree[:]))
                v.wait_ge(rows_in, 48)
                for t in range(T):
                    banks.wait_full(v, S0 + t)
                    link(v.tensor_tensor(keep.res[:, t], banks[S0 + t][0:P, :], row3[:, 0], ALU.add))
                    banks.release(v, S0 + t)
                def never(t):
                    v.wait_ge(from_ok, 3 * t + 3)
                    if t >= 2:
                        v.wait_ge(worth_out[t % 2], 16 * (t // 2))
                    v.tensor_scalar(worth[:, t % 2], from_src[:, t % 2], 0.0, NEVER, ALU.is_equal, ALU.mult).then_inc(never_ok, 1)

                never(0)
                for t in range(T):
                    if t + 1 < T:
                        never(t + 1)
                    r = keep.res[:, t]
                    j = sum_job(t)
                    banks.wait_full(v, j)
                    link(v.scalar_tensor_tensor(r, banks[j][0:P, :], rdeg[:, t:t + 1], r, ALU.mult, ALU.add))
                    banks.release(v, j)

                    def normed(k, to):
                        link(v.bn_stats(stats[:, t, k], r))
                        link(v.bn_aggr(mv[:, t, k], stats[:, t, k]))
                        v.tensor_scalar(var[:, t, k:k + 1], mv[:, t, k, 1:2], EPS, None, ALU.add).then_inc(var_ok, 1)
                        v.wait_ge(rstd_ok, roots + 2 * t + k + 1)
                        link(v.tensor_scalar(to, r, mv[:, t, k, 0:1], rstd[:, t, k:k + 1], ALU.subtract, ALU.mult))

                    normed(1, r)
                    link(v.tensor_tensor(r, r, row3[:, 1], ALU.mult))
                    link(v.tensor_tensor(r, r, row3[:, 2], ALU.add))
                    if t == 0:
                        v.wait_ge(x_again_in, 16)
                    link(v.tensor_tensor(r, r, x_again[:, t], ALU.add))
                    normed(2, x_again[:, t])
                banks.wait_full(v, sum_job(T - 1))
                v.tensor_copy(keep.y, x_again)


def turn_rows(pe, banks, first, rows, ident, ready=None, quads=range(len(QUADS))):
    for q in quads:
        t0, n = QUADS[q]
        if ready:
            pe.wait_ge(ready, q + 1)
        for c in range(C):
            j = first + C * q + c
            banks.wait_free(pe, j)
            for t in range(n):
                ins = pe.transpose(banks[j][:, P * t:P * t + P], rows[:, t0 + t, 128 * c:128 * c + 128], ident[0:P, 0:P])
            banks.filled(ins, j)


def turned_out(act, banks, first, cols, quads=range(len(QUADS))):
    for q in quads:
        t0, n = QUADS[q]
        for c in range(C):
            j = first + C * q + c
            banks.wait_full(act, j)
            banks.emptied(act.activation(cols[:, c, P * t0:P * (t0 + n)], banks[j][:, 0:P * n], ACT.Copy), j)


def attention(b, keep):
    nc, a = b.nc, b.a
    H, HD = 8, 64
    PAIRS = H // 2
    U = 2 * T
    with ExitStack() as ctx:
        y_t = b.sb(ctx, "y_t", [128, C, NODES])
        vals = b.sb(ctx, "vals", [P, T, H, HD])
        w_v = b.sb(ctx, "w_v", [128, C, D])
        bv = b.sb(ctx, "bv", [P, D])
        bq = b.sb(ctx, "bq", [128, 2, PAIRS])
        w_qk = b.sb(ctx, "w_qk", [128, 2, C, 128])
        v_in = b.sem(ctx, "v_in")
        bqk_in = b.sem(ctx, "bqk_in")
        w_qk_in = b.sem(ctx, "w_qk_in")
        sources = [a["L0_ffn_" + n].rearrange("(c p) n -> p c n", p=128) for n in ("Wq", "Wk")]
        with ExitStack() as stage:
            banks = Banks(b, stage, "value_banks")
            with nc.Block() as block:

                @block.sync
                def _(sp):
                    sp.dma_start(w_v[:], a["L0_ffn_Wv"].rearrange("(c p) n -> p c n", p=128)).then_inc(v_in, 16)
                    sp.dma_start(bv[:], a["L0_ffn_bv"].unsqueeze(0).to_broadcast([P, D])).then_inc(v_in, 16)
                    for k, n in enumerate(("bq", "bk")):
                        sp.dma_start(bq[:, k], a["L0_ffn_" + n].rearrange("(i p) -> p i", p=128),
                                     allow_slow_non_contiguous=True).then_inc(bqk_in, 16)
                    for k in range(2):
                        sp.dma_start(w_qk[:, k], sources[k][:, :, 0:128]).then_inc(w_qk_in, 16)

                @block.tensor
                def _(pe):
                    turn_rows(pe, banks, 0, keep.y, keep.ident)
                    first = C * len(QUADS)
                    pe.wait_ge(v_in, 32)
                    for j in range(first - BANKS, first):
                        banks.wait_emptied(pe, j)
                    for t in range(T):
                        j = first + t
                        banks.wait_free(pe, j)
                        for c in range(C):
                            ins = pe.matmul(banks[j][0:P, :], y_t[:, c, P * t:P * t + P], w_v[:, c],
                                            start=(c == 0), stop=(c == C - 1))
                        banks.filled(ins, j)

                @block.scalar
                def _(act):
                    turned_out(act, banks, 0, y_t)

                @block.vector
                def _(v):
                    v.wait_ge(v_in, 32)
                    for t in range(T):
                        j = C * len(QUADS) + t
                        banks.wait_full(v, j)
                        banks.emptied(v.tensor_tensor(vals[:, t].rearrange("p h d -> p (h d)"), banks[j][0:P, :], bv[:], ALU.add), j)

        with ExitStack() as stage:
            S, HALF = HD ** -0.5, T // 2
            KEPT = 8
            q_t = b.sb(stage, "q_t", [128, 2, NODES])
            k_t = b.sb(stage, "k_t", [128, NODES])
            zeros_ok = b.sem(stage, "q_zeros_ok")
            probs = b.sb(stage, "probs", [P, 2, NODES])
            probs_t = b.sb(stage, "probs_t", [P, 4, T, P])
            mixed_t = b.sb(stage, "mixed_t", [128, 2, P])
            top = b.sb(stage, "top", [P, 2])
            shift = b.sb(stage, "neg_max", [P, 2])
            bq_now = b.sb(stage, "bq_now", [128, 1])
            total = b.sb(stage, "total", [P, KEPT])
            share = b.sb(stage, "share", [P, 2, 2])
            vals_now = b.sb(stage, "vals_now", [P, T, 2, HD])
            vals_ok = b.sem(stage, "vals_ok")
            scores = b.ps(stage, "scores", [128, 2, 3 * 512])
            turned = b.ps(stage, "turned", [128, 512])
            mixed = b.ps(stage, "mixed", [128, 512])
            bq_ok = b.sem(stage, "bq_ok")
            proj_ok = b.sem(stage, "proj_ok")
            q_ok = b.sem(stage, "q_ok")
            k_ok = b.sem(stage, "k_ok")
            scores_ok = b.sem(stage, "scores_ok")
            max_ok = b.sem(stage, "max_ok")
            shift_ok = b.sem(stage, "shift_ok")
            probs_ok = b.sem(stage, "probs_ok")
            turned_ok = [b.sem(stage, f"turned_ok{q}") for q in range(3)]
            copied = [b.sem(stage, f"copied{q}") for q in range(3)]
            mixed_ok = b.sem(stage, "mixed_ok")
            mixed_out = b.sem(stage, "mixed_out")
            back_ok = b.sem(stage, "back_ok")
            share_ok = b.sem(stage, "share_ok")
            back_out = b.sem(stage, "back_out")
            STEPS = U + 6

            def turning(j):
                return j - 2 if 2 <= j < U + 2 else None

            def mixing(j):
                return divmod(j - 4, 2) if 4 <= j < U + 4 else (None, 0)

            def turns_back(j):
                return (j - 6) // 2 if j >= 6 and j % 2 == 0 else None

            with nc.Block() as block:

                @block.gpsimd
                def _(pool):
                    for h in range(2):
                        pool.memset(q_t[HD * (1 - h):HD * (2 - h), h], 0.0).then_inc(zeros_ok, 1)

                @block.sync
                def _(sp):
                    with sp.Fori(1, PAIRS) as i:
                        sp.wait_ge(proj_ok, 6 * i)
                        for k in range(2):
                            sp.dma_start(w_qk[:, k], sources[k][:, :, bass.ds(128 * i, 128)]).then_inc(w_qk_in, 16)

                @block.tensor
                def _(pe):
                    def project(x):
                        c0, w = COLS[x % 3]
                        for c in range(C):
                            ins = pe.matmul(scores[:, x // 3, c0:c0 + w], w_qk[:, 1 - x // 3, c], y_t[:, c, c0:c0 + w],
                                            start=(c == 0), stop=(c == C - 1))
                        ins.then_inc(proj_ok, 1)

                    def turn(i, j, q):
                        k = turning(j)
                        if k is None:
                            return
                        n = U * i + k
                        if q == 0:
                            pe.wait_ge(probs_ok, n + 3)
                            pe.wait_ge(copied[2], n + 1)
                            pe.wait_ge(back_out, T * i + max(0, (j - 5) // 2) + 1)
                        else:
                            pe.wait_ge(copied[q - 1], n + 2)
                        s0, m = QUADS[q]
                        for s in range(m):
                            ins = pe.transpose(turned[0:P, P * s:P * s + P], probs[:, k % 2, P * (s0 + s):P * (s0 + s) + P],
                                               keep.ident[0:P, 0:P])
                        ins.then_inc(turned_ok[q], 1)

                    def mix(i, j, s0, s1):
                        t, half = mixing(j)
                        if t is None:
                            return
                        m = T * i + t
                        if s0 == 0:
                            if half == 0:
                                pe.wait_ge(mixed_out, m + 1)
                                pe.wait_ge(copied[0], 2 * m + 3)
                                pe.wait_ge(copied[1], 2 * m + 3)
                            else:
                                pe.wait_ge(copied[2], 2 * m + 3)
                        for s in range(HALF * half + s0, HALF * half + s1):
                            for h in range(2):
                                rows = slice(HD * h, HD * h + HD)
                                ins = pe.matmul(mixed[rows, 0:P], vals_now[:, s, h], probs_t[:, (2 * t + h) % 4, s],
                                                start=(s == 0), stop=(s == T - 1), tile_position=(0, HD * h))
                        if half and s1 == HALF:
                            ins.then_inc(mixed_ok, 1)

                    def turn_back(i, j):
                        t = turns_back(j)
                        if t is None:
                            return
                        m = T * i + t
                        pe.wait_ge(mixed_out, m + 2)
                        pe.wait_ge(copied[2], U * i + min(j - 2, U - 1) + 2)
                        pe.wait_ge(back_out, m + 1)
                        pe.transpose(turned[0:P, 0:128], mixed_t[:, t % 2], keep.ident[:]).then_inc(back_ok, 1)

                    def steps(i, last=False):
                        for j in range(STEPS):
                            if mixing(j) == (0, 0):
                                pe.wait_ge(vals_ok, i + 1)
                            if j < U:
                                if j == 0:
                                    pe.wait_ge(k_ok, 3 * i + 3)
                                    pe.wait_ge(q_ok, 6 * i + 2)
                                if j == 1:
                                    pe.wait_ge(q_ok, 6 * i + 6)
                                pe.wait_ge(probs_ok, U * i + j + 1)
                                t, h = divmod(j, 2)
                            elif not last:
                                x = j - U
                                if x == 0:
                                    pe.wait_ge(w_qk_in, 32 * i + 64)
                                pe.wait_ge(probs_ok, U * i + U - 2 + x // 3 + 3)
                            for part, (c0, w) in enumerate(COLS):
                                if j < U:
                                    ins = pe.matmul(scores[0:P, h, c0:c0 + w], q_t[:, h, P * t:P * t + P], k_t[:, c0:c0 + w],
                                                    start=True, stop=True)
                                elif part == 0 and not last:
                                    project(x)
                                turn(i, j, part)
                                mix(i, j, max(0, 2 * part - 1), 2 * part + 1)
                            if j < U:
                                ins.then_inc(scores_ok, 1)
                            turn_back(i, j)

                    pe.sem_inc(mixed_ok, 2)
                    pe.sem_inc(back_ok, 2)
                    pe.sem_inc(turned_ok[2], 2)
                    pe.wait_ge(zeros_ok, 2)
                    pe.wait_ge(w_qk_in, 32)
                    for x in range(6):
                        project(x)
                    with pe.Fori(0, PAIRS - 1) as i:
                        steps(i)
                    steps(PAIRS - 1, last=True)

                @block.scalar
                def _(act):
                    def queries(p, x):
                        c0, w = COLS[x]
                        if x == 0:
                            act.wait_ge(bq_ok, p + 1)
                        act.wait_ge(proj_ok, 6 * p + 3 + x + 1)
                        for h in range(2):
                            rows = slice(HD * h, HD * h + HD)
                            act.activation(q_t[rows, h, c0:c0 + w], scores[rows, 1, c0:c0 + w], ACT.Identity,
                                           bias=bq_now[rows, :]).then_inc(q_ok, 1)

                    def copy(i, j, q):
                        k = turning(j)
                        if k is None:
                            return
                        n = U * i + k
                        if q == 0:
                            act.wait_ge(mixed_ok, T * i + k // 2 + 1)
                            act.wait_ge(turned_ok[0], n + 1)
                        else:
                            act.wait_ge(turned_ok[2], n + 3)
                        s0, m = QUADS[q]
                        act.activation(probs_t[:, k % 4, s0:s0 + m], turned[0:P, 0:P * m].rearrange("p (s d) -> p s d", s=m),
                                       ACT.Copy).then_inc(copied[q], 1)

                    def steps(i, last=False):
                        for j in range(STEPS):
                            copy(i, j, 0)
                            if 1 <= j <= U:
                                k = j - 1
                                n = U * i + k
                                act.wait_ge(shift_ok, n + 1)
                                act.wait_ge(turned_ok[2], n + 1)
                                act.activation(probs[:, k % 2], scores[0:P, k % 2, 0:NODES], ACT.Exp, bias=shift[:, k % 2:k % 2 + 1],
                                               scale=S, accum_out=total[:, k % KEPT:k % KEPT + 1]).then_inc(probs_ok, 1)
                            copy(i, j, 2)
                            if not last and j >= U + 3:
                                queries(i + 1, j - U - 3)

                    act.sem_inc(probs_ok, 2)
                    act.sem_inc(copied[0], 1)
                    act.sem_inc(copied[2], 1)
                    for x in range(3):
                        queries(0, x)
                    with act.Fori(0, PAIRS - 1) as i:
                        steps(i)
                    steps(PAIRS - 1, last=True)

                @block.vector
                def _(v):
                    def prepare(p):
                        v.tensor_scalar(bq_now[:], bq[:, 0, bass.ds(p, 1)], 1.0, None, ALU.mult).then_inc(bq_ok, 1)

                    def keys(p, x):
                        c0, w = COLS[x]
                        v.wait_ge(proj_ok, 6 * p + x + 1)
                        v.tensor_scalar(k_t[:, c0:c0 + w], scores[:, 0, c0:c0 + w], bq[:, 1, bass.ds(p, 1)], None,
                                        ALU.add).then_inc(k_ok, 1)

                    def steps(i, last=False):
                        for j in range(STEPS):
                            if j == 3:
                                v.wait_ge(mixed_ok, T * i + 2)
                                v.tensor_scalar(vals_now[:].rearrange("p s h d -> p s (h d)"),
                                                vals[:, :, bass.ds(2 * i, 2), :].rearrange("p s h d -> p s (h d)"),
                                                1.0, None, ALU.mult).then_inc(vals_ok, 1)
                            t = turns_back(j)
                            if t is not None:
                                m = T * i + t
                                v.wait_ge(mixed_ok, m + 3)
                                v.wait_ge(back_ok, m + 1)
                                v.tensor_copy(mixed_t[:, t % 2], mixed[:, 0:P]).then_inc(mixed_out, 1)
                            if 1 <= j <= U:
                                k = j - 1
                                n = U * i + k
                                at = slice(k % 2, k % 2 + 1)
                                v.wait_ge(scores_ok, n + 1)
                                v.tensor_reduce(top[:, at], scores[0:P, k % 2, 0:NODES], AX.X, ALU.max).then_inc(max_ok, 1)
                                v.wait_ge(max_ok, n + 1)
                                v.wait_ge(probs_ok, n + 1)
                                v.tensor_scalar(shift[:, at], top[:, at], -S, None, ALU.mult).then_inc(shift_ok, 1)
                            k = turning(j)
                            if k is not None:
                                s0, m = QUADS[1]
                                v.wait_ge(mixed_ok, T * i + k // 2 + 1)
                                v.wait_ge(turned_ok[1], U * i + k + 1)
                                v.tensor_copy(probs_t[:, k % 4, s0:s0 + m],
                                              turned[0:P, 0:P * m].rearrange("p (s d) -> p s d", s=m)).then_inc(copied[1], 1)
                            if not last and j == U - 1:
                                v.wait_ge(q_ok, 6 * i + 6)
                                prepare(i + 1)
                            if not last and U <= j < U + 3:
                                keys(i + 1, j - U)
                            t = turns_back(j)
                            if t is not None:
                                m = T * i + t
                                k = (2 * t) % KEPT
                                v.reciprocal(share[:, t % 2], total[:, k:k + 2]).then_inc(share_ok, 1)
                                v.wait_ge(share_ok, m + 1)
                                v.wait_ge(back_ok, m + 3)
                                for h in range(2):
                                    ins = v.tensor_scalar(keep.o[:, t, bass.ds(HD * (2 * i + h), HD)], turned[0:P, HD * h:HD * h + HD],
                                                          share[:, t % 2, h:h + 1], None, ALU.mult)
                                ins.then_inc(back_out, 1)

                    v.sem_inc(copied[1], 1)
                    v.sem_inc(mixed_out, 1)
                    v.sem_inc(back_out, 1)
                    v.wait_ge(bqk_in, 32)
                    prepare(0)
                    for x in range(3):
                        keys(0, x)
                    with v.Fori(0, PAIRS - 1) as i:
                        steps(i)
                    steps(PAIRS - 1, last=True)


def load_w1(b, keep, sp, e, half):
    sp.dma_start(keep.w1[:, half], b.a["L0_ffn_W1"][bass.ds(e, 1)].rearrange("a (c p) f -> p (a c) f", p=128)
                 ).then_inc(keep.w1_in[half], 16)


def routing(b, keep):
    nc, a = b.nc, b.a
    with ExitStack() as ctx:
        o_t = b.sb(ctx, "o_t", [128, C, NODES])
        t_t = b.sb(ctx, "t_t", [128, C, NODES])
        w_o = b.sb(ctx, "w_o", [128, C, D])
        rows = b.sb(ctx, "route_rows", [P, 3, D])
        gate_w = b.sb(ctx, "gate_w", [128, C, EXPERTS])
        gate_b = b.sb(ctx, "gate_b", [P, EXPERTS])
        earlier = b.sb(ctx, "earlier", [P, P])
        expert_no = b.sb(ctx, "expert_no", [P, EXPERTS])
        slot_no = b.sb(ctx, "slot_no", [1, SLOTS + 1])
        J = -(-NODES // SLOT)
        slot_steps = b.sb(ctx, "slot_steps", [128, J])
        stats = b.sb(ctx, "route_stats", [P, T, 6])
        mv = b.sb(ctx, "route_mv", [P, T, 2])
        var = b.sb(ctx, "route_var", [P, T])
        rstd = b.sb(ctx, "route_rstd", [P, T])
        logits = b.sb(ctx, "logits", [P, T, EXPERTS])
        best = b.sb(ctx, "best", [P, T])
        exps = b.sb(ctx, "exps", [P, T, EXPERTS])
        chosen = b.sb(ctx, "chosen", [P, T, EXPERTS])
        before = b.sb(ctx, "before", [P, T + 1, EXPERTS])
        place = b.sb(ctx, "place_f", [P, T])
        placed = b.sb(ctx, "placed", [P, T, EXPERTS])
        counts = b.sb(ctx, "expert_counts", [128, EXPERTS])
        over = b.sb(ctx, "over", [128, EXPERTS, J])
        n_slots = b.sb(ctx, "n_slots", [128, EXPERTS])
        ends = b.sb(ctx, "slot_ends", [128, EXPERTS])
        base = b.sb(ctx, "slot_base", [128, EXPERTS])
        passed = b.sb(ctx, "passed", [1, SLOTS + 1, EXPERTS])
        tables = b.sb(ctx, "slot_tables", [1, 4, SLOTS + 1])
        banks = Banks(b, ctx, "route_banks")
        w_in = b.sem(ctx, "route_w_in")
        const_ok = b.sem(ctx, "route_const_ok")
        o_t_ok = b.sem(ctx, "o_t_ok")
        var_ok, rstd_ok, roots = b.roots(T)
        t_ok = b.sem(ctx, "t_ok")
        shifted_ok = b.sem(ctx, "shifted_ok")
        exps_ok = b.sem(ctx, "exps_ok")
        chosen_ok = b.sem(ctx, "chosen_ok")
        place_ok = b.sem(ctx, "place_ok")
        sent = b.sem(ctx, "tokens_sent")
        bo_ok = b.sem(ctx, "bo_ok")
        N = C * len(QUADS)
        SPLIT = T - 2
        TURN = [N + SPLIT, N + T + C + 1, N + T + 2 * C + 1]
        GATE = [N + T + C, N + T + 3 * C + 1, N + T + 3 * C + 2]
        RANK = GATE[-1] + 1

        def proj(t):
            return N + t + (C if t >= SPLIT else 0)

        with nc.Block() as block:

            @block.sync
            def _(sp):
                sp.dma_start(w_o[:], a["L0_ffn_Wo"].rearrange("(c p) n -> p c n", p=128)).then_inc(w_in, 16)
                for k, n in enumerate(("bo", "ln1_g", "ln1_b")):
                    sp.dma_start(rows[:, k], a["L0_ffn_" + n].unsqueeze(0).to_broadcast([P, D])).then_inc(w_in, 16)
                sp.dma_start(gate_w[:], a["L0_ffn_gate_W"].rearrange("(c p) n -> p c n", p=128)).then_inc(w_in, 16)
                sp.dma_start(gate_b[:], a["L0_ffn_gate_b"].unsqueeze(0).to_broadcast([P, EXPERTS])).then_inc(w_in, 16)
                sp.dma_start(keep.b1_rows[:], a["L0_ffn_b1"].rearrange("e (f p) -> (e f) p", p=128)).then_inc(keep.b1_in, 16)
                sp.sem_inc(keep.w1_in[1], 16)
                for e in range(2):
                    load_w1(b, keep, sp, e, e)

            @block.gpsimd
            def _(pool):
                iota = dict(base=0, channel_multiplier=0, allow_small_or_imprecise_dtypes=True)
                pool.iota(expert_no[:], [[1, EXPERTS]], **iota).then_inc(const_ok, 1)
                pool.iota(slot_no[:], [[1, SLOTS + 1]], **iota).then_inc(const_ok, 1)
                pool.iota(slot_steps[:], [[SLOT, J]], **iota).then_inc(const_ok, 1)
                pool.memset(earlier[:], 1.0).then_inc(const_ok, 1)
                pool.wait_ge(const_ok, 4)
                pool.affine_select(out=earlier[:], in_=earlier[:], compare_op=ALU.is_gt, fill=0.0, base=0,
                                   pattern=[[1, P]], channel_multiplier=-1).then_inc(const_ok, 1)
                pool.wait_ge(w_in, 96)
                for t in range(T):
                    pool.tensor_tensor(keep.y[:, t], keep.y[:, t], rows[:, 0], ALU.add).then_inc(bo_ok, 1)
                for t in range(T):
                    pool.wait_ge(var_ok, roots + t + 1)
                    variance_root(pool, rstd[:, t:t + 1], var[:, t:t + 1], keep.minus_half[0:P, 0:1]).then_inc(rstd_ok, 1)
                pool.wait_ge(place_ok, 1)
                for t in range(T):
                    pool.indirect_dma_start(out=keep.slots_in, out_offset=bass.IndirectOffsetOnAxis(ap=keep.place[:, t:t + 1], axis=0),
                                            in_=keep.y[:, t], in_offset=None).then_inc(sent, 16)
                pool.wait_ge(sent, 16 * T)

            @block.tensor
            def _(pe):
                turn_rows(pe, banks, 0, keep.o, keep.ident)
                pe.wait_ge(w_in, 96)
                pe.wait_ge(o_t_ok, 1)
                def project(t):
                    j = proj(t)
                    banks.wait_free(pe, j)
                    for c in range(C):
                        ins = pe.matmul(banks[j][0:P, :], o_t[:, c, P * t:P * t + P], w_o[:, c], start=(c == 0), stop=(c == C - 1))
                    banks.filled(ins, j)

                def turn(q):
                    t0, n = QUADS[q]
                    pe.wait_ge(t_ok, t0 + n)
                    turn_rows(pe, banks, TURN[q] - C * q, keep.y, keep.ident, quads=(q,))

                def gate(q):
                    t0, n = QUADS[q]
                    pe.wait_ge(o_t_ok, q + 2)
                    banks.wait_free(pe, GATE[q])
                    for t in range(n):
                        for c in range(C):
                            ins = pe.matmul(banks[GATE[q]][0:P, EXPERTS * t:EXPERTS * t + EXPERTS],
                                            t_t[:, c, P * (t0 + t):P * (t0 + t) + P], gate_w[:, c], start=(c == 0), stop=(c == C - 1))
                    banks.filled(ins, GATE[q])

                for t in range(SPLIT):
                    project(t)
                turn(0)
                for t in range(SPLIT, T):
                    project(t)
                gate(0)
                turn(1)
                turn(2)
                gate(1)
                gate(2)
                pe.wait_ge(chosen_ok, 1)
                pe.wait_ge(const_ok, 5)
                banks.wait_free(pe, RANK)
                flat = "p t e -> p (t e)"
                pe.matmul(banks[RANK][0:P, 0:T * EXPERTS], earlier[:], chosen[:].rearrange(flat), start=True, stop=False)
                ins = pe.matmul(banks[RANK][0:P, 0:T * EXPERTS], keep.ones[0:P, 0:P], before[:, 0:T].rearrange(flat),
                                start=False, stop=True)
                banks.filled(ins, RANK)
                banks.wait_free(pe, RANK + 1)
                ins = pe.matmul(banks[RANK + 1][:, 0:EXPERTS], keep.ones[0:P, :], before[:, T], start=True, stop=True)
                banks.filled(ins, RANK + 1)

            @block.scalar
            def _(act):
                turned_out(act, banks, 0, o_t)
                for j in range(N - BANKS, N):
                    banks.wait_emptied(act, j)
                act.sem_inc(o_t_ok, 1)
                for q in range(len(QUADS)):
                    turned_out(act, banks, TURN[q] - C * q, t_t, quads=(q,))
                    for j in range(TURN[q], TURN[q] + C):
                        banks.wait_emptied(act, j)
                    act.sem_inc(o_t_ok, 1)
                act.wait_ge(shifted_ok, 1)
                act.activation(exps[:], exps[:], ACT.Exp).then_inc(exps_ok, 1)

            @block.vector
            def _(v):
                link = b.steps_of(v)
                v.wait_ge(w_in, 96)
                for t in range(T + 1):
                    if t < T:
                        y = keep.y[:, t]
                        j = proj(t)
                        v.wait_ge(bo_ok, t + 1)
                        banks.wait_full(v, j)
                        link(v.tensor_tensor(y, banks[j][0:P, :], y, ALU.add))
                        banks.release(v, j)
                        link(v.bn_stats(stats[:, t], y))
                        link(v.bn_aggr(mv[:, t], stats[:, t]))
                        v.tensor_scalar(var[:, t:t + 1], mv[:, t, 1:2], EPS, None, ALU.add).then_inc(var_ok, 1)
                    if t >= 1:
                        y = keep.y[:, t - 1]
                        v.wait_ge(rstd_ok, roots + t)
                        link(v.tensor_scalar(y, y, mv[:, t - 1, 0:1], rstd[:, t - 1:t], ALU.subtract, ALU.mult))
                        link(v.tensor_tensor(y, y, rows[:, 1], ALU.mult))
                        v.tensor_tensor(y, y, rows[:, 2], ALU.add).then_inc(t_ok, 1)
                wide = [P, T, EXPERTS]
                for q, (t0, n) in enumerate(QUADS):
                    banks.wait_full(v, GATE[q])
                    link(v.tensor_tensor(logits[:, t0:t0 + n], banks[GATE[q]][0:P, 0:n * EXPERTS].rearrange("p (t e) -> p t e", t=n),
                                         gate_b[:].unsqueeze(1).to_broadcast([P, n, EXPERTS]), ALU.add))
                    banks.release(v, GATE[q])
                link(v.tensor_reduce(best[:], logits[:], AX.X, ALU.max))
                v.tensor_tensor(exps[:], logits[:], best[:].unsqueeze(2).to_broadcast(wide), ALU.subtract).then_inc(shifted_ok, 1)
                link(v.tensor_tensor(chosen[:], logits[:], best[:].unsqueeze(2).to_broadcast(wide), ALU.is_equal))
                v.wait_ge(const_ok, 5)
                link(v.scalar_tensor_tensor(chosen[:], chosen[:], -float(EXPERTS), expert_no[:].unsqueeze(1).to_broadcast(wide),
                                            ALU.mult, ALU.add))
                link(v.tensor_reduce(best[:], chosen[:], AX.X, ALU.min))
                link(v.tensor_scalar(best[:], best[:], float(EXPERTS), None, ALU.add))
                link(v.tensor_tensor(chosen[:], expert_no[:].unsqueeze(1).to_broadcast(wide),
                                     best[:].unsqueeze(2).to_broadcast(wide), ALU.is_equal))
                link(v.memset(before[:, 0], 0.0))
                for t in range(T - 1):
                    link(v.tensor_tensor(before[:, t + 1], before[:, t], chosen[:, t], ALU.add))
                v.tensor_tensor(before[:, T], before[:, T - 1], chosen[:, T - 1], ALU.add).then_inc(chosen_ok, 1)
                v.wait_ge(exps_ok, 1)
                link(v.tensor_reduce(keep.gate[:], exps[:], AX.X, ALU.add))
                link(v.reciprocal(keep.gate[:], keep.gate[:]))
                banks.wait_full(v, RANK + 1)
                link(v.tensor_copy(counts[:], banks[RANK + 1][:, 0:EXPERTS]))
                link(v.tensor_tensor(over[:], counts[:].unsqueeze(2).to_broadcast([128, EXPERTS, J]),
                                     slot_steps[:].unsqueeze(1).to_broadcast([128, EXPERTS, J]), ALU.is_gt))
                link(v.tensor_reduce(n_slots[:], over[:], AX.X, ALU.add))
                link(v.tensor_tensor_scan(ends[:], keep.ones[:, 0:EXPERTS], n_slots[:], 0.0, ALU.mult, ALU.add))
                link(v.tensor_tensor(base[:], ends[:], n_slots[:], ALU.subtract))
                link(v.tensor_scalar(base[:], base[:], float(SLOT), None, ALU.mult))
                link(v.tensor_tensor(placed[:], banks[RANK][0:P, 0:T * EXPERTS].rearrange("p (t e) -> p t e", t=T),
                                     base[0:P].unsqueeze(1).to_broadcast(wide), ALU.add))
                link(v.tensor_tensor(placed[:], placed[:], chosen[:], ALU.mult))
                link(v.tensor_reduce(place[:], placed[:], AX.X, ALU.add))
                v.tensor_copy(keep.place[:], place[:]).then_inc(place_ok, 1)
                link(v.tensor_tensor(passed[:], slot_no[:].unsqueeze(2).to_broadcast([1, SLOTS + 1, EXPERTS]),
                                     ends[0:1].unsqueeze(1).to_broadcast([1, SLOTS + 1, EXPERTS]), ALU.is_ge))
                evens = passed[:, :, 1:7:2]
                odds = passed[:, :, 0:7:2]
                link(v.tensor_reduce(tables[:, 0], evens, AX.X, ALU.add))
                link(v.tensor_reduce(tables[:, 1], odds, AX.X, ALU.add))
                link(v.tensor_scalar(tables[:, 0], tables[:, 0], 1.0, None, ALU.add))
                link(v.tensor_tensor(tables[:, 2], tables[:, 1], tables[:, 0], ALU.subtract))
                link(v.tensor_scalar(tables[:, 2], tables[:, 2], 1.0, None, ALU.add))
                link(v.tensor_reduce(tables[:, 3], passed[:, :, 0:EXPERTS - 1], AX.X, ALU.add))
                link(v.tensor_copy(keep.slot_tables[:], tables[:]))
                link(v.tensor_copy(keep.slot_ends[:], ends[0:1]))


def experts(b, keep):
    nc, a = b.nc, b.a
    FB = FF // 128
    with ExitStack() as ctx:
        w1, w1_in, b1_rows, b1_in = keep.w1, keep.w1_in, keep.b1_rows, keep.b1_in
        w2 = b.sb(ctx, "w2", [128, 2, FB, D])
        b1 = b.sb(ctx, "b1", [128, EXPERTS, FB])
        b1_now = b.sb(ctx, "b1_now", [128, FB])

        def cut(free, *sizes):
            ends = [sum(sizes[:i + 1]) for i in range(len(sizes))]
            return [free[:, end - size:end] for end, size in zip(ends, sizes)]

        hid, rows_t, *rest = cut(keep.y_all, FF, D, *[D] * 4)
        rows_t = rows_t.rearrange("p (c n) -> p c n", c=C)
        rows, done = rest[:2], rest[2:]
        hid_t, b2 = cut(keep.o_all, FB * SLOT, 2 * D)
        hid_t = hid_t.rearrange("p (f n) -> p f n", f=FB)
        b2 = b2.rearrange("p (a d) -> p a d", a=2)
        up = b.ps(ctx, "up", [128, 2, 512])
        turned = b.ps(ctx, "hid_turned", [128, 4, 512])
        down = b.ps(ctx, "down", [128, 512])
        x_turned = b.ps(ctx, "x_turned", [128, 512])
        b1_turned = b.sem(ctx, "b1_turned")
        b1_ok = b.sem(ctx, "b1_ok")
        b1_now_ok = b.sem(ctx, "b1_now_ok")
        rows_in = [b.sem(ctx, f"rows_in{u}") for u in range(2)]
        w2_in = [b.sem(ctx, f"w2_in{u}") for u in range(2)]
        x_turned_ok = b.sem(ctx, "x_turned_ok")
        rows_t_ok = b.sem(ctx, "rows_t_ok")
        up_ok = b.sem(ctx, "up_ok")
        hid_ok = b.sem(ctx, "hid_ok")
        turned_ok = b.sem(ctx, "hid_turned_ok")
        gelu_ok = b.sem(ctx, "gelu_ok")
        down_ok = b.sem(ctx, "down_ok")
        done_ok = b.sem(ctx, "done_ok")
        done_out = [b.sem(ctx, f"done_out{u}") for u in range(2)]
        slots_in = keep.slots_in.rearrange("(s p) d -> s p d", p=SLOT)
        slots_out = keep.slots_out.rearrange("(s p) d -> s p d", p=SLOT)

        def table(eng, row, k):
            return eng.value_load(keep.slot_tables[0:1, row, bass.ds(k, 1)], min_val=0, max_val=(4, 4, 1, EXPERTS - 1)[row])

        with nc.Block() as block:

            @block.sync
            def _(sp):
                def load_w2(e, u):
                    sp.dma_start(w2[:, u], a["L0_ffn_W2"][bass.ds(e, 1)].rearrange("a (f p) d -> p (a f) d", p=128)).then_inc(w2_in[u], 16)
                    sp.dma_start(b2[:, u], a["L0_ffn_b2"][bass.ds(e, 1)].to_broadcast([128, D])).then_inc(w2_in[u], 16)

                sp.sem_inc(w2_in[1], 32)
                for u in range(2):
                    sp.wait_ge(rows_in[u], 16)
                load_w2(0, 0)
                load_w2(1, 1)
                with sp.Fori(1, EXPERTS // 2) as i:
                    for u in range(2):
                        end = sp.value_load(keep.slot_ends[0:1, bass.ds(2 * i + u - 2, 1)], min_val=0, max_val=SLOTS)
                        sp.wait_ge(up_ok, 4 * end + 4)
                        load_w1(b, keep, sp, 2 * i + u, u)
                        sp.wait_ge(done_ok, end + 1)
                        load_w2(2 * i + u, u)

            @block.tensor
            def _(pe):
                def turn_x(k, u, nth):
                    pe.wait_ge(rows_in[u], 16 * nth)
                    pe.wait_ge(rows_t_ok, k)
                    for c in range(C):
                        ins = pe.transpose(x_turned[:, SLOT * c:SLOT * c + SLOT], rows[u][:, 128 * c:128 * c + 128], keep.ident[:])
                    ins.then_inc(x_turned_ok, 1)

                def product_up(k):
                    even, odd, half = (table(pe, r, k) for r in range(3))
                    pe.wait_ge(w1_in[0], 16 * even)
                    pe.wait_ge(w1_in[1], 16 * odd + 16)
                    pe.wait_ge(rows_t_ok, k + 1)
                    w = w1[:, bass.ds(half, 1)].rearrange("p a c f -> p (a c) f")
                    for f in range(4):
                        if f >= 2:
                            pe.wait_ge(hid_ok, 4 * k + f - 1)
                        else:
                            pe.wait_ge(hid_ok, 4 * k)
                        for c in range(C):
                            ins = pe.matmul(up[:, f % 2], rows_t[:, c], w[:, c, 512 * f:512 * f + 512],
                                            start=(c == 0), stop=(c == C - 1))
                        ins.then_inc(up_ok, 1)

                def turn_hid(k):
                    for f in range(4):
                        pe.wait_ge(hid_ok, 4 * k + f + 1)
                        pe.wait_ge(gelu_ok, 4 * k)
                        for n in range(4):
                            ins = pe.transpose(turned[:, f, 128 * n:128 * n + 128],
                                               hid[:, 512 * f + 128 * n:512 * f + 128 * n + 128], keep.ident[:])
                        ins.then_inc(turned_ok, 1)

                def product_down(k):
                    even, odd, half = (table(pe, r, k) for r in range(3))
                    pe.wait_ge(w2_in[0], 32 * even)
                    pe.wait_ge(w2_in[1], 32 * odd + 32)
                    pe.wait_ge(gelu_ok, 4 * k + 4)
                    pe.wait_ge(done_ok, k + 1)
                    pe.wait_ge(b1_ok, 1)
                    w = w2[:, bass.ds(half, 1)].rearrange("p a f d -> p (a f) d")
                    for f in range(FB):
                        ins = pe.matmul(down[:], hid_t[:, f], w[:, f], start=(f == 0), stop=(f == FB - 1))
                    ins.then_inc(down_ok, 1)

                pe.sem_inc(up_ok, 4)
                pe.sem_inc(down_ok, 1)
                pe.wait_ge(b1_in, 16)
                pe.transpose(down[:, 0:128], b1_rows[:], keep.ident[:]).then_inc(b1_turned, 1)
                turn_x(0, 0, 1)
                product_up(0)
                turn_x(1, 1, 1)
                turn_hid(0)
                with pe.Fori(0, SLOTS // 2) as i:
                    for u in range(2):
                        k = 2 * i + 1 + u
                        product_up(k)
                        turn_x(k + 1, u, i + 2)
                        product_down(k - 1)
                        turn_hid(k)
                product_down(SLOTS - 1)

            @block.scalar
            def _(act):
                def load(k, u):
                    act.wait_ge(x_turned_ok, k - 1)
                    act.dma_start(rows[u], slots_in[bass.ds(k, 1)].rearrange("a p d -> p (a d)")).then_inc(rows_in[u], 16)

                def store(k, u):
                    act.wait_ge(done_ok, k + 2)
                    act.dma_start(slots_out[bass.ds(k, 1)].rearrange("a p d -> p (a d)"), done[u]).then_inc(done_out[u], 16)

                def gelu(k):
                    act.wait_ge(b1_now_ok, k + 1)
                    for f in range(FB):
                        if f % 4 == 0:
                            act.wait_ge(turned_ok, 4 * k + f // 4 + 1)
                            act.wait_ge(down_ok, k + 1)
                        ins = act.activation(hid_t[:, f], turned[:, f // 4, 128 * (f % 4):128 * (f % 4) + 128],
                                             ACT.Gelu_apprx_tanh,
                                             bias=b1_now[:, f:f + 1])
                        if f % 4 == 3:
                            ins.then_inc(gelu_ok, 1)

                for k in range(2):
                    act.sem_inc(done_out[k], 16)
                    act.dma_start(rows[k], slots_in[k]).then_inc(rows_in[k], 16)
                load(2, 0)
                gelu(0)
                load(3, 1)
                with act.Fori(0, (SLOTS - 3) // 2) as i:
                    for u in range(2):
                        k = 2 * i + 1 + u
                        gelu(k)
                        store(k - 1, u)
                        load(k + 3, u)
                for k in range(SLOTS - 2, SLOTS):
                    gelu(k)
                    store(k - 1, (k - 1) % 2)
                store(SLOTS - 1, (SLOTS - 1) % 2)
                act.wait_ge(done_out[0], 16 * (SLOTS // 2 + 2))
                act.wait_ge(done_out[1], 16 * (SLOTS // 2 + 1))

            @block.vector
            def _(v):
                def turned_in(k):
                    v.wait_ge(x_turned_ok, k + 1)
                    v.wait_ge(up_ok, 4 * k + 4)
                    v.tensor_copy(rows_t, x_turned[:].rearrange("p (c n) -> p c n", c=C)).then_inc(rows_t_ok, 1)

                def hidden(k):
                    for f in range(4):
                        v.wait_ge(up_ok, 4 * k + f + 5)
                        v.wait_ge(turned_ok, 4 * k)
                        v.tensor_copy(hid[:, 512 * f:512 * f + 512], up[:, f % 2]).then_inc(hid_ok, 1)
                    e = table(v, 3, k)
                    v.wait_ge(gelu_ok, 4 * k)
                    v.tensor_scalar(b1_now[:], b1[:, bass.ds(e, 1)].rearrange("p a f -> p (a f)"), 1.0, None, ALU.mult
                                    ).then_inc(b1_now_ok, 1)

                def finish(k, u, nth):
                    half = table(v, 2, k)
                    v.wait_ge(down_ok, k + 2)
                    v.wait_ge(done_out[u], 16 * nth)
                    v.tensor_tensor(done[u], down[:], b2[:, bass.ds(half, 1)].rearrange("p a d -> p (a d)"), ALU.add
                                    ).then_inc(done_ok, 1)

                v.sem_inc(done_ok, 1)
                v.wait_ge(b1_turned, 1)
                v.tensor_copy(b1[:].rearrange("p e f -> p (e f)"), down[:, 0:128]).then_inc(b1_ok, 1)
                turned_in(0)
                v.wait_ge(b1_ok, 1)
                hidden(0)
                turned_in(1)
                with v.Fori(0, SLOTS // 2) as i:
                    for u in range(2):
                        k = 2 * i + 1 + u
                        hidden(k)
                        turned_in(k + 1)
                        finish(k - 1, u, i + 1)
                finish(SLOTS - 1, (SLOTS - 1) % 2, SLOTS // 2 + 1)


def gat_inputs(b, keep):
    nc, a = b.nc, b.a
    with ExitStack() as ctx:
        got = keep.worth[:, :, 0:D]
        a_w = b.sb(ctx, "a_w", [128, HEADS, 2, HD])
        w_a = b.sb(ctx, "w_a", [128, C, 2 * HEADS])
        a_rows = b.sb(ctx, "a_rows", [2 * HEADS, HD])
        b_rows = b.sb(ctx, "b_rows", [2 * HEADS, HD])
        a_b = b.sb(ctx, "a_b", [2 * HEADS, 1])
        bias = b.sb(ctx, "halves_bias", [2 * HEADS, 1])
        prod = b.sb(ctx, "prod", [128, HEADS, HD])
        stats = b.sb(ctx, "gat_stats", [P, T, 6])
        mv = b.sb(ctx, "gat_mv", [P, T, 2])
        var = b.sb(ctx, "gat_var", [P, T])
        rstd = b.sb(ctx, "gat_rstd", [P, T])
        halves_t = b.sb(ctx, "halves_t", [2 * HEADS, NODES])
        banks = Banks(b, ctx, "gat_banks")
        w_in = keep.gat_w_in
        a_in = b.sem(ctx, "a_in")
        got_in = [b.sem(ctx, f"got_in{q}") for q in range(len(QUADS))]
        var_ok, rstd_ok, roots = b.roots(len(QUADS))
        y2_ok = b.sem(ctx, "y2_ok")
        y2_t_ok = b.sem(ctx, "y2_t_ok")
        w_a_ok = b.sem(ctx, "w_a_ok")
        halves_t_ok = b.sem(ctx, "halves_t_ok")
        halves_out = b.sem(ctx, "halves_out")
        N = C * len(QUADS)
        BACK = N + len(QUADS)
        with nc.Block() as block:

            @block.sync
            def _(sp):
                for c in range(C):
                    sp.dma_start(keep.w_s[:, c], a["L1_gnn_Ws"][:, 128 * c:128 * c + 128, :].rearrange("h p e -> p h e")).then_inc(w_in, 16)
                sp.dma_start(a_w[:].rearrange("p h k e -> p (h k e)"),
                             a["L1_gnn_a_w"].rearrange("(a h) e -> a (h e)", a=1).to_broadcast([128, 2 * D])).then_inc(a_in, 16)
                for k in range(2):
                    rows = slice(HEADS * k, HEADS * k + HEADS)
                    sp.dma_start(a_rows[rows, :], a["L1_gnn_a_w"][:, HD * k:HD * k + HD]).then_inc(a_in, 16)
                    sp.dma_start(b_rows[rows, :], a["L1_gnn_Wb"]).then_inc(a_in, 16)
                sp.dma_start(a_b[0:HEADS, :], a["L1_gnn_a_b"].unsqueeze(1), allow_slow_non_contiguous=True).then_inc(a_in, 16)
                sp.dma_start(keep.w_b[:].rearrange("p h e -> p (h e)"),
                             a["L1_gnn_Wb"].rearrange("(a h) e -> a (h e)", a=1).to_broadcast([P, D])).then_inc(w_in, 16)
                for q, (t0, n) in enumerate(QUADS):
                    sp.wait_ge(got_in[q], 16 * n)
                for t in range(T):
                    sp.dma_start(keep.no_edge[:, t], keep.absent[P * t:P * t + P, :]).then_inc(keep.absent_in, 16)
                sp.wait_ge(halves_t_ok, len(QUADS))
                sp.dma_start(keep.halves, halves_t[:]).then_inc(halves_out, 16)
                sp.wait_ge(halves_out, 16)

            @block.gpsimd
            def _(pool):
                for q, (t0, n) in enumerate(QUADS):
                    for t in range(t0, t0 + n):
                        pool.indirect_dma_start(out=got[:, t], out_offset=None, in_=keep.slots_out,
                                                in_offset=bass.IndirectOffsetOnAxis(ap=keep.place[:, t:t + 1], axis=0)).then_inc(got_in[q], 16)
                for q, (t0, n) in enumerate(QUADS):
                    pool.wait_ge(var_ok, roots + q + 1)
                    variance_root(pool, rstd[:, t0:t0 + n], var[:, t0:t0 + n], keep.minus_half[0:P, 0:n]).then_inc(rstd_ok, 1)

            @block.tensor
            def _(pe):
                turn_rows(pe, banks, 0, keep.y, keep.ident, y2_ok)
                pe.wait_ge(w_a_ok, 2 * C + 1)
                pe.wait_ge(y2_t_ok, 1)
                for q, (t0, n) in enumerate(QUADS):
                    banks.wait_free(pe, N + q)
                    for c in range(C):
                        ins = pe.matmul(banks[N + q][0:2 * HEADS, 0:P * n], w_a[:, c], keep.y_t[:, c, P * t0:P * (t0 + n)],
                                        start=(c == 0), stop=(c == C - 1))
                    banks.filled(ins, N + q)
                pe.wait_ge(halves_t_ok, len(QUADS))
                banks.wait_free(pe, BACK)
                for t in range(T):
                    ins = pe.transpose(banks[BACK][0:P, 2 * HEADS * t:2 * HEADS * (t + 1)], halves_t[:, P * t:P * t + P],
                                       keep.ident[0:2 * HEADS, 0:2 * HEADS])
                banks.filled(ins, BACK)

            @block.scalar
            def _(act):
                turned_out(act, banks, 0, keep.y_t)
                for j in range(N - BANKS, N):
                    banks.wait_emptied(act, j)
                act.sem_inc(y2_t_ok, 1)
                act.wait_ge(w_a_ok, 2 * C + 1)
                for q, (t0, n) in enumerate(QUADS):
                    banks.wait_full(act, N + q)
                    act.activation(halves_t[:, P * t0:P * (t0 + n)], banks[N + q][0:2 * HEADS, 0:P * n], ACT.Identity, bias=bias[:]
                                   ).then_inc(halves_t_ok, 1)
                    act.wait_ge(halves_t_ok, q + 1)
                    banks.release(act, N + q)

            @block.vector
            def _(v):
                link = b.steps_of(v)
                v.memset(keep.w[:, :, :, HD:HD + 1], 1.0)
                v.wait_ge(a_in, 16 * 6)
                v.wait_ge(w_in, 16 * (C + 1))
                for c in range(C):
                    for k in range(2):
                        link(v.tensor_tensor(prod[:], keep.w_s[:, c], a_w[:, :, k], ALU.mult))
                        v.tensor_reduce(w_a[:, c, HEADS * k:HEADS * k + HEADS], prod[:], AX.X, ALU.add).then_inc(w_a_ok, 1)
                        v.wait_ge(w_a_ok, 2 * c + k + 1)
                link(v.tensor_tensor(b_rows[:], b_rows[:], a_rows[:], ALU.mult))
                link(v.tensor_reduce(bias[:], b_rows[:], AX.X, ALU.add))
                v.tensor_tensor(bias[0:HEADS, :], bias[0:HEADS, :], a_b[0:HEADS, :], ALU.add).then_inc(w_a_ok, 1)
                for q, (t0, n) in enumerate(QUADS):
                    v.wait_ge(got_in[q], 16 * n)
                    tiles = range(t0, t0 + n)
                    for t in tiles:
                        ins = v.scalar_tensor_tensor(keep.res[:, t], got[:, t], keep.gate[:, t:t + 1], keep.res[:, t], ALU.mult, ALU.add)
                    link(ins)
                    for t in tiles:
                        ins = v.bn_stats(stats[:, t], keep.res[:, t])
                    link(ins)
                    for t in tiles:
                        ins = v.bn_aggr(mv[:, t], stats[:, t])
                    link(ins)
                    v.tensor_scalar(var[:, t0:t0 + n], mv[:, t0:t0 + n, 1], EPS, None, ALU.add).then_inc(var_ok, 1)
                    v.wait_ge(rstd_ok, roots + q + 1)
                    for t in tiles:
                        ins = v.tensor_scalar(keep.y[:, t], keep.res[:, t], mv[:, t, 0:1], rstd[:, t:t + 1], ALU.subtract, ALU.mult)
                    ins.then_inc(y2_ok, 1)
                banks.wait_full(v, BACK)
                link(v.tensor_copy(keep.halves_p[:].rearrange("p t k -> p (t k)"), banks[BACK][0:P, 0:2 * HEADS * T]))
                banks.release(v, BACK)


def gat_max(b, keep):
    nc = b.nc
    with ExitStack() as ctx:
        src = b.sb(ctx, "src_halves", [P, 2, NODES])
        masked = b.sb(ctx, "masked", [P, 2, NODES], BF16)
        top = b.sb(ctx, "gat_top", [P, T, HEADS])
        shifts = b.sb(ctx, "shifts", [P, T, 2, HEADS])
        shifts_t = b.sb(ctx, "shifts_t", [2 * HEADS, NODES])
        banks = Banks(b, ctx, "max_banks")
        src_in = [b.sem(ctx, f"src_in{u}") for u in range(2)]
        top_ok = b.sem(ctx, "top_ok")
        shifts_ok = b.sem(ctx, "shifts_ok")
        shifts_t_ok = b.sem(ctx, "shifts_t_ok")
        shifts_out = b.sem(ctx, "shifts_out")
        products_ok = b.sem(ctx, "w_products_ok")
        with nc.Block() as block:

            @block.sync
            def _(sp):
                for h in range(HEADS):
                    if h >= 2:
                        sp.wait_ge(top_ok, T * (h - 1))
                    sp.dma_start(src[:, h % 2], keep.halves[HEADS + h:HEADS + h + 1, :].to_broadcast([P, NODES])).then_inc(src_in[h % 2], 16)
                    if h == 1:
                        sp.dma_start(keep.worth[:], keep.worth_rows.rearrange("(t p) n -> p t n", p=P)).then_inc(keep.worth_in, 16)
                sp.wait_ge(shifts_t_ok, len(QUADS))
                sp.dma_start(keep.shifts, shifts_t[:]).then_inc(shifts_out, 16)
                sp.wait_ge(shifts_out, 16)
                sp.wait_ge(keep.worth_in, 16)

            @block.gpsimd
            def _(pool):
                for t in range(T):
                    pool.wait_ge(products_ok, t + 1)
                    w = keep.w[:, t, :, 0:HD]
                    pool.tensor_tensor(w, w, keep.w_b[:], ALU.add)

            @block.tensor
            def _(pe):
                for t in range(T):
                    banks.wait_free(pe, t)
                    for c in range(C):
                        ins = pe.matmul(banks[t][0:P, :], keep.y_t[:, c, P * t:P * t + P], keep.w_s[:, c].rearrange("p h e -> p (h e)"),
                                        start=(c == 0), stop=(c == C - 1))
                    banks.filled(ins, t)
                pe.wait_ge(shifts_ok, 1)
                for q, (t0, n) in enumerate(QUADS):
                    banks.wait_free(pe, T + q)
                    for t in range(n):
                        ins = pe.transpose(banks[T + q][0:2 * HEADS, P * t:P * t + P],
                                           shifts[:, t0 + t].rearrange("p k h -> p (k h)"), keep.ident[0:P, 0:P])
                    banks.filled(ins, T + q)

            @block.scalar
            def _(act):
                for t in range(T):
                    banks.wait_full(act, t)
                    act.activation(keep.w[:, t, :, 0:HD], banks[t][0:P, :].rearrange("p (h e) -> p h e", h=HEADS), ACT.Copy
                                   ).then_inc(products_ok, 1)
                    act.wait_ge(products_ok, t + 1)
                    banks.release(act, t)
                for q, (t0, n) in enumerate(QUADS):
                    banks.wait_full(act, T + q)
                    act.activation(shifts_t[:, P * t0:P * (t0 + n)], banks[T + q][0:2 * HEADS, 0:P * n], ACT.Copy).then_inc(shifts_t_ok, 1)
                    act.wait_ge(shifts_t_ok, q + 1)
                    banks.release(act, T + q)

            @block.vector
            def _(v):
                link = b.steps_of(v)
                v.wait_ge(keep.absent_in, 16 * T)
                for h in range(HEADS):
                    v.wait_ge(src_in[h % 2], 16 * (h // 2 + 1))
                    for t in range(T):
                        n = T * h + t
                        if n >= 2:
                            v.wait_ge(top_ok, n - 1)
                        v.tensor_tensor_reduce(out=masked[:, n % 2], in0=keep.no_edge[:, t], in1=src[:, h % 2], scale=1.0, scalar=LOWEST,
                                               op0=ALU.add, op1=ALU.max, accum_out=top[:, t, h:h + 1]).then_inc(top_ok, 1)
                v.wait_ge(top_ok, T * HEADS)
                own = keep.halves_p[:, :, 0:HEADS]
                link(v.tensor_tensor(top[:], top[:], own, ALU.add))
                link(v.scalar_tensor_tensor(top[:], top[:], SLOPE, top[:], ALU.mult, ALU.max))
                link(v.tensor_tensor(shifts[:, :, 0], top[:], own, ALU.subtract))
                link(v.scalar_tensor_tensor(shifts[:, :, 1], own, -SLOPE, top[:], ALU.mult, ALU.add))
                v.tensor_scalar(keep.minus_src[:, :, 0], keep.halves_p[:, :, HEADS:2 * HEADS], -1.0, None, ALU.mult)
                v.tensor_scalar(keep.minus_src[:, :, 1], keep.halves_p[:, :, HEADS:2 * HEADS], -SLOPE, None, ALU.mult)
                v.sem_inc(shifts_ok, 1)


def gat(b, keep):
    nc = b.nc
    HALF = T // 2
    WIDE = HD + 1
    RING = 5
    AHEAD = 3
    LATE = 7
    U = 2 * T
    TURNS = HEADS // 2
    POOLED = (1, 3, 6, 8, 11, 13, 16, 18)

    def worthy(i, j):
        more, j = divmod(j, U)
        pooled = j in POOLED
        mine = [k for k in range(U) if (k in POOLED) == pooled]
        return pooled, len(mine) * (i + more) + mine.index(j)

    with ExitStack() as ctx:
        rows = b.sb(ctx, "shift_rows", [P, 2, 2, NODES])
        far = b.sb(ctx, "far", [P, RING, NODES])
        weight = b.sb(ctx, "weight", [P, 2, NODES])
        share = b.sb(ctx, "gat_share", [P, T])
        mean = b.sb(ctx, "gat_mean", [P, T, HD])
        minus_now = b.sb(ctx, "minus_now", [P, 2, T, 2])
        w_now = b.sb(ctx, "w_now", [P, 2, T, WIDE])
        sums_t = b.sb(ctx, "sums_t", [WIDE, NODES])
        sums = b.ps(ctx, "gat_sums", [128, 2, 3 * 512])
        back = b.ps(ctx, "sums_back", [128, 2, 512])
        w_now_ok = b.sem(ctx, "w_now_ok")
        sums_out = b.sem(ctx, "sums_out")
        back_ok = b.sem(ctx, "sums_back_ok")
        rows_in = [b.sem(ctx, f"shift_rows_in{u}") for u in range(2)]
        minus_ok = b.sem(ctx, "minus_ok")
        far_ok = b.sem(ctx, "far_ok")
        near_ok = b.sem(ctx, "near_ok2")
        worthy_ok = [b.sem(ctx, f"worthy_ok_{name}") for name in ("vector", "pool")]
        weight_ok = b.sem(ctx, "weight_ok")
        summed = b.sem(ctx, "gat_summed")
        head_ok = b.sem(ctx, "head_ok")
        step = b.sem(ctx, "gat_v_step")

        with nc.Block() as block:

            @block.sync
            def _(sp):
                def load(h, u):
                    for k in range(2):
                        sp.dma_start(rows[:, u, k], keep.shifts[bass.ds(HEADS * k + h, 1), :].to_broadcast([P, NODES])).then_inc(rows_in[u], 16)

                load(0, 0)
                load(1, 1)
                w = b.a["L1_ffn_W"]
                sp.dma_start(keep.m_rows[:], w[:, 0:128, :].rearrange("l e d -> e l d")).then_inc(keep.m_in, 16)
                sp.dma_start(keep.m_rows_hi[:], w[:, 128:, :].rearrange("l e d -> e l d")).then_inc(keep.m_in, 16)
                with sp.Fori(1, TURNS) as i:
                    for u in range(2):
                        sp.wait_ge(near_ok, U * i + T * (u - 1))
                        load(2 * i + u, u)

            @block.scalar
            def _(act):
                def line(i, j):
                    u, s = divmod(j, T)
                    if s == 0:
                        act.wait_ge(rows_in[u], 32 * i + 32)
                        act.wait_ge(minus_ok, 2 * i + u + 1)
                    act.activation(far[:, j % RING], rows[:, u, 1], ACT.Identity, bias=minus_now[:, u, s, 1:2]).then_inc(far_ok, 1)

                def values(h, u):
                    act.activation(w_now[:, u], keep.w[:, :, bass.ds(h, 1), :].rearrange("p t a e -> p t (a e)"), ACT.Copy
                                   ).then_inc(w_now_ok, 1)

                def take(i, u):
                    h = 2 * i + u
                    act.wait_ge(summed, 2 + T * h + T)
                    act.wait_ge(back_ok, h + 1)
                    act.activation(sums_t[:], sums[0:WIDE, u, 0:NODES], ACT.Copy).then_inc(sums_out, 1)

                def weights(i, steps):
                    for j in steps:
                        n = U * i + j
                        if n_left(i, j) > AHEAD:
                            act.wait_ge(weight_ok, n + AHEAD - RING + 3)
                            ahead, j_ahead = divmod(j + AHEAD, U)
                            line(i + ahead, j_ahead)
                        pooled, nth = worthy(i, j)
                        act.wait_ge(worthy_ok[pooled], nth + 1)
                        act.wait_ge(summed, n + 1)
                        act.activation(weight[:, j % 2], far[:, j % RING], ACT.Exp, scale=-1.0).then_inc(weight_ok, 1)
                        if j in (T + 2, U + 2):
                            u = j // T - 1
                            take(i, u)
                            if n_left(i, j) > T:
                                values(2 * i + 2 + u, u)

                def n_left(i, j):
                    return U * (TURNS - i) - j if isinstance(i, int) else U

                act.sem_inc(weight_ok, 2)
                for u in range(2):
                    values(u, u)
                for j in range(AHEAD):
                    line(0, j)
                weights(0, range(LATE))
                with act.Fori(0, TURNS - 1) as i:
                    weights(i, range(LATE, U + LATE))
                weights(TURNS - 1, range(LATE, U))
                take(TURNS - 1, 1)

            @block.tensor
            def _(pe):
                def turn_back(i, u):
                    h = 2 * i + u
                    pe.wait_ge(sums_out, h + 3)
                    pe.wait_ge(head_ok, h + 1)
                    for t in range(T):
                        ins = pe.transpose(back[0:P, t // HALF, WIDE * (t % HALF):WIDE * (t % HALF) + WIDE],
                                           sums_t[:, P * t:P * t + P], keep.ident[0:WIDE, 0:WIDE])
                    ins.then_inc(back_ok, 1)

                def products(i, steps):
                    for j in steps:
                        u, s = divmod(j % U, T)
                        n = U * i + j
                        if s == 0:
                            h = 2 * i + j // T
                            pe.wait_ge(sums_out, h + 1)
                            pe.wait_ge(w_now_ok, h + 1)
                        pe.wait_ge(weight_ok, n + 3)
                        for c0, w in COLS:
                            ins = pe.matmul(sums[0:WIDE, u, c0:c0 + w], w_now[:, u, s], weight[:, j % 2, c0:c0 + w],
                                            start=(s == 0), stop=(s == T - 1))
                        ins.then_inc(summed, 1)
                        if j in (T + 3, U + 3):
                            turn_back(i, j // T - 1)

                pe.sem_inc(summed, 2)
                pe.sem_inc(sums_out, 2)
                pe.sem_inc(back_ok, 1)
                products(0, range(LATE))
                with pe.Fori(0, TURNS - 1) as i:
                    products(i, range(LATE, U + LATE))
                products(TURNS - 1, range(LATE, U))
                turn_back(TURNS - 1, 1)

            @block.gpsimd
            def _(pool):
                with pool.Fori(0, TURNS) as i:
                    for j in POOLED:
                        pool.wait_ge(near_ok, U * i + j + 1)
                        to = far[:, j % RING]
                        pool.tensor_tensor(to, to, keep.worth[:, j % T], ALU.add).then_inc(worthy_ok[1], 1)

            @block.vector
            def _(v):
                def minus(h, u):
                    v.tensor_scalar(minus_now[:, u], keep.minus_src[:, :, :, bass.ds(h, 1)].rearrange("p t k a -> p t (k a)"),
                                    1.0, None, ALU.mult).then_inc(minus_ok, 1)

                def near(i, j):
                    u, s = divmod(j, T)
                    v.wait_ge(far_ok, U * i + j + 1)
                    to = far[:, j % RING]
                    v.scalar_tensor_tensor(to, rows[:, u, 0], minus_now[:, u, s, 0:1], to, ALU.add, ALU.min).then_inc(near_ok, 1)

                def unit(i, j, last=False):
                    n = U * i + j
                    if not last:
                        if j + 1 < U:
                            near(i, j + 1)
                        else:
                            near(i + 1, j + 1 - U)
                    if not worthy(i, j)[0]:
                        v.wait_ge(near_ok, n + 1)
                        to = far[:, j % RING]
                        v.tensor_tensor(to, to, keep.worth[:, j % T], ALU.add).then_inc(worthy_ok[0], 1)

                def finish(i, u, link):
                    h = 2 * i + u
                    v.wait_ge(back_ok, h + 2)
                    for k in range(2):
                        part = back[0:P, k, 0:WIDE * HALF].rearrange("p (t e) -> p t e", t=HALF)
                        link(v.tensor_scalar(share[:, HALF * k:HALF * k + HALF], part[:, :, HD], 1e-30, None, ALU.max))
                    link(v.reciprocal(share[:], share[:]))
                    for k in range(2):
                        part = back[0:P, k, 0:WIDE * HALF].rearrange("p (t e) -> p t e", t=HALF)
                        link(v.tensor_tensor(mean[:, HALF * k:HALF * k + HALF], part[:, :, 0:HD],
                                             share[:, HALF * k:HALF * k + HALF].unsqueeze(2).to_broadcast([P, HALF, HD]), ALU.mult))
                    to = keep.res[:, :, bass.ds(HD * h, HD)]
                    link(v.tensor_tensor(to, mean[:], to, ALU.add))
                    v.sem_inc(head_ok, 1)

                def both(i, link, last=False):
                    for j in range(LATE, U if last else U + LATE):
                        if j in (T + LATE - 1, U + LATE - 1):
                            finish(i, j // T - 1, link)
                        if j == T + LATE and not last:
                            v.wait_ge(far_ok, U * i + T)
                            v.wait_ge(near_ok, U * i + T)
                            minus(2 * i + 2, 0)
                        if j == U + LATE - 1:
                            minus(2 * i + 3, 1)
                        unit(i, j, last and j == U - 1)
                    if last:
                        finish(i, 1, link)

                v.sem_inc(head_ok, 1)
                minus(0, 0)
                minus(1, 1)
                near(0, 0)
                for j in range(LATE):
                    unit(0, j)
                PER_TURN = 12
                with v.Fori(0, TURNS - 1) as i:
                    link = Steps(v, step, base=PER_TURN * i)
                    both(i, link)
                    assert link.n == PER_TURN
                both(TURNS - 1, Steps(v, step, base=PER_TURN * (TURNS - 1)), last=True)


def last_mlp(b, keep):
    nc, a = b.nc, b.a
    G = 160
    HI = G - 128
    L = 7
    MARKS, OUT0, OP = 64, 128, 29
    COLS2 = 2 * NODES
    BLOCKS = 128 // HI
    WIDE = COLS2 // BLOCKS
    PIECES = ((0, (WIDE + 1) // 2), ((WIDE + 1) // 2, WIDE // 2))
    ROUND = 1.5 * 2 ** 23
    with ExitStack() as ctx:
        w_rows, w_rows_hi = keep.m_rows, keep.m_rows_hi
        again = b.sb(ctx, "m_again", [128, L, BLOCKS, HI])
        again_hi = b.sb(ctx, "m_again_hi", [HI, L, BLOCKS, HI])
        w_t = b.sb(ctx, "m_t", [128, L, G])
        w_from_hi = b.sb(ctx, "m_from_hi", [128, L, BLOCKS, 128])
        w_hi_hi = b.sb(ctx, "m_hi_hi", [128, L, BLOCKS, HI])
        block_of = b.sb(ctx, "block_of", [128, BLOCKS])
        w_last_hi = b.sb(ctx, "m_last_hi", [128, BLOCKS])
        w_first = b.sb(ctx, "m_first", [3, G])
        w_last = b.sb(ctx, "m_last", [128, 2])
        bias = b.sb(ctx, "m_bias", [128, 2, L])
        bias_last = b.sb(ctx, "m_bias_last", [P, 1])
        marks = b.sb(ctx, "marks", [P, T, 4, 16])
        weigh = b.sb(ctx, "weigh", [P, 16])
        sixteen = b.sb(ctx, "sixteen", [P, 16])
        high = b.sb(ctx, "high", [P, T, 4])
        seen = b.sb(ctx, "seen", [P, T, 4])
        feats = b.sb(ctx, "feats", [P, T, 2, 3])
        feats_t = b.sb(ctx, "feats_t", [3, 2, NODES])
        lo = b.sb(ctx, "h_lo", [128, 2, COLS2])
        hi = b.sb(ctx, "h_hi", [128, 2, WIDE])
        asked = b.sb(ctx, "asked", [P, T, 2])
        mask = b.sb(ctx, "mask", [P, T])
        result = b.sb(ctx, "result", [P, 2, T])
        hot = b.sb(ctx, "hot", [P, T, 2, 16])
        stats = b.sb(ctx, "m_stats", [P, T, 6])
        mv = b.sb(ctx, "m_mv", [P, T, 2])
        var = b.sb(ctx, "m_var", [P, T])
        rstd = b.sb(ctx, "m_rstd", [P, T])
        banks = Banks(b, ctx, "m_banks")
        w_in = b.sem(ctx, "m_w_in")
        const_ok = b.sem(ctx, "m_const_ok")
        var_ok, rstd_ok, roots = b.roots(1)
        feats_ok = b.sem(ctx, "feats_ok")
        feats_t_ok = b.sem(ctx, "feats_t_ok")
        w_t_ok = b.sem(ctx, "m_t_ok")
        w_hi_ok = b.sem(ctx, "m_hi_ok")
        last_ok = b.sem(ctx, "m_last_ok")
        again_ok = b.sem(ctx, "again_ok")
        layer_a = b.sem(ctx, "layer_a")
        layer_v = b.sem(ctx, "layer_v")
        sum_ok = b.sem(ctx, "sum_ok")
        out_ok = b.sem(ctx, "rows_ok")
        out_sent = b.sem(ctx, "out_sent")
        W = L - 2
        F0 = 2 * W
        M0 = F0 + 2 * len(QUADS)
        LAST = M0 + (BLOCKS + 1) * len(PIECES) * (W + 1)

        def job(l, x, block):
            return M0 + (BLOCKS + 1) * (len(PIECES) * l + x) + block

        def done(l, x):
            return len(PIECES) * l + x + 1

        N_IN = 5 + 2 * BLOCKS
        with nc.Block() as stage:

            @stage.sync
            def _(sp):
                slow = dict(allow_slow_non_contiguous=True)
                w = a["L1_ffn_W"]
                sp.dma_start(w_first[0:2], w[0, :, 0:2].rearrange("e d -> d e"), **slow).then_inc(w_in, 16)
                sp.dma_start(w_first[2:3], w[0, :, 30:31].rearrange("e d -> d e"), **slow).then_inc(w_in, 16)
                sp.dma_start(w_last[:, 0:1], w[L - 1, 2, 0:128].unsqueeze(1), **slow).then_inc(w_in, 16)
                bb = a["L1_ffn_b"]
                sp.dma_start(bias[:, 0], bb[:, 0:128].rearrange("l e -> e l"), **slow).then_inc(w_in, 16)
                for block in range(BLOCKS):
                    rows = slice(HI * block, HI * block + HI)
                    sp.dma_start(w_last[rows, 1:2], w[L - 1, 2, 128:G].unsqueeze(1), **slow).then_inc(w_in, 16)
                    sp.dma_start(bias[rows, 1], bb[:, 128:G].rearrange("l e -> e l"), **slow).then_inc(w_in, 16)
                sp.dma_start(bias_last[:], bb[L - 1:L, 2:3].to_broadcast([P, 1]), **slow).then_inc(w_in, 16)
                rows_of = b.out.rearrange("(t p) d -> p t d", p=P)
                sp.wait_ge(sum_ok, 1)
                for c in (slice(0, OUT0), slice(OUT0 + 32, D)):
                    sp.dma_start(rows_of[:, :, c], keep.res[:, :, c]).then_inc(out_sent, 16)
                sp.wait_ge(out_ok, 1)
                c = slice(OUT0, OUT0 + 32)
                sp.dma_start(rows_of[:, :, c], keep.res[:, :, c]).then_inc(out_sent, 16)
                sp.wait_ge(out_sent, 48)

            @stage.gpsimd
            def _(pool):
                iota = dict(channel_multiplier=0, allow_small_or_imprecise_dtypes=True)
                pool.iota(weigh[:], [[-1, 16]], base=16, **iota).then_inc(const_ok, 1)
                pool.iota(sixteen[:], [[1, 16]], base=0, **iota).then_inc(const_ok, 1)
                pool.memset(block_of[:], 0.0).then_inc(const_ok, 1)
                pool.wait_ge(const_ok, 3)
                for block in range(BLOCKS):
                    pool.memset(block_of[HI * block:HI * block + HI, block:block + 1], 1.0).then_inc(const_ok, 1)
                pool.wait_ge(const_ok, 3 + BLOCKS)
                pool.wait_ge(keep.m_in, 32)
                for block in range(BLOCKS):
                    pool.tensor_copy(again[:, 1:W + 1, block], w_rows[:, 1:W + 1, 128:G]).then_inc(again_ok, 1)
                    pool.tensor_copy(again_hi[:, 1:W + 1, block], w_rows_hi[:, 1:W + 1, 128:G]).then_inc(again_ok, 1)
                pool.wait_ge(var_ok, roots + 1)
                variance_root(pool, rstd[:], var[:], keep.minus_half[0:P, 0:T]).then_inc(rstd_ok, 1)
                pool.wait_ge(feats_ok, 1)
                pool.tensor_tensor(keep.res[:], keep.res[:], keep.y, ALU.add).then_inc(sum_ok, 1)

            @stage.tensor
            def _(pe):
                pe.wait_ge(keep.m_in, 32)
                pe.wait_ge(again_ok, 2 * BLOCKS)
                for l in range(W):
                    banks.wait_free(pe, 2 * l)
                    pe.transpose(banks[2 * l][:, 0:128], w_rows[:, l + 1, 0:128], keep.ident[:])
                    ins = pe.transpose(banks[2 * l][:, 128:G], w_rows_hi[:, l + 1, 0:128], keep.ident[0:HI, 0:HI])
                    banks.filled(ins, 2 * l)
                    banks.wait_free(pe, 2 * l + 1)
                    pe.transpose(banks[2 * l + 1][:, 0:128], again[:, l + 1].rearrange("e b d -> e (b d)"), keep.ident[:])
                    ins = pe.transpose(banks[2 * l + 1][:, 128:G], again_hi[:, l + 1].rearrange("e b d -> e (b d)"),
                                       keep.ident[0:HI, 0:HI])
                    banks.filled(ins, 2 * l + 1)
                pe.wait_ge(feats_ok, 1)
                for p in range(2):
                    for q, (t0, n) in enumerate(QUADS):
                        j = F0 + 3 * p + q
                        banks.wait_free(pe, j)
                        for t in range(n):
                            ins = pe.transpose(banks[j][0:3, P * t:P * t + P], feats[:, t0 + t, p], keep.ident[0:P, 0:P])
                        banks.filled(ins, j)
                f = feats_t[:].rearrange("f p n -> f (p n)")
                pe.wait_ge(feats_t_ok, 2 * len(QUADS))
                pe.wait_ge(w_t_ok, W)
                pe.wait_ge(w_hi_ok, W)
                pe.wait_ge(last_ok, 1)
                pe.wait_ge(w_in, 16 * N_IN)
                for l in range(W + 1):
                    for x, (c0, n) in enumerate(PIECES):
                        if l:
                            pe.wait_ge(layer_a, 3 * done(l - 1, x))
                            pe.wait_ge(layer_v, 2 * done(l - 1, x))
                        h = hi[:, (l - 1) % 2, c0:c0 + n]
                        for block in range(BLOCKS):
                            c = slice(WIDE * block + c0, WIDE * block + c0 + n)
                            j = job(l, x, block)
                            banks.wait_free(pe, j)
                            to = banks[j][:, 0:n]
                            if l == 0:
                                ins = pe.matmul(to, w_first[:, 0:128], f[:, c], start=True, stop=True)
                            else:
                                pe.matmul(to, w_t[:, l, 0:128], lo[:, (l - 1) % 2, c], start=True, stop=False)
                                ins = pe.matmul(to, w_from_hi[:, l, block], h, start=False, stop=True)
                            banks.filled(ins, j)
                        j = job(l, x, BLOCKS)
                        banks.wait_free(pe, j)
                        for block in range(BLOCKS):
                            c = slice(WIDE * block + c0, WIDE * block + c0 + n)
                            to = banks[j][HI * block:HI * block + HI, 0:n]
                            if l == 0:
                                ins = pe.matmul(to, w_first[:, 128:G], f[:, c], start=True, stop=True, tile_position=(0, HI * block))
                            else:
                                pe.matmul(to, w_t[:, l, 128:G], lo[:, (l - 1) % 2, c], start=True, stop=False,
                                          tile_position=(0, HI * block), skip_group_check=True)
                        if l:
                            ins = pe.matmul(banks[j][:, 0:n], w_hi_hi[:, l].rearrange("p b e -> p (b e)"), h, start=False, stop=True,
                                            skip_group_check=True)
                        banks.filled(ins, j)
                pe.wait_ge(layer_a, 3 * done(W, 1))
                pe.wait_ge(layer_v, 2 * done(W, 1))
                banks.wait_free(pe, LAST)
                PER = 2 * T // BLOCKS
                for t in range(2 * T):
                    pe.matmul(banks[LAST][0:P, t:t + 1], lo[:, W % 2, P * t:P * t + P], w_last[:, 0:1],
                              start=(t == 0), stop=False, skip_group_check=True)
                for r in range(PER):
                    ins = pe.matmul(banks[LAST][0:P, r:2 * T:PER], hi[:, W % 2, P * r:P * r + P], w_last_hi[:],
                                    start=False, stop=True, skip_group_check=True)
                banks.filled(ins, LAST)

            @stage.scalar
            def _(act):
                act.wait_ge(const_ok, 3 + BLOCKS)
                for l in range(W):
                    banks.wait_full(act, 2 * l)
                    act.activation(w_t[:, l + 1], banks[2 * l][:, 0:G], ACT.Copy).then_inc(w_t_ok, 1)
                    act.wait_ge(w_t_ok, l + 1)
                    banks.release(act, 2 * l)
                    j = 2 * l + 1
                    banks.wait_full(act, j)
                    for block in range(BLOCKS):
                        here = block_of[:, block:block + 1]
                        act.activation(w_from_hi[:, l + 1, block], banks[j][:, 0:128], ACT.Identity, scale=here)
                        ins = act.activation(w_hi_hi[:, l + 1, block], banks[j][:, 128:G], ACT.Identity, scale=here)
                    ins.then_inc(w_hi_ok, 1)
                    act.wait_ge(w_hi_ok, l + 1)
                    banks.release(act, j)
                for p in range(2):
                    for q, (t0, n) in enumerate(QUADS):
                        j = F0 + 3 * p + q
                        banks.wait_full(act, j)
                        act.activation(feats_t[:, p, P * t0:P * (t0 + n)], banks[j][0:3, 0:P * n], ACT.Copy).then_inc(feats_t_ok, 1)
                        act.wait_ge(feats_t_ok, 3 * p + q + 1)
                        banks.release(act, j)
                act.wait_ge(w_in, 16 * N_IN)
                for l in range(W + 1):
                    for x, (c0, n) in enumerate(PIECES):
                        for k, block in enumerate((0, 2, BLOCKS)):
                            j = job(l, x, block)
                            banks.wait_full(act, j)
                            if block < BLOCKS:
                                to = lo[:, l % 2, WIDE * block + c0:WIDE * block + c0 + n]
                            else:
                                to = hi[:, l % 2, c0:c0 + n]
                            act.activation(to, banks[j][:, 0:n], ACT.Relu, bias=bias[:, block // BLOCKS, l:l + 1]).then_inc(layer_a, 1)
                            act.wait_ge(layer_a, 3 * done(l, x) - 2 + k)
                            banks.release(act, j)

            @stage.vector
            def _(v):
                link = b.steps_of(v)
                for t in range(T):
                    ins = v.bn_stats(stats[:, t], keep.res[:, t])
                link(ins)
                for t in range(T):
                    ins = v.bn_aggr(mv[:, t], stats[:, t])
                link(ins)
                v.tensor_scalar(var[:], mv[:, :, 1], EPS, None, ALU.add).then_inc(var_ok, 1)
                v.wait_ge(rstd_ok, roots + 1)
                for t in range(T):
                    ins = v.tensor_scalar(keep.y[:, t], keep.res[:, t], mv[:, t, 0:1], rstd[:, t:t + 1], ALU.subtract, ALU.mult)
                link(ins)
                v.wait_ge(const_ok, 3 + BLOCKS)
                for t in range(T):
                    ins = v.scalar_tensor_tensor(marks[:, t], keep.y[:, t, MARKS:MARKS + 64].rearrange("p (m k) -> p m k", m=4), 0.5,
                                                 weigh[:].unsqueeze(1).to_broadcast([P, 4, 16]), ALU.is_gt, ALU.mult)
                link(ins)
                link(v.tensor_reduce(high[:], marks[:], AX.X, ALU.max))
                link(v.tensor_scalar(seen[:], high[:], 0.0, None, ALU.is_gt))
                link(v.tensor_scalar(high[:], high[:], -1.0, 16.0, ALU.mult, ALU.add))
                link(v.tensor_tensor(high[:], high[:], seen[:], ALU.mult))
                for p in range(2):
                    v.tensor_copy(feats[:, :, p, 0:2], high[:, :, p:4:2])
                    ins = v.tensor_copy(feats[:, :, p, 2], keep.y[:, :, OP])
                ins.then_inc(feats_ok, 1)
                v.wait_ge(w_in, 16 * N_IN)
                v.tensor_scalar(w_last_hi[:], block_of[:], w_last[:, 1:2], None, ALU.mult).then_inc(last_ok, 1)
                link(v.tensor_scalar(asked[:], keep.y[:, :, 0:2], 0.5, None, ALU.is_ge))
                link(v.tensor_tensor(mask[:], asked[:, :, 0], asked[:, :, 1], ALU.mult))
                link(v.tensor_scalar(mask[:], mask[:], 2.0, None, ALU.mult))
                for l in range(W + 1):
                    for x, (c0, n) in enumerate(PIECES):
                        for k, block in enumerate((1, 3)):
                            j = job(l, x, block)
                            banks.wait_full(v, j)
                            v.tensor_scalar(lo[:, l % 2, WIDE * block + c0:WIDE * block + c0 + n], banks[j][:, 0:n],
                                            bias[:, 0, l:l + 1], 0.0, ALU.add, ALU.max).then_inc(layer_v, 1)
                            v.wait_ge(layer_v, 2 * done(l, x) - 1 + k)
                            banks.release(v, j)
                banks.wait_full(v, LAST)
                link(v.tensor_scalar(result[:].rearrange("p a t -> p (a t)"), banks[LAST][0:P, 0:2 * T], bias_last[:, 0:1], 0.0,
                                     ALU.add, ALU.max))
                link(v.tensor_scalar(result[:], result[:], 15.0, ROUND, ALU.min, ALU.add))
                link(v.tensor_scalar(result[:], result[:], ROUND, None, ALU.subtract))
                for p in range(2):
                    link(v.tensor_tensor(hot[:, :, p], sixteen[:].unsqueeze(1).to_broadcast([P, T, 16]),
                                         result[:, p].unsqueeze(2).to_broadcast([P, T, 16]), ALU.is_equal))
                flat = hot[:].rearrange("p t a k -> p t (a k)")
                link(v.tensor_tensor(flat, flat, mask[:].unsqueeze(2).to_broadcast([P, T, 32]), ALU.mult))
                to = keep.res[:, :, OUT0:OUT0 + 32]
                v.wait_ge(sum_ok, 1)
                v.tensor_tensor(to, to, flat, ALU.add).then_inc(out_ok, 1)


class Keep:
    pass


def program(nc, a, out, upto=99):
    with ExitStack() as ctx:
        b = Build(nc, a, out, ctx)
        keep = Keep()
        keep.edges = nc.dram_tensor("edge_lists", [2, EDGES + GROUP], F32).ap()
        keep.ident = b.sb(ctx, "ident", [128, 128])
        keep.ones = b.sb(ctx, "ones", [128, 128])
        keep.minus_half = b.sb(ctx, "minus_half", [128, T])
        keep.node_no = b.sb(ctx, "node_no", [128, NODES], I16)
        keep.tile_base = b.sb(ctx, "tile_base", [128, GROUPS])
        keep.group_offset = b.sb(ctx, "group_offset", [1, GROUPS], I32)
        keep.group_tile = b.sb(ctx, "group_tile", [1, GROUPS], I32)
        keep.x_in = b.sem(ctx, "x_in")
        keep.w_in = b.sem(ctx, "w_in")
        keep.y_all = b.sb(ctx, "y", [128, T * D])
        keep.y = keep.y_all[0:P].rearrange("p (t d) -> p t d", t=T)
        keep.x = keep.y
        keep.res = b.sb(ctx, "res", [P, T, D])
        keep.worth_rows = nc.dram_tensor("worth_rows", [NODES, NODES], F32).ap()
        keep.slots_in = nc.dram_tensor("slots_in", [(SLOTS + 1) * SLOT, D], F32).ap()
        keep.slots_out = nc.dram_tensor("slots_out", [SLOTS * SLOT, D], F32).ap()
        keep.place = b.sb(ctx, "place", [P, T], mybir.dt.uint32)
        keep.gate = b.sb(ctx, "gate", [P, T])
        keep.slot_tables = b.sb(ctx, "slot_tables_i", [1, 4, SLOTS + 1], I32)
        keep.slot_ends = b.sb(ctx, "slot_ends_i", [1, EXPERTS], I32)
        keep.absent = nc.dram_tensor("absent_rows", [NODES, NODES], BF16).ap()
        with ExitStack() as stage:
            keep.count = b.sb(stage, "count", [P, T + 1, NODES])
            with ExitStack() as weights:
                keep.w_rows = b.sb(weights, "w_rows", [128, 2, C, D])
                keep.zeros = b.sb(weights, "zeros", [128, D])
                keep.zeros_out = b.sem(ctx, "zeros_out")
                index_edges(b, keep)
                if upto > 1:
                    count_edges(b, keep)
                if upto > 2:
                    sage(b, keep)
        with ExitStack() as stage:
            keep.o_all = b.sb(stage, "o", [128, T * D])
            keep.o = keep.o_all[0:P].rearrange("p (t d) -> p t d", t=T)
            if upto > 3:
                attention(b, keep)
            keep.w1 = b.sb(stage, "w1", [128, 2, C, FF])
            keep.w1_in = [b.sem(ctx, f"w1_in{u}") for u in range(2)]
            keep.b1_rows = b.sb(stage, "b1_rows", [EXPERTS * FF // 128, 128])
            keep.b1_in = b.sem(ctx, "b1_in")
            if upto > 4:
                routing(b, keep)
            if upto > 5:
                experts(b, keep)
        keep.m_rows = b.sb(ctx, "m_rows", [128, *a["L1_ffn_W"].shape[0::2]])
        keep.m_rows_hi = b.sb(ctx, "m_rows_hi", [a["L1_ffn_W"].shape[1] - 128, *a["L1_ffn_W"].shape[0::2]])
        keep.m_in = b.sem(ctx, "m_in")
        if upto > 6:
            with ExitStack() as stage:
                keep.worth_in = b.sem(ctx, "worth_in")
                keep.halves = nc.dram_tensor("halves_rows", [2 * HEADS, NODES], F32).ap()
                keep.shifts = nc.dram_tensor("shifts_rows", [2 * HEADS, NODES], F32).ap()
                keep.w = b.sb(stage, "w", [P, T, HEADS, HD + 1])
                keep.halves_p = b.sb(stage, "halves", [P, T, 2 * HEADS])
                keep.minus_src = b.sb(stage, "minus_src", [P, T, 2, HEADS])
                keep.worth = b.sb(stage, "worth", [P, T, NODES])
                keep.gat_w_in = b.sem(ctx, "gat_w_in")
                keep.absent_in = b.sem(ctx, "absent_in")
                with ExitStack() as before:
                    keep.w_s = b.sb(before, "w_s", [128, C, HEADS, HD])
                    keep.w_b = b.sb(before, "w_b", [P, HEADS, HD])
                    keep.y_t = b.sb(before, "y2_t", [128, C, NODES])
                    keep.no_edge = b.sb(before, "no_edge", [P, T, NODES], BF16)
                    gat_inputs(b, keep)
                    if upto > 7:
                        gat_max(b, keep)
                if upto > 7:
                    gat(b, keep)
        if upto > 8:
            last_mlp(b, keep)


def kernel(**inputs):
    import numpy as np
    import concourse.bacc as bacc
    from concourse.bass_utils import run_bass_kernel_spmd

    nc = bacc.Bacc("TRN2", target_bir_lowering=False, num_devices=1)
    arrays, args = {}, {}
    for name, value in inputs.items():
        arrays[f"in_{name}"] = value = np.ascontiguousarray(value)
        args[name] = nc.dram_tensor(f"in_{name}", value.shape, mybir.dt.from_np(value.dtype), kind="ExternalInput").ap()
    out = nc.dram_tensor("out", [NODES, D], F32, kind="ExternalOutput").ap()
    program(nc, args, out)
    return run_bass_kernel_spmd(nc, [arrays], core_ids=[0]).results[0]["out"]
```
